# Optimizing a Trainium2 kernel written in Bass

```python
import numpy as np
import jax
import jax.numpy as jnp

def _softmax(x, axis=-1):
    return jax.nn.softmax(x, axis=axis)

def _gelu(x):
    return jax.nn.gelu(x, approximate=True)

def _silu(x):
    return jax.nn.silu(x)

def _sigmoid(x):
    return jax.nn.sigmoid(x)

def _layernorm(x, axis=-1, eps=1e-05):
    m = jnp.mean(x, axis=axis, keepdims=True)
    v = jnp.var(x, axis=axis, keepdims=True)
    return (x - m) / jnp.sqrt(v + eps)

def _scatter_add(tgt, idx, src, axis=0):
    return tgt.at[idx].add(src)

def _segment_sum(src, seg, n):
    return jax.ops.segment_sum(src, seg, n)
kernel_name = 'mk_vit_tower_d2_tok_img512_r4_27a1b4'

def setup_inputs(seed: int=0):
    np.random.seed(seed)
    _w = jnp.asarray

    def _rec_inputs():
        import jax
        import jax.numpy as jnp
        _rk = jax.random.key(seed)
        x = -0.000222058 + 0.999998 * jax.random.normal(jax.random.fold_in(_rk, 1), (32, 3, 64, 64), jnp.float32)
        return x
    x = _rec_inputs()

    def _L0_tok_setup():
        import jax, jax.numpy as jnp
        import numpy as np
        IMG, P, C, D = (64, 16, 3, 128)
        NP = (IMG // P) ** 2
        PD = P * P * C
        key = jax.random.key(seed)
        k1, k2, k3 = jax.random.split(key, 3)
        x = jax.random.normal(k1, (128, C, IMG, IMG), dtype=jnp.float32)
        W = jax.random.normal(k2, (D, PD), dtype=jnp.float32) * (1.0 / np.sqrt(PD))
        b = jax.random.normal(k3, (D,), dtype=jnp.float32) * 0.01
        return {'x': x, 'W': W, 'b': b}
    _L0_tok_all = _L0_tok_setup()
    _L0_tok_in = {k: v for k, v in _L0_tok_all.items() if k in ('W', 'b')}
    del _L0_tok_all

    def _L0_attn_setup():
        import jax, jax.numpy as jnp
        import numpy as np
        HEADS = 8
        DIM_HEAD = 64
        NEG_MAX = -jnp.finfo(jnp.float32).max

        def _sn_weight(W, u, sigma):
            v = jax.lax.stop_gradient(W @ u)
            v = v / jnp.linalg.norm(v)
            u2 = jax.lax.stop_gradient(W.T @ v)
            u2 = u2 / jnp.linalg.norm(u2)
            v = jax.lax.stop_gradient(v)
            u2 = jax.lax.stop_gradient(u2)
            sig = jnp.einsum('c,cd,d->', v, W, u2)
            return W / sig * sigma
        key = jax.random.key(seed)
        ks = jax.random.split(key, 5)
        dim, inner = (128, HEADS * DIM_HEAD)
        x = jax.random.normal(ks[0], (4, 512, dim), dtype=jnp.float32)
        w_qkv = 0.02 * jax.random.normal(ks[1], (3 * inner, dim), dtype=jnp.float32)
        u_qkv = jax.random.normal(ks[2], (dim,), dtype=jnp.float32)
        u_qkv = u_qkv / jnp.linalg.norm(u_qkv)
        w_out = 0.02 * jax.random.normal(ks[3], (dim, inner), dtype=jnp.float32)
        b_out = jnp.zeros((dim,), dtype=jnp.float32)
        u_out = jax.random.normal(ks[4], (inner,), dtype=jnp.float32)
        u_out = u_out / jnp.linalg.norm(u_out)
        sigma_qkv = jnp.array(1.0, dtype=jnp.float32)
        sigma_out = jnp.array(1.0, dtype=jnp.float32)
        temperature = jnp.log(jnp.array(DIM_HEAD ** (-0.5), dtype=jnp.float32))
        return {'x': x, 'w_qkv': w_qkv, 'u_qkv': u_qkv, 'sigma_qkv': sigma_qkv, 'w_out': w_out, 'b_out': b_out, 'u_out': u_out, 'sigma_out': sigma_out, 'temperature': temperature}
    _L0_attn_all = _L0_attn_setup()
    _L0_attn_in = {k: v for k, v in _L0_attn_all.items() if k in ('w_qkv', 'u_qkv', 'sigma_qkv', 'w_out', 'b_out', 'u_out', 'sigma_out', 'temperature')}
    del _L0_attn_all

    def _L0_ffn_setup():
        import jax, jax.numpy as jnp
        import numpy as np
        B, S, D, F, E, K = (64, 128, 128, 512, 8, 2)
        key = jax.random.key(seed)
        k0, k1, k2, k3 = jax.random.split(key, 4)
        x = jax.random.normal(k0, (B, S, D), dtype=jnp.float32)
        Wr = jax.random.normal(k1, (D, E), dtype=jnp.float32) * D ** (-0.5)
        br = jnp.zeros((E,), dtype=jnp.float32)
        W1 = jax.random.normal(k2, (E, D, F), dtype=jnp.float32) * D ** (-0.5)
        b1 = jnp.zeros((E, F), dtype=jnp.float32)
        W2 = jax.random.normal(k3, (E, F, D), dtype=jnp.float32) * F ** (-0.5)
        b2 = jnp.zeros((E, D), dtype=jnp.float32)
        return {'x': x, 'Wr': Wr, 'br': br, 'W1': W1, 'b1': b1, 'W2': W2, 'b2': b2}
    _L0_ffn_all = _L0_ffn_setup()
    _L0_ffn_in = {k: v for k, v in _L0_ffn_all.items() if k in ('Wr', 'br', 'W1', 'b1', 'W2', 'b2')}
    del _L0_ffn_all

    def _L1_attn_setup():
        import jax, jax.numpy as jnp
        import numpy as np
        EPS = 1.1920929e-07

        def _rmsnorm(x, g):
            inv = jax.lax.rsqrt(jnp.mean(x * x, axis=-1, keepdims=True) + EPS)
            return x * inv * g
        key = jax.random.key(seed)
        k1, k2, k3 = jax.random.split(key, 3)
        B, T, C, H = (4, 512, 128, 8)
        D = C // H
        x = jax.random.normal(k1, (B, T, C), dtype=jnp.float32)
        delta_w = jax.random.normal(k2, (C, C), dtype=jnp.float32) * 0.02
        qkv_w = jax.random.normal(k3, (C, C), dtype=jnp.float32) * 0.02
        g1 = jnp.ones((D,), dtype=jnp.float32)
        g2 = jnp.ones((D,), dtype=jnp.float32)
        g3 = jnp.ones((D,), dtype=jnp.float32)
        return {'x': x, 'delta_w': delta_w, 'qkv_w': qkv_w, 'g1': g1, 'g2': g2, 'g3': g3}
    _L1_attn_all = _L1_attn_setup()
    _L1_attn_in = {k: v for k, v in _L1_attn_all.items() if k in ('delta_w', 'qkv_w', 'g1', 'g2', 'g3')}
    del _L1_attn_all

    def _L1_ffn_setup():
        import jax, jax.numpy as jnp
        import numpy as np
        DIM = 128
        INTER = 64
        N_SHARED = 2
        N_ROUTED = 64
        TOPK = 6
        ROUTE_SCALE = 1.0
        B, T = (2, 128)
        key = jax.random.key(seed)
        ks = jax.random.split(key, 5)
        E = N_SHARED + N_ROUTED
        x = jax.random.normal(ks[0], (B, T, DIM), jnp.float32)
        g_w = jax.random.normal(ks[1], (N_ROUTED, DIM), jnp.float32) * 0.02
        gate_bias = jnp.ones((N_ROUTED,), jnp.float32)
        w1 = jax.random.normal(ks[2], (E, DIM, INTER), jnp.float32) * 0.02
        w2 = jax.random.normal(ks[3], (E, INTER, DIM), jnp.float32) * 0.02
        w3 = jax.random.normal(ks[4], (E, DIM, INTER), jnp.float32) * 0.02
        return {'x': x, 'g_w': g_w, 'gate_bias': gate_bias, 'w1': w1, 'w2': w2, 'w3': w3}
    _L1_ffn_all = _L1_ffn_setup()
    _L1_ffn_in = {k: v for k, v in _L1_ffn_all.items() if k in ('g_w', 'gate_bias', 'w1', 'w2', 'w3')}
    del _L1_ffn_all
    return {'x': x, 'L0_tok_W': _L0_tok_in['W'], 'L0_tok_b': _L0_tok_in['b'], 'L0_attn_w_qkv': _L0_attn_in['w_qkv'], 'L0_attn_u_qkv': _L0_attn_in['u_qkv'], 'L0_attn_sigma_qkv': _L0_attn_in['sigma_qkv'], 'L0_attn_w_out': _L0_attn_in['w_out'], 'L0_attn_b_out': _L0_attn_in['b_out'], 'L0_attn_u_out': _L0_attn_in['u_out'], 'L0_attn_sigma_out': _L0_attn_in['sigma_out'], 'L0_attn_temperature': _L0_attn_in['temperature'], 'L0_ffn_Wr': _L0_ffn_in['Wr'], 'L0_ffn_br': _L0_ffn_in['br'], 'L0_ffn_W1': _L0_ffn_in['W1'], 'L0_ffn_b1': _L0_ffn_in['b1'], 'L0_ffn_W2': _L0_ffn_in['W2'], 'L0_ffn_b2': _L0_ffn_in['b2'], 'L1_attn_delta_w': _L1_attn_in['delta_w'], 'L1_attn_qkv_w': _L1_attn_in['qkv_w'], 'L1_attn_g1': _L1_attn_in['g1'], 'L1_attn_g2': _L1_attn_in['g2'], 'L1_attn_g3': _L1_attn_in['g3'], 'L1_ffn_g_w': _L1_ffn_in['g_w'], 'L1_ffn_gate_bias': _L1_ffn_in['gate_bias'], 'L1_ffn_w1': _L1_ffn_in['w1'], 'L1_ffn_w2': _L1_ffn_in['w2'], 'L1_ffn_w3': _L1_ffn_in['w3']}

def reference(x, L0_tok_W, L0_tok_b, L0_attn_w_qkv, L0_attn_u_qkv, L0_attn_sigma_qkv, L0_attn_w_out, L0_attn_b_out, L0_attn_u_out, L0_attn_sigma_out, L0_attn_temperature, L0_ffn_Wr, L0_ffn_br, L0_ffn_W1, L0_ffn_b1, L0_ffn_W2, L0_ffn_b2, L1_attn_delta_w, L1_attn_qkv_w, L1_attn_g1, L1_attn_g2, L1_attn_g3, L1_ffn_g_w, L1_ffn_gate_bias, L1_ffn_w1, L1_ffn_w2, L1_ffn_w3):
    import jax
    import jax.numpy as jnp

    def _L0_tok_ref(x, W, b):
        import jax, jax.numpy as jnp
        import numpy as np
        IMG, P, C, D = (64, 16, 3, 128)
        NP = (IMG // P) ** 2
        PD = P * P * C
        B, c, H, Wd = x.shape
        xp = x.reshape(B, c, H // P, P, Wd // P, P)
        xp = xp.transpose(0, 2, 4, 1, 3, 5).reshape(B, NP, c * P * P)
        return jnp.einsum('bnk,dk->bnd', xp, W) + b

    def _L0_attn_ref(x, w_qkv, u_qkv, sigma_qkv, w_out, b_out, u_out, sigma_out, temperature):
        import jax, jax.numpy as jnp
        import numpy as np
        HEADS = 8
        DIM_HEAD = 64
        NEG_MAX = -jnp.finfo(jnp.float32).max

        def _sn_weight(W, u, sigma):
            v = jax.lax.stop_gradient(W @ u)
            v = v / jnp.linalg.norm(v)
            u2 = jax.lax.stop_gradient(W.T @ v)
            u2 = u2 / jnp.linalg.norm(u2)
            v = jax.lax.stop_gradient(v)
            u2 = jax.lax.stop_gradient(u2)
            sig = jnp.einsum('c,cd,d->', v, W, u2)
            return W / sig * sigma
        b, n, _ = x.shape
        Wq = _sn_weight(w_qkv, u_qkv, sigma_qkv)
        qkv = x @ Wq.T
        q, k, v = jnp.split(qkv, 3, axis=-1)

        def heads(t):
            return t.reshape(b, n, HEADS, DIM_HEAD).transpose(0, 2, 1, 3)
        q, k, v = (heads(q), heads(k), heads(v))
        dots = jnp.einsum('bhid,bhjd->bhij', q, k) * jnp.exp(temperature)
        eye = jnp.eye(n, dtype=bool)
        dots = jnp.where(eye, NEG_MAX, dots)
        attn = jax.nn.softmax(dots, axis=-1)
        out = jnp.einsum('bhij,bhjd->bhid', attn, v)
        out = out.transpose(0, 2, 1, 3).reshape(b, n, HEADS * DIM_HEAD)
        Wo = _sn_weight(w_out, u_out, sigma_out)
        return out @ Wo.T + b_out

    def _L0_ffn_ref(x, Wr, br, W1, b1, W2, b2):
        import jax, jax.numpy as jnp
        import numpy as np
        B, S, D, F, E, K = (64, 128, 128, 512, 8, 2)
        orig_shape = x.shape
        t = x.reshape(-1, orig_shape[-1])
        logits = t @ Wr + br
        gates = jax.nn.softmax(logits, axis=-1)
        top_vals, top_idx = jax.lax.top_k(gates, K)
        top_vals = top_vals / top_vals.sum(axis=-1, keepdims=True)
        onehot = jax.nn.one_hot(top_idx, E, dtype=t.dtype)
        combine = jnp.einsum('tk,tke->te', top_vals, onehot)
        out = jnp.zeros_like(t)
        for e in range(E):
            h = jax.nn.relu(t @ W1[e] + b1[e])
            y = h @ W2[e] + b2[e]
            out = out + combine[:, e:e + 1] * y
        return out.reshape(orig_shape)

    def _L1_attn_ref(x, delta_w, qkv_w, g1, g2, g3):
        import jax, jax.numpy as jnp
        import numpy as np
        EPS = 1.1920929e-07

        def _rmsnorm(x, g):
            inv = jax.lax.rsqrt(jnp.mean(x * x, axis=-1, keepdims=True) + EPS)
            return x * inv * g
        B, T, C = x.shape
        H = 8
        D = C // H
        sqrt_d = jnp.float32(D) ** 0.5
        W = qkv_w + delta_w
        w = (x @ W.T).reshape(B, T, H, D).transpose(0, 2, 1, 3)
        att = jnp.einsum('bhif,bhjf->bhij', _rmsnorm(w, g1), _rmsnorm(w, g2)) / sqrt_d
        score = jax.nn.softmax(att, axis=-1) + jax.nn.softmax(att, axis=-2)
        y = jnp.einsum('bhij,bhjf->bihf', score, _rmsnorm(w, g3))
        return y.reshape(B, T, C) @ W

    def _L1_ffn_ref(x, g_w, gate_bias, w1, w2, w3):
        import jax, jax.numpy as jnp
        import numpy as np
        DIM = 128
        INTER = 64
        N_SHARED = 2
        N_ROUTED = 64
        TOPK = 6
        ROUTE_SCALE = 1.0
        B, T = (2, 128)
        Bx, Tx, C = x.shape
        K = TOPK + N_SHARED
        scores = jnp.einsum('btd,ed->bte', x, g_w)
        scores = jax.nn.softmax(scores.astype(jnp.float32), axis=-1)
        _, idx = jax.lax.top_k(scores + gate_bias, TOPK)
        rweights = jnp.take_along_axis(scores, idx, axis=-1) * ROUTE_SCALE
        rweights = rweights.astype(x.dtype)
        shared_idx = jnp.broadcast_to(jnp.arange(N_SHARED), (Bx, Tx, N_SHARED))
        expert_idx = jnp.concatenate([shared_idx, idx + N_SHARED], axis=-1)
        comb_w = jnp.concatenate([jnp.ones((Bx, Tx, N_SHARED), x.dtype), rweights], axis=-1)
        flat_idx = expert_idx.reshape(-1)
        x_rep = jnp.broadcast_to(x[:, :, None, :], (Bx, Tx, K, C)).reshape(-1, C)
        h1 = jnp.einsum('nd,nde->ne', x_rep, w1[flat_idx])
        h3 = jnp.einsum('nd,nde->ne', x_rep, w3[flat_idx])
        out = jnp.einsum('ne,ned->nd', jax.nn.silu(h1) * h3, w2[flat_idx])
        out = out * comb_w.reshape(-1, 1)
        return out.reshape(Bx, Tx, K, C).sum(axis=2)
    h = _L0_tok_ref(x, L0_tok_W, L0_tok_b)
    h = h + _L0_attn_ref(_layernorm(h, axis=-1), L0_attn_w_qkv, L0_attn_u_qkv, L0_attn_sigma_qkv, L0_attn_w_out, L0_attn_b_out, L0_attn_u_out, L0_attn_sigma_out, L0_attn_temperature)
    h = h + _L0_ffn_ref(_layernorm(h, axis=-1), L0_ffn_Wr, L0_ffn_br, L0_ffn_W1, L0_ffn_b1, L0_ffn_W2, L0_ffn_b2)
    h = h + _L1_attn_ref(_layernorm(h, axis=-1), L1_attn_delta_w, L1_attn_qkv_w, L1_attn_g1, L1_attn_g2, L1_attn_g3)
    h = h + _L1_ffn_ref(_layernorm(h, axis=-1), L1_ffn_g_w, L1_ffn_gate_bias, L1_ffn_w1, L1_ffn_w2, L1_ffn_w3)
    return h

_drawn_inputs = setup_inputs


def setup_inputs(seed=0):
    import zlib

    import numpy as np

    out = dict(_drawn_inputs(seed))
    spreads = {'L0_attn_b_out': (0.0, 0.1),
     'L0_ffn_br': (0.0, 0.1),
     'L0_ffn_b1': (0.0, 0.1),
     'L0_ffn_b2': (0.0, 0.1),
     'L1_attn_g1': (1.0, 0.6),
     'L1_attn_g2': (1.0, 0.6),
     'L1_attn_g3': (1.0, 0.2),
     'L1_ffn_gate_bias': (1.0, 0.6)}
    factors = {'L0_tok_b': 3.535,
     'L0_attn_u_qkv': 8.0,
     'L0_attn_u_out': 8.0,
     'L1_ffn_g_w': 8.0,
     'L1_ffn_w1': 8.0,
     'L1_ffn_w2': 8.0,
     'L1_ffn_w3': 8.0}
    for name, (base, spread) in spreads.items():
        noise = np.random.default_rng([zlib.crc32(name.encode()), seed]).standard_normal(out[name].shape)
        drawn = base * np.exp(spread * noise) if base else spread * noise
        out[name] = jnp.asarray(drawn.astype(out[name].dtype))
    for name, factor in factors.items():
        out[name] = (out[name] * factor).astype(out[name].dtype)
    return out
```

```python
from contextlib import ExitStack

import concourse.bass as bass
from concourse import mybir

F32 = mybir.dt.float32
F16 = mybir.dt.float16
BF16 = mybir.dt.bfloat16
ALU = mybir.AluOpType
ACT = mybir.ActivationFunctionType
AX = mybir.AxisListType.X

P = 128
NT = 4
N = NT * P
KC = 6
H = 8
DH0, DH1 = 64, 16
INNER = H * DH0
E0, F0 = 8, 512
C0 = F0 // P
NP = 33
ER = 64
TOPK1 = 6
PW = 3 * P
BIG = float(2 ** 100)
WS, HS, LS = 64.0, 16.0, 2048.0
EPS_LN, EPS_RMS = 1e-5, 1.1920929e-07

ROW = {"tok_b": (0, 128), "b_out": (128, 256), "br": (256, 264), "g1": (264, 280), "g2": (280, 296),
       "g3": (296, 312), "gate_bias": (312, 376), "sigma": (376, 378), "temp": (378, 379)}
ROWN = 379
COL = {"u_qkv": (0, 1), "u_out": (1, 5), "b1": (5, 37), "wr": (37, 45), "gw": (45, 109)}
COLN = 109
CST = {"ident": (0, 128), "mask0": (128, 256), "mask1": (256, 384), "pick1": (384, 448), "pick0": (448, 456),
       "heads": (456, 464), "b2scale": (464, 465)}
CSTN = 465


def tower(nc, xT, tokWT, rows, cols, consts, wqkvT, wqkvN, woT, woN, l1w, b2x, wl0, wl1, out):
    with ExitStack() as ctx:
        def sb(name, shape, dt=F32):
            return ctx.enter_context(nc.sbuf_tensor(name, shape, dt))

        def sem(name):
            return ctx.enter_context(nc.semaphore(name))

        x_sb = sb("x_sb", [P, NT, KC, P])
        tokw = sb("tokw", [P, KC, P])
        rows_sb = sb("rows_sb", [P, ROWN])
        cols_sb = sb("cols_sb", [P, COLN])
        cst = sb("cst", [P, CSTN])
        wqkvT_sb = sb("wqkvT_sb", [P, 3 * INNER])
        wqkvN_sb = sb("wqkvN_sb", [P, 3 * INNER // P, P])
        woT_sb = sb("woT_sb", [P, C0, P])
        woN_sb = sb("woN_sb", [P, INNER])
        l1w_sb = sb("l1w_sb", [P, 4, P])
        w1n = sb("w1n", [P, P])
        w1t = sb("w1t", [P, P])
        b2_sb = sb("b2_sb", [16, P])
        stage = sb("stage", [P, NP * PW])
        st0 = stage[:, 0:E0 * 2 * F0].rearrange("p (a b) -> p a b", b=2 * F0)
        st1 = stage
        w0h = sb("w0h", [P, E0 * 2 * F0], F16)
        w0l = sb("w0l", [P, E0 * 2 * F0], F16)
        w1h = sb("w1h", [P, 4, PW], F16)
        w1l = sb("w1l", [P, 4, PW], F16)
        negI = sb("negI", [P, P], BF16)
        m0b = sb("m0b", [P, 4, P], BF16)
        m1b = sb("m1b", [P, 4, P], BF16)
        ones = sb("ones", [P, P])
        mhalf = sb("mhalf", [P, 32])
        phalf = sb("phalf", [P, 2])
        sel1 = sb("sel1", [P, ER, DH0], F16)
        sel0 = sb("sel0", [P, E0, P], F16)
        wrs = sb("wrs", [P, 2, ER + E0], F16)
        h = sb("h", [P, NT, P])
        hb = sb("hb", [P, NT, P])
        stats = sb("stats", [P, NT, 6])
        mv = sb("mv", [P, NT, 2])
        vpe = sb("vpe", [P, NT])
        rstd = sb("rstd", [P, NT])
        xn = sb("xn", [P, NT, P])
        xnT = sb("xnT", [P, N])
        xfh = sb("xfh", [P, N], F16)
        xfl = sb("xfl", [P, N], F16)
        big = sb("big", [P, 8, N])
        qT1 = sb("qT1", [P, N])
        vA = sb("vA", [P, NT, H, DH0 + 1])
        pb = sb("pb", [P, 2, 4, P])
        pc = sb("pc", [P, 2, 4, P])
        pT = sb("pT", [P, 2, 4, P])
        on = sb("on", [P, 2, H, DH0])
        oT = sb("oT", [P, 2, 4, P])
        mx = sb("mx", [P, 2, 4])
        mxc = sb("mxc", [P, 2, 4])
        rs = sb("rs", [P, 2, 4])
        cs = sb("cs", [P, 2, 4])
        vcs = sb("vcs", [P, 2, 4, DH1])
        sna = sb("sna", [P, 13])
        snb = sb("snb", [P, 5])
        sna2 = sb("sna2", [P, 13])
        snb2 = sb("snb2", [P, 5])
        sn4 = sb("sn4", [P, 4])
        snr = sb("snr", [P, 8])
        etemp = sb("etemp", [P, 1])
        cexp = sb("cexp", [P, 1])
        cout = sb("cout", [P, 1])
        lg0 = sb("lg0", [P, NT, ER])
        lgm = sb("lgm", [P, NT])
        lgs = sb("lgs", [P, NT])
        top8 = sb("top8", [P, NT, 8])
        rep = sb("rep", [P, NT, ER])
        bia = sb("bia", [P, NT, ER])
        gates = sb("gates", [P, NT, ER])
        g16 = sb("g16", [P, NT, ER], F16)
        gcb = sb("gcb", [P, NT, 2 * ER])
        gT = sb("gT", [P, N], F16)
        gT32 = sb("gT32", [16, N])
        b1s = sb("b1s", [P, E0 * C0])
        ms = sb("ms", [P, 32])
        xf = x_sb[:].rearrange("p a b c -> p (a b c)")

        def two(ap):
            return ap.rearrange("p (a b) -> p a b", b=N)
        r, u, s = two(xf[:, 0:2 * N]), two(xf[:, 2 * N:4 * N]), two(xf[:, 4 * N:6 * N])
        G, acc = two(wqkvT_sb[:, 0:2 * N]), wqkvT_sb[:, 2 * N:3 * N]
        nf = wqkvN_sb[:].rearrange("p a b -> p (a b)")
        yt, wtm = two(nf[:, 0:2 * N]), nf[:, 2 * N:3 * N]
        wsq = tokw[:].rearrange("p a b -> p (a b)")[:, 0:N]
        pcf = pc[:].rearrange("p a b c -> p (a b c)")
        qn, kn = pcf[:, 0:N], pcf[:, N:2 * N]
        bf = big[:].rearrange("p a b -> p (a b)")
        hh, hl = two(bf[:, 0:2 * N].bitcast(F16)), two(bf[:, 2 * N:4 * N].bitcast(F16))
        outs = hb

        B = [ctx.enter_context(nc.psum_tensor(f"bank{i}", [P, 512], F32)) for i in range(8)]

        def row(name):
            a, b = ROW[name]
            return rows_sb[:, a:b]

        def col(name):
            a, b = COL[name]
            return cols_sb[:, a:b]

        def con(name):
            a, b = CST[name]
            return cst[:, a:b]

        def over(ap, n):
            return ap.unsqueeze(2).broadcast_to([ap.shape[0], ap.shape[1], n])

        def along(ap, n):
            return ap.unsqueeze(1).broadcast_to([ap.shape[0], n, ap.shape[1]])

        def tile(t):
            return slice(P * t, P * t + P)

        ident = con("ident")

        d_col, d_row, d_cst, d_tokw = sem("d_col"), sem("d_row"), sem("d_cst"), sem("d_tokw")
        d_x = [sem(f"d_x{t}") for t in range(NT)]
        d_wqT, d_wqN, d_wo, d_l1w = sem("d_wqT"), sem("d_wqN"), sem("d_wo"), sem("d_l1w")
        d_w0 = [sem(f"d_w0_{e}") for e in range(E0)]
        d_w1 = [sem(f"d_w1_{c}") for c in range(NP // 3)]
        d_out = sem("d_out")
        pool_const = sem("pool_const")
        mask_ready = sem("mask_ready")
        act_setup = sem("act_setup")
        sn_a, sn_acopy, sn_b, sn_sums, sn_tot, sn_ratio, sn_norm, sn_scales, temp_exp = (
            sem(n) for n in ("sn_a", "sn_acopy", "sn_b", "sn_sums", "sn_tot", "sn_ratio", "sn_norm", "sn_scales",
                             "temp_exp"))
        tok_done, ln_var, ln_rstd, ln_xn, ln_T = (sem(n) for n in ("tok_done", "ln_var", "ln_rstd", "ln_xn", "ln_T"))
        xnT_a, xfl_v = sem("xnT_a"), sem("xfl_v")
        qkv_mm, qkv_ev_a, qkv_ev_v = sem("qkv_mm"), sem("qkv_ev_a"), sem("qkv_ev_v")
        s_mm, s_sub, s_exp, s_T, s_pT, s_av, s_on, s_oTp, s_oT, s_proj, s_hup, hb_done = (
            sem(n) for n in ("s_mm", "s_sub", "s_exp", "s_T", "s_pT", "s_av", "s_on", "s_oTp", "s_oT", "s_proj",
                             "s_hup", "hb_done"))
        w0_hi = sem("w0_hi")
        w0_lo = sem("w0_lo")
        r0_mm, r0_sub, r0_exp, r0_gcb, r0_T, r0_gT, r0_b2, r0_acc = (
            sem(n) for n in ("r0_mm", "r0_sub", "r0_exp", "r0_gcb", "r0_T", "r0_gT", "r0_b2", "r0_acc"))
        up0, relu0, hi0, lo0v, lo0p, down0, gmm0, gev0, y0, yt0, acc0 = (
            sem(n) for n in ("up0", "relu0", "hi0", "lo0v", "lo0p", "down0", "gmm0", "gev0", "y0", "yt0", "acc0"))
        f0_T, f0_h = sem("f0_T"), sem("f0_h")
        w1_sum, w_mm, w_sq, w_ms, w_inv, qk_n, qk_T, qT_ev, kM_v, kM_a = (
            sem(n) for n in ("w1_sum", "w_mm", "w_sq", "w_ms", "w_inv", "qk_n", "qk_T", "qT_ev", "kM_v", "kM_a"))
        t_mm, t_subr, t_subc, t_expr, t_expc, t_T, t_pT, t_vcs, t_av, t_y, t_yTp, t_yT, t_proj, t_hup = (
            sem(n) for n in ("t_mm", "t_subr", "t_subc", "t_expr", "t_expc", "t_T", "t_pT", "t_vcs", "t_av", "t_y",
                             "t_yTp", "t_yT", "t_proj", "t_hup"))
        r1_mm, r1_sub, r1_exp, r1_gcb, r1_T, r1_gT = (
            sem(n) for n in ("r1_mm", "r1_sub", "r1_exp", "r1_gcb", "r1_T", "r1_gT"))
        w1_hi, w1_lo, h1mm, h3mm, g1mm, silu1, u1, r1, hi1, lo1, down1, y1, y1_ev, y1_T, out_v = (
            sem(n) for n in ("w1_hi", "w1_lo", "h1mm", "h3mm", "g1mm", "silu1", "u1", "r1", "hi1", "lo1", "down1",
                             "y1", "y1_ev", "y1_T", "out_v"))
        dve_step, pool_step, act_step = sem("dve_step"), sem("pool_step"), sem("act_step")

        block = ctx.enter_context(nc.Block())

        @block.sync
        def _(sp):
            sp.dma_start(cst[:], consts).then_inc(d_cst, 16)
            sp.dma_start(tokw[:], tokWT).then_inc(d_tokw, 16)
            sp.dma_start(cols_sb[:], cols).then_inc(d_col, 16)
            sp.dma_start(rows_sb[:], rows.broadcast_to([P, ROWN])).then_inc(d_row, 16)
            for t in range(NT):
                sp.dma_start(x_sb[:, t], xT[t]).then_inc(d_x[t], 16)
            sp.dma_start(wqkvT_sb[:], wqkvT).then_inc(d_wqT, 16)
            sp.dma_start(woT_sb[:], woT).then_inc(d_wo, 16)
            sp.dma_start(woN_sb[:], woN).then_inc(d_wo, 16)
            sp.dma_start(wqkvN_sb[:], wqkvN).then_inc(d_wqN, 16)
            for e in range(E0):
                sp.dma_start(st0[:, e], wl0[e]).then_inc(d_w0[e], 16)
            sp.dma_start(l1w_sb[:], l1w).then_inc(d_l1w, 16)
            sp.dma_start(b2_sb[:], b2x).then_inc(d_l1w, 16)
            for c in range(NP // 3):
                if c < 8:
                    sp.wait_ge(w0_lo, min(3 * PW * (c + 1) - 1, E0 * 1024 - 1) // 1024 + 1)
                sp.dma_start(st1[:, 3 * PW * c:3 * PW * (c + 1)], wl1[c]).then_inc(d_w1[c], 16)
            for t in range(NT):
                sp.wait_ge(out_v, t + 1)
                sp.dma_start(out[t], outs[:, t]).then_inc(d_out, 16)
            sp.wait_ge(d_out, 16 * NT)

        @block.gpsimd
        def _(pool):
            nc.gpsimd.memset(ones[:], 1.0)
            nc.gpsimd.memset(mhalf[:], -0.5)
            nc.gpsimd.memset(phalf[:], 0.5)
            nc.gpsimd.memset(gT[:], 0.0)
            nc.gpsimd.memset(vA[:, :, :, DH0:DH0 + 1], 1.0).then_inc(pool_const, 1)

            def norm(k):
                for t in range(NT):
                    pool.wait_ge(ln_var, NT * k + t + 1)
                    nc.gpsimd.tensor_tensor(rstd[:, t:t + 1], vpe[:, t:t + 1], mhalf[:, 0:1],
                                            ALU.pow).then_inc(ln_rstd, 1)

            pool.wait_ge(pool_const, 1)
            norm(0)
            for t in range(NT):
                nc.gpsimd.tensor_tensor(hb[:, t], h[:, t], row("b_out"), ALU.add).then_inc(hb_done, 1)
            pool.wait_ge(sn_ratio, 1)
            nc.gpsimd.tensor_tensor(snr[:, 4:6], snr[:, 2:4], phalf[:], ALU.pow).then_inc(sn_norm, 1)
            pool.wait_ge(d_l1w, 32)
            nc.gpsimd.tensor_tensor(w1n[:], l1w_sb[:, 0], l1w_sb[:, 1], ALU.add)
            nc.gpsimd.tensor_tensor(w1t[:], l1w_sb[:, 2], l1w_sb[:, 3], ALU.add).then_inc(w1_sum, 1)
            norm(1)

            def lo_half(n, slot):
                pool.wait_ge(hi0, n + 1)
                nc.gpsimd.tensor_tensor(hl[:, slot, 256:512], r[:, slot % 2, 256:512], hh[:, slot, 256:512],
                                        ALU.subtract).then_inc(lo0p, 1)

            def add_expert(e, b):
                pool.wait_ge(yt0, e + 1)
                nc.gpsimd.tensor_tensor(acc[:], acc[:], yt[:, b], ALU.add).then_inc(acc0, 1)
                pool.wait_ge(acc0, e + 1)

            for n in range(4):
                lo_half(n, n)
            pool.wait_ge(r0_acc, 1)
            with pool.Fori(0, 3) as m:
                for k in range(8):
                    lo_half(8 * m + 4 + k, k % 4)
                    if k in (2, 6):
                        add_expert(2 * m + k // 4, k // 4)
            for n in range(28, 32):
                lo_half(n, n % 4)
                if n == 30:
                    add_expert(6, 0)
            add_expert(7, 1)
            norm(2)
            pool.wait_ge(w_ms, 1)
            nc.gpsimd.tensor_tensor(ms[:], ms[:], mhalf[:], ALU.pow).then_inc(w_inv, 1)
            norm(3)

            def lo_pair(p, slot):
                pool.wait_ge(hi1, p + 1)
                src = u if slot is None else r
                b = 0 if slot is None else slot % 2
                nc.gpsimd.tensor_tensor(hl[:, b, :], src[:, b, :], hh[:, b, :], ALU.subtract).then_inc(lo1, 1)

            lo_pair(0, None)
            for p in range(1, 4):
                lo_pair(p, p)
            with pool.Fori(0, 6) as m:
                for k in range(4):
                    lo_pair(4 * m + 4 + k, k)
            for p in range(28, NP):
                lo_pair(p, p % 4)

        @block.scalar
        def _(act):
            act.wait_ge(d_row, 16)
            nc.scalar.activation(etemp[:], row("temp"), ACT.Exp).then_inc(temp_exp, 1)
            act.wait_ge(d_col, 16)
            nc.scalar.activation(wrs[:, 0, 0:ER], col("gw"), ACT.Copy, scale=WS)
            nc.scalar.activation(wrs[:, 0, ER:ER + E0], col("wr"), ACT.Copy, scale=WS)
            nc.scalar.activation(b1s[:], col("b1"), ACT.Copy, scale=HS).then_inc(act_setup, 1)
            act.wait_ge(d_cst, 16)
            for e in range(0, ER, 16):
                nc.scalar.activation(sel1[:, e:e + 16, :], over(con("pick1")[:, e:e + 16], DH0), ACT.Copy)
            nc.scalar.activation(sel0[:], over(con("pick0"), P), ACT.Copy).then_inc(act_setup, 1)

            act.wait_ge(ln_T, NT)
            nc.scalar.activation(xnT[:], B[0][:], ACT.Copy).then_inc(xnT_a, 1)
            for k in range(0, 12, 2):
                act.wait_ge(qkv_mm, k + 1)
                if k < 8:
                    nc.scalar.activation(big[:, k, :], B[2 + k % 4][:], ACT.Copy).then_inc(qkv_ev_a, 1)
                else:
                    nc.scalar.activation(vA[:, k - 8, :, 0:DH0], B[2 + k % 4][:].rearrange("p (a b) -> p a b", b=DH0),
                                         ACT.Copy).then_inc(qkv_ev_a, 1)

            def exp0(i):
                if i == 0:
                    act.wait_ge(sn_scales, 1)
                act.wait_ge(s_sub, i + 1)
                nc.scalar.activation(pb[:, i % 2], pb[:, i % 2], ACT.Exp, scale=cexp[:]).then_inc(s_exp, 1)

            def ev_pT(i):
                act.wait_ge(s_T, i + 1)
                if i >= 2:
                    act.wait_ge(s_av, i - 1)
                nc.scalar.activation(pT[:, i % 2], B[2 + i % 2][:].rearrange("p (a b) -> p a b", b=P),
                                     ACT.Copy).then_inc(s_pT, 1)

            def ev_oT(t):
                act.wait_ge(s_oTp, t + 1)
                if t >= 2:
                    act.wait_ge(s_proj, t - 1)
                nc.scalar.activation(oT[:, t % 2], B[6][:].rearrange("p (a b) -> p a b", b=P),
                                     ACT.Copy).then_inc(s_oT, 1)

            exp0(0)
            for i in range(8):
                if i + 1 < 8:
                    exp0(i + 1)
                ev_pT(i)
                if i >= 2 and i % 2 == 0:
                    ev_oT((i - 2) // 2)
                act.wait_ge(d_w0[i], 16)
                nc.scalar.activation(w0h[:, 1024 * i:1024 * (i + 1)], st0[:, i, :], ACT.Copy,
                                     scale=WS).then_inc(w0_hi, 1)
            ev_oT(3)

            act.wait_ge(ln_T, 2 * NT)
            nc.scalar.activation(xfh[:], B[0][:], ACT.Copy).then_inc(xnT_a, 1)
            act.wait_ge(r0_sub, 1)
            nc.scalar.activation(lg0[:, :, 0:E0], lg0[:, :, 0:E0], ACT.Exp).then_inc(r0_exp, 1)

            def relu(n, c, slot):
                act.wait_ge(up0, n + 1)
                if slot is not None:
                    act.wait_ge(lo0v, n - 1)
                    act.wait_ge(lo0p, n - 1)
                nc.scalar.activation(r[:, c % 2], B[3 + c % 2][:], ACT.Relu, scale=HS / WS,
                                     bias=b1s[:, bass.ds(n, 1)]).then_inc(relu0, 1)

            def ev_gate(e, b, used):
                act.wait_ge(gmm0, e + 1)
                if used:
                    act.wait_ge(yt0, e - 1)
                nc.scalar.activation(G[:, b], B[5 + b][:], ACT.Copy).then_inc(gev0, 1)

            for n in range(2):
                relu(n, n, None)
            act.wait_ge(r0_T, 1)
            nc.scalar.activation(gT[0:16, :], B[2][0:16, :], ACT.Copy)
            nc.scalar.activation(gT32[:], B[2][0:16, :], ACT.Copy).then_inc(r0_gT, 1)
            for n in range(2, 4):
                relu(n, n, n)
            act.wait_ge(r0_b2, 1)
            nc.scalar.activation(acc[:], B[1][:], ACT.Copy).then_inc(r0_acc, 1)
            ev_gate(0, 0, False)
            with act.Fori(0, 3) as m:
                for k in range(8):
                    relu(8 * m + 4 + k, k, k)
                    if k == 3:
                        ev_gate(2 * m + 1, 1, False)
                    if k == 7:
                        ev_gate(2 * m + 2, 0, True)
            for n in range(28, 32):
                relu(n, n, n)
                if n == 31:
                    ev_gate(7, 1, True)

            act.wait_ge(ln_T, 3 * NT)
            nc.scalar.activation(xnT[:], B[0][:], ACT.Copy).then_inc(xnT_a, 1)
            act.wait_ge(w_mm, NT)
            nc.scalar.activation(wsq[:], B[1][:], ACT.Square).then_inc(w_sq, 1)
            act.wait_ge(qk_T, 1)
            nc.scalar.activation(qT1[:], B[2][:], ACT.Copy).then_inc(qT_ev, 1)
            act.wait_ge(qk_T, 2)
            for hd in range(4, H):
                nc.scalar.activation(big[:, hd, :], B[4][:], ACT.Copy, scale=con("heads")[:, hd:hd + 1]).then_inc(kM_a, 1)

            def exp1(i):
                act.wait_ge(t_subr, i + 1)
                nc.scalar.activation(pb[:, i % 2], pb[:, i % 2], ACT.Exp, scale=0.25).then_inc(t_expr, 1)
                act.wait_ge(t_subc, i + 1)
                nc.scalar.activation(pc[:, i % 2], pc[:, i % 2], ACT.Exp, scale=0.25).then_inc(t_expc, 1)

            def ev_pT1(i):
                act.wait_ge(t_T, i + 1)
                if i >= 2:
                    act.wait_ge(t_av, i - 1)
                nc.scalar.activation(pT[:, i % 2], B[2 + i % 2][:].rearrange("p (a b) -> p a b", b=P),
                                     ACT.Copy).then_inc(t_pT, 1)

            def ev_yT(t):
                act.wait_ge(t_yTp, t + 1)
                if t >= 2:
                    act.wait_ge(t_proj, t - 1)
                nc.scalar.activation(oT[:, t % 2, 0], B[7][:, 0:P], ACT.Copy).then_inc(t_yT, 1)

            exp1(0)
            for i in range(8):
                if i + 1 < 8:
                    exp1(i + 1)
                ev_pT1(i)
                if i >= 2 and i % 2 == 0:
                    ev_yT((i - 2) // 2)
            ev_yT(3)

            def hi_weights(p, slot):
                nc.scalar.activation(w1h[:, slot], st1[:, bass.ds(PW * p, PW)], ACT.Copy, scale=WS).then_inc(w1_hi, 1)

            for c in range(NP // 3):
                act.wait_ge(d_w1[c], 16)
            for p in range(2):
                hi_weights(p, p)
            act.wait_ge(ln_T, 4 * NT)
            nc.scalar.activation(xfh[:], B[0][:], ACT.Copy).then_inc(xnT_a, 1)
            act.wait_ge(r1_sub, 1)
            nc.scalar.activation(lg0[:], lg0[:], ACT.Exp, scale=1.0 / WS).then_inc(r1_exp, 1)

            def silu(p, b, used):
                act.wait_ge(h1mm, p + 1)
                if used:
                    act.wait_ge(u1, p - 1)
                nc.scalar.activation(s[:, b], B[3 + b][:], ACT.Silu, scale=1.0 / WS).then_inc(silu1, 1)

            def hi_hidden(p, b, used):
                act.wait_ge(r1, p + 1)
                if used:
                    act.wait_ge(down1, p - 1)
                nc.scalar.activation(hh[:, b], r[:, b], ACT.Copy).then_inc(hi1, 1)

            def next_weights(p, slot):
                if not (isinstance(p, int) and p < 4):
                    act.wait_ge(down1, p - 3)
                hi_weights(p, slot)

            silu(0, 0, False)
            act.wait_ge(u1, 1)
            nc.scalar.activation(hh[:, 0], u[:, 0], ACT.Copy).then_inc(hi1, 1)
            next_weights(2, 2)
            act.wait_ge(r1_T, 1)
            nc.scalar.activation(gT[:], B[2][:], ACT.Copy).then_inc(r1_gT, 1)
            for p in range(1, 4):
                silu(p, p % 2, p >= 2)
                next_weights(p + 2, (p + 2) % 4)
                hi_hidden(p, p % 2, p >= 2)
            with act.Fori(0, 6) as m:
                for k in range(4):
                    silu(4 * m + 4 + k, k % 2, True)
                    next_weights(4 * m + 6 + k, (k + 2) % 4)
                    hi_hidden(4 * m + 4 + k, k % 2, True)
            for p in range(28, NP):
                silu(p, p % 2, True)
                if p + 2 < NP:
                    next_weights(p + 2, (p + 2) % 4)
                hi_hidden(p, p % 2, True)
            act.wait_ge(y1, 1)
            nc.scalar.activation(acc[:], B[0][:], ACT.Copy, scale=1.0 / (WS * HS)).then_inc(y1_ev, 1)

        @block.vector
        def _(dve):
            count = [0]

            def link(ins):
                count[0] += 1
                ins.then_inc(dve_step, 1)
                dve.wait_ge(dve_step, count[0])

            dve.wait_ge(act_setup, 1)
            nc.vector.scalar_tensor_tensor(wrs[:, 1, 0:ER], col("gw"), WS, wrs[:, 0, 0:ER], ALU.mult, ALU.subtract)
            nc.vector.scalar_tensor_tensor(wrs[:, 1, ER:ER + E0], col("wr"), WS, wrs[:, 0, ER:ER + E0],
                                           ALU.mult, ALU.subtract).then_inc(mask_ready, 1)
            dve.wait_ge(d_cst, 16)
            nc.vector.tensor_scalar(negI[:], ident, -BIG, None, ALU.mult)
            nc.vector.tensor_copy(m0b[:], along(con("mask0"), 4))
            nc.vector.tensor_copy(m1b[:], along(con("mask1"), 4)).then_inc(mask_ready, 1)

            def norm_stats(k, t):
                link(nc.vector.bn_stats(stats[:, t], h[:, t]))
                link(nc.vector.bn_aggr(mv[:, t], stats[:, t]))
                nc.vector.tensor_scalar_add(vpe[:, t:t + 1], mv[:, t, 1:2], EPS_LN).then_inc(ln_var, 1)

            def norm_apply(k):
                for t in range(NT):
                    dve.wait_ge(ln_rstd, NT * k + t + 1)
                    nc.vector.tensor_scalar(xn[:, t], h[:, t], mv[:, t, 0:1], rstd[:, t:t + 1],
                                            ALU.subtract, ALU.mult).then_inc(ln_xn, 1)

            dve.wait_ge(d_row, 16)
            for t in range(NT):
                dve.wait_ge(tok_done, t + 1)
                link(nc.vector.tensor_tensor(h[:, t], B[t][:, 0:P], row("tok_b"), ALU.add))
                norm_stats(0, t)
            norm_apply(0)

            dve.wait_ge(sn_a, 1)
            nc.vector.tensor_copy(sna[:], B[6][:, 0:13]).then_inc(sn_acopy, 1)
            dve.wait_ge(sn_acopy, 1)
            link(nc.vector.tensor_tensor(sna2[:], sna[:], sna[:], ALU.mult))
            nc.vector.tensor_reduce(sn4[:, 0:1], sna2[:, 0:12], AX, ALU.add)
            nc.vector.tensor_copy(sn4[:, 1:2], sna2[:, 12:13])
            dve.wait_ge(sn_b, 1)
            link(nc.vector.tensor_copy(snb[:], B[7][:, 0:5]))
            link(nc.vector.tensor_tensor(snb2[:], snb[:], snb[:], ALU.mult))
            nc.vector.tensor_copy(sn4[:, 2:3], snb2[:, 0:1])
            nc.vector.tensor_reduce(sn4[:, 3:4], snb2[:, 1:5], AX, ALU.add).then_inc(sn_sums, 1)
            dve.wait_ge(sn_tot, 1)
            link(nc.vector.reciprocal(snr[:, 0:2], B[7][:, 10:12]))
            nc.vector.tensor_tensor(snr[:, 2:4], B[7][:, 8:10], snr[:, 0:2], ALU.mult).then_inc(sn_ratio, 1)
            dve.wait_ge(sn_norm, 1)
            link(nc.vector.tensor_tensor(snr[:, 6:8], snr[:, 4:6], row("sigma"), ALU.mult))
            link(nc.vector.tensor_tensor(snr[:, 0:1], snr[:, 6:7], snr[:, 6:7], ALU.mult))
            nc.vector.tensor_tensor(cout[:], snr[:, 6:7], snr[:, 7:8], ALU.mult)
            dve.wait_ge(temp_exp, 1)
            nc.vector.tensor_tensor(cexp[:], snr[:, 0:1], etemp[:], ALU.mult).then_inc(sn_scales, 1)

            for k in range(1, 12, 2):
                dve.wait_ge(qkv_mm, k + 1)
                if k < 8:
                    nc.vector.tensor_copy(big[:, k, :], B[2 + k % 4][:]).then_inc(qkv_ev_v, 1)
                else:
                    nc.vector.tensor_copy(vA[:, k - 8, :, 0:DH0],
                                          B[2 + k % 4][:].rearrange("p (a b) -> p a b", b=DH0)).then_inc(qkv_ev_v, 1)

            def center0(i):
                bank = B[i % 2][:].rearrange("p (a b) -> p a b", b=P)
                dve.wait_ge(s_mm, i + 1)
                link(nc.vector.tensor_reduce(mx[:, i % 2], bank, AX, ALU.max))
                if i >= 2:
                    dve.wait_ge(s_T, i - 1)
                nc.vector.tensor_tensor(pb[:, i % 2], bank, over(mx[:, i % 2], P), ALU.subtract).then_inc(s_sub, 1)

            def norm0(i):
                t, par = i // 2, i % 2
                dve.wait_ge(s_av, i + 1)
                o = B[4 + par][:, 0:4 * (DH0 + 1)].rearrange("p (a b) -> p a b", b=DH0 + 1)
                link(nc.vector.reciprocal(rs[:, par], o[:, :, DH0]))
                if t >= 2:
                    dve.wait_ge(s_oTp, t - 1)
                nc.vector.tensor_tensor(on[:, t % 2].rearrange("p (j two) d -> p two j d", two=2)[:, par],
                                        o[:, :, 0:DH0], over(rs[:, par], DH0), ALU.mult).then_inc(s_on, 1)

            def residual0(t):
                dve.wait_ge(s_proj, t + 1)
                dve.wait_ge(hb_done, NT)
                nc.vector.scalar_tensor_tensor(h[:, t], B[7][:, tile(t % 2)], cout[:], hb[:, t], ALU.mult,
                                               ALU.add).then_inc(s_hup, 1)
                dve.wait_ge(s_hup, t + 1)
                norm_stats(1, t)

            center0(0)
            for i in range(8):
                if i + 1 < 8:
                    center0(i + 1)
                if i >= 3 and i % 2 == 1:
                    residual0((i - 3) // 2)
                norm0(i)
                dve.wait_ge(w0_hi, i + 1)
                nc.vector.scalar_tensor_tensor(w0l[:, 1024 * i:1024 * (i + 1)], st0[:, i, :], WS,
                                               w0h[:, 1024 * i:1024 * (i + 1)], ALU.mult, ALU.subtract).then_inc(w0_lo, 1)
            residual0(3)
            norm_apply(1)

            dve.wait_ge(xnT_a, 2)
            nc.vector.tensor_tensor(xfl[:], B[0][:], xfh[:], ALU.subtract).then_inc(xfl_v, 1)
            dve.wait_ge(r0_mm, 1)
            lg = lg0[:, :, 0:E0]
            link(nc.vector.scalar_tensor_tensor(lg, B[1][:, 0:NT * E0].rearrange("p (a b) -> p a b", b=E0), 1.0 / WS,
                                                along(row("br"), NT), ALU.mult, ALU.add))
            link(nc.vector.tensor_reduce(lgm[:], lg, AX, ALU.max))
            nc.vector.tensor_tensor(lg, lg, over(lgm[:], E0), ALU.subtract).then_inc(r0_sub, 1)
            dve.wait_ge(r0_exp, 1)
            for t in range(NT):
                last = nc.vector.max(top8[:, t], lg0[:, t, 0:E0])
            link(last)
            link(nc.vector.memset(top8[:, :, 2:8], -3.0))
            for t in range(NT):
                last = nc.vector.match_replace(rep[:, t, 0:E0], top8[:, t], lg0[:, t, 0:E0], -1.0)
            link(last)
            gt = gates[:, :, 0:E0]
            link(nc.vector.scalar_tensor_tensor(gt, rep[:, :, 0:E0], 0.0, lg, ALU.is_lt, ALU.mult))
            link(nc.vector.tensor_reduce(lgs[:], gt, AX, ALU.add))
            link(nc.vector.reciprocal(lgs[:], lgs[:]))
            link(nc.vector.tensor_tensor(gt, gt, over(lgs[:], E0), ALU.mult))
            link(nc.vector.tensor_copy(g16[:, :, 0:E0], gt))
            nc.vector.tensor_copy(gcb[:, :, 0:E0], g16[:, :, 0:E0])
            link(nc.vector.tensor_tensor(gcb[:, :, E0:2 * E0], gt, g16[:, :, 0:E0], ALU.subtract))
            nc.vector.tensor_scalar(gcb[:, :, E0:2 * E0], gcb[:, :, E0:2 * E0], LS, None, ALU.mult).then_inc(r0_gcb, 1)
            dve.wait_ge(d_l1w, 32)
            nc.vector.tensor_scalar(b2_sb[:], b2_sb[:], con("b2scale")[0:16], None, ALU.mult).then_inc(r0_gcb, 1)

            def hi_lo(n, slot, used):
                dve.wait_ge(relu0, n + 1)
                if used:
                    dve.wait_ge(down0, n - 3)
                nc.vector.tensor_copy(hh[:, slot], r[:, slot % 2]).then_inc(hi0, 1)
                dve.wait_ge(hi0, n + 1)
                nc.vector.tensor_tensor(hl[:, slot, 0:256], r[:, slot % 2, 0:256], hh[:, slot, 0:256],
                                        ALU.subtract).then_inc(lo0v, 1)

            def gate0(e, b, used):
                dve.wait_ge(y0, e + 1)
                dve.wait_ge(gev0, e + 1)
                if used:
                    dve.wait_ge(acc0, e - 1)
                nc.vector.scalar_tensor_tensor(yt[:, b], B[7 * (1 - b)][:], 1.0 / (WS * HS), G[:, b], ALU.mult,
                                               ALU.mult).then_inc(yt0, 1)

            for n in range(4):
                hi_lo(n, n, False)
            with dve.Fori(0, 3) as m:
                for k in range(8):
                    hi_lo(8 * m + 4 + k, k % 4, True)
                    if k == 2:
                        gate0(2 * m, 0, False)
                    if k == 6:
                        gate0(2 * m + 1, 1, False)
            for n in range(28, 32):
                hi_lo(n, n % 4, True)
                if n == 30:
                    gate0(6, 0, True)
            gate0(7, 1, True)
            for t in range(NT):
                dve.wait_ge(f0_T, t + 1)
                nc.vector.tensor_tensor(h[:, t], h[:, t], B[1 + t][:, 0:P], ALU.add).then_inc(f0_h, 1)
                dve.wait_ge(f0_h, t + 1)
                norm_stats(2, t)
            norm_apply(2)

            dve.wait_ge(w_sq, 1)
            nc.vector.tensor_copy(wtm[:], B[1][:])
            link(nc.vector.tensor_reduce(ms[:], wsq[:].rearrange("p (a b) -> p a b", b=DH1), AX, ALU.add))
            nc.vector.tensor_scalar(ms[:], ms[:], 1.0 / DH1, EPS_RMS, ALU.mult, ALU.add).then_inc(w_ms, 1)
            dve.wait_ge(w_inv, 1)

            def heads(ap):
                return ap.rearrange("p (a b) -> p a b", b=DH1)
            link(nc.vector.tensor_tensor(heads(wtm[:]), heads(wtm[:]), over(ms[:], DH1), ALU.mult))
            nc.vector.tensor_tensor(heads(qn[:]), heads(wtm[:]), along(row("g1"), 32), ALU.mult).then_inc(qk_n, 1)
            nc.vector.tensor_tensor(heads(kn[:]), heads(wtm[:]), along(row("g2"), 32), ALU.mult).then_inc(qk_n, 1)
            for t in range(NT):
                nc.vector.tensor_tensor(vA[:, t, :, 0:DH1], heads(wtm[:, tile(t)]), along(row("g3"), H), ALU.mult)
            link(nc.vector.memset(vA[:, :, :, DH1:DH1 + 1], 1.0))
            dve.wait_ge(qk_T, 2)
            for hd in range(4):
                nc.vector.tensor_scalar(big[:, hd, :], B[3][:], con("heads")[:, hd:hd + 1], None,
                                        ALU.mult).then_inc(kM_v, 1)

            def center1(i):
                for bank, m, dst, used, done in ((B[i % 2], mx, pb, t_T, t_subr), (B[4 + i % 2], mxc, pc, t_av, t_subc)):
                    b = bank[:].rearrange("p (a b) -> p a b", b=P)
                    if done is t_subr:
                        dve.wait_ge(t_mm, 2 * i + 1)
                    else:
                        dve.wait_ge(t_mm, 2 * i + 2)
                    link(nc.vector.tensor_reduce(m[:, i % 2], b, AX, ALU.max))
                    if i >= 2:
                        dve.wait_ge(used, i - 1)
                    nc.vector.tensor_tensor(dst[:, i % 2], b, over(m[:, i % 2], P), ALU.subtract).then_inc(done, 1)

            def column_sums(i):
                t, g = i // 2, i % 2
                dve.wait_ge(t_expc, i + 1)
                link(nc.vector.tensor_reduce(cs[:, i % 2], pc[:, i % 2], AX, ALU.add))
                link(nc.vector.reciprocal(cs[:, i % 2], cs[:, i % 2]))
                nc.vector.tensor_tensor(vcs[:, i % 2], vA[:, t, 4 * g:4 * g + 4, 0:DH1], over(cs[:, i % 2], DH1),
                                        ALU.mult).then_inc(t_vcs, 1)

            def combine1(i):
                t, g = i // 2, i % 2
                dve.wait_ge(t_av, i + 1)
                o = B[6][:, 256 * g:256 * g + 4 * (DH1 + 1)].rearrange("p (a b) -> p a b", b=DH1 + 1)
                oc = B[6][:, 256 * g + 128:256 * g + 192].rearrange("p (a b) -> p a b", b=DH1)
                link(nc.vector.reciprocal(rs[:, g], o[:, :, DH1]))
                y = on[:, t % 2, g, :].rearrange("p (a b) -> p a b", b=DH1)
                if t >= 2:
                    dve.wait_ge(t_yTp, t - 1)
                link(nc.vector.tensor_tensor(y, o[:, :, 0:DH1], over(rs[:, g], DH1), ALU.mult))
                nc.vector.tensor_tensor(y, y, oc, ALU.add).then_inc(t_y, 1)

            def residual1(t):
                dve.wait_ge(t_proj, t + 1)
                nc.vector.tensor_tensor(h[:, t], h[:, t], B[7][:, P + P * (t % 2):2 * P + P * (t % 2)],
                                        ALU.add).then_inc(t_hup, 1)
                dve.wait_ge(t_hup, t + 1)
                norm_stats(3, t)

            center1(0)
            for i in range(8):
                column_sums(i)
                if i + 1 < 8:
                    center1(i + 1)
                if i >= 3 and i % 2 == 1:
                    residual1((i - 3) // 2)
                combine1(i)
            residual1(3)
            norm_apply(3)

            def lo_weights(p, slot):
                dve.wait_ge(w1_hi, p + 1)
                nc.vector.scalar_tensor_tensor(w1l[:, slot], st1[:, bass.ds(PW * p, PW)], WS, w1h[:, slot], ALU.mult,
                                               ALU.subtract).then_inc(w1_lo, 1)

            lo_weights(0, 0)
            lo_weights(1, 1)
            dve.wait_ge(xnT_a, 4)
            nc.vector.tensor_tensor(xfl[:], B[0][:], xfh[:], ALU.subtract).then_inc(xfl_v, 1)
            dve.wait_ge(r1_mm, 1)
            bank = B[1][:, 0:NT * ER].rearrange("p (a b) -> p a b", b=ER)
            link(nc.vector.tensor_reduce(lgm[:], bank, AX, ALU.max))
            nc.vector.tensor_tensor(lg0[:], bank, over(lgm[:], ER), ALU.subtract).then_inc(r1_sub, 1)

            def hidden(p, b, used, gated=True):
                dve.wait_ge(silu1, p + 1)
                dve.wait_ge(h3mm, p + 1)
                if used:
                    dve.wait_ge(r1, p - 1)
                if isinstance(p, int) and p == 2:
                    dve.wait_ge(lo1, 1)
                nc.vector.scalar_tensor_tensor(u[:, b], B[5 + b][:], HS / WS, s[:, b], ALU.mult, ALU.mult).then_inc(u1, 1)
                if gated:
                    dve.wait_ge(u1, p + 1)
                    dve.wait_ge(g1mm, p)
                    if used:
                        dve.wait_ge(lo1, p - 1)
                    nc.vector.tensor_tensor(r[:, b], u[:, b], B[[7, 2][b] if b else 7][:], ALU.mult).then_inc(r1, 1)

            dve.wait_ge(r1_exp, 1)
            hidden(0, 0, False, gated=False)
            link(nc.vector.tensor_reduce(lgs[:], lg0[:], AX, ALU.add))
            link(nc.vector.reciprocal(lgs[:], lgs[:]))
            link(nc.vector.tensor_tensor(lg0[:], lg0[:], over(lgs[:], ER), ALU.mult))
            link(nc.vector.tensor_tensor(bia[:], lg0[:], along(row("gate_bias"), NT), ALU.add))
            for t in range(NT):
                last = nc.vector.max(top8[:, t], bia[:, t])
            link(last)
            link(nc.vector.memset(top8[:, :, TOPK1:8], -2.0e38))
            for t in range(NT):
                last = nc.vector.match_replace(rep[:, t], top8[:, t], bia[:, t], -3.0e38)
            link(last)
            link(nc.vector.scalar_tensor_tensor(gates[:], rep[:], -2.5e38, lg0[:], ALU.is_lt, ALU.mult))
            link(nc.vector.tensor_copy(g16[:], gates[:]))
            nc.vector.tensor_copy(gcb[:, :, 0:ER], g16[:])
            link(nc.vector.tensor_tensor(gcb[:, :, ER:2 * ER], gates[:], g16[:], ALU.subtract))
            nc.vector.tensor_scalar(gcb[:, :, ER:2 * ER], gcb[:, :, ER:2 * ER], LS, None, ALU.mult).then_inc(r1_gcb, 1)
            dve.wait_ge(r1_gcb, 1)
            nc.vector.tensor_copy(lgm[:], lgs[:]).then_inc(r1, 1)
            lo_weights(2, 2)
            for p in range(1, 4):
                hidden(p, p % 2, p >= 2)
                lo_weights(p + 2, (p + 2) % 4)
            with dve.Fori(0, 6) as m:
                for k in range(4):
                    hidden(4 * m + 4 + k, k % 2, True)
                    lo_weights(4 * m + 6 + k, (k + 2) % 4)
            for p in range(28, NP):
                hidden(p, p % 2, True)
                if p + 2 < NP:
                    lo_weights(p + 2, (p + 2) % 4)
            for t in range(NT):
                dve.wait_ge(y1_T, t + 1)
                nc.vector.tensor_tensor(outs[:, t], h[:, t], B[1 + t][:, 0:P], ALU.add).then_inc(out_v, 1)

        @block.tensor
        def _(pe):
            def mm(o, l, rr, start=True, stop=True):
                return nc.tensor.matmul(o, l, rr, start=start, stop=stop)

            pe.wait_ge(d_tokw, 16)
            for t in range(NT):
                pe.wait_ge(d_x[t], 16)
                for c in range(KC):
                    last = mm(B[t][:, 0:P], x_sb[:, t, c, :], tokw[:, c, :], c == 0, c == KC - 1)
                last.then_inc(tok_done, 1)

            def transpose_norm(k):
                for t in range(NT):
                    pe.wait_ge(ln_xn, NT * k + t + 1)
                    nc.tensor.transpose(B[0][:, tile(t)], xn[:, t], ident).then_inc(ln_T, 1)

            pe.wait_ge(d_cst, 16)
            transpose_norm(0)
            pe.wait_ge(d_wqT, 16)
            pe.wait_ge(d_col, 16)
            for c in range(12):
                mm(B[6][:, c:c + 1], wqkvT_sb[:, P * c:P * c + P], col("u_qkv"))
            pe.wait_ge(d_wo, 32)
            for c in range(C0):
                last = mm(B[6][:, 12:13], woT_sb[:, c, :], col("u_out")[:, c:c + 1], c == 0, c == C0 - 1)
            last.then_inc(sn_a, 1)
            pe.wait_ge(xnT_a, 1)
            for k in range(12):
                if k >= 4:
                    if k % 2 == 0:
                        pe.wait_ge(qkv_ev_a, (k - 4) // 2 + 1)
                    else:
                        pe.wait_ge(qkv_ev_v, (k - 5) // 2 + 1)
                if k < 8:
                    last = mm(B[2 + k % 4][:], wqkvT_sb[:, P * k:P * k + P], xnT[:])
                else:
                    last = mm(B[2 + k % 4][:], xnT[:, tile(k - 8)], wqkvT_sb[:, 2 * INNER:3 * INNER])
                last.then_inc(qkv_mm, 1)
                if k == 0:
                    pe.wait_ge(sn_acopy, 1)
                    pe.wait_ge(d_wqN, 16)
                    for c in range(12):
                        mm(B[7][:, 0:1], wqkvN_sb[:, c, :], sna[:, c:c + 1], c == 0, c == 11)
                    for c in range(C0):
                        last = mm(B[7][:, 1 + c:2 + c], woN_sb[:, P * c:P * c + P], sna[:, 12:13])
                    last.then_inc(sn_b, 1)
                if k == 1:
                    pe.wait_ge(pool_const, 1)
                    pe.wait_ge(sn_sums, 1)
                    mm(B[7][:, 8:12], ones[:], sn4[:]).then_inc(sn_tot, 1)

            def scores0(i):
                t, par = i // 2, i % 2
                bank = B[i % 2]
                if i >= 2:
                    pe.wait_ge(s_sub, i - 1)
                mm(bank[:], negI[:], m0b[:].rearrange("p a b -> p (a b)"), True, False)
                for j in range(4):
                    last = mm(bank[:, tile(j)], big[64 * par:64 * par + 64, j, tile(t)],
                              big[64 * par:64 * par + 64, 4 + j, tile(t)], False, j == 3)
                last.then_inc(s_mm, 1)

            def transpose_p(i, exped, done):
                pe.wait_ge(exped, i + 1)
                for j in range(4):
                    last = nc.tensor.transpose(B[2 + i % 2][:, tile(j)], pb[:, i % 2, j, :], ident)
                last.then_inc(done, 1)

            def values0(i):
                t, par = i // 2, i % 2
                pe.wait_ge(s_pT, i + 1)
                if i >= 2:
                    pe.wait_ge(s_on, i - 1)
                for j in range(4):
                    last = mm(B[4 + par][:, 65 * j:65 * j + 65], pT[:, i % 2, j, :], vA[:, t, 2 * j + par, :])
                last.then_inc(s_av, 1)

            def transpose_o(t):
                pe.wait_ge(s_on, 2 * t + 2)
                if t >= 1:
                    pe.wait_ge(s_oT, t)
                flat = on[:, t % 2].rearrange("p a b -> p (a b)")
                for c in range(4):
                    last = nc.tensor.transpose(B[6][:, tile(c)], flat[:, tile(c)], ident)
                last.then_inc(s_oTp, 1)

            def project0(t):
                pe.wait_ge(s_oT, t + 1)
                if t >= 1:
                    pe.wait_ge(s_hup, t)
                for c in range(4):
                    last = mm(B[7][:, tile(t % 2)], oT[:, t % 2, c, :], woT_sb[:, c, :], c == 0, c == 3)
                last.then_inc(s_proj, 1)

            pe.wait_ge(mask_ready, 2)
            pe.wait_ge(qkv_ev_a, 6)
            pe.wait_ge(qkv_ev_v, 6)
            scores0(0)
            scores0(1)
            for i in range(10):
                if i < 8:
                    transpose_p(i, s_exp, s_T)
                    if i + 2 < 8:
                        scores0(i + 2)
                if i >= 2 and i % 2 == 0:
                    transpose_o((i - 2) // 2)
                if i >= 3 and i % 2 == 1:
                    project0((i - 3) // 2)
                if i < 8:
                    values0(i)

            transpose_norm(1)
            pe.wait_ge(xfl_v, 1)

            def router(n, c0, done):
                for t in range(NT):
                    o = B[1][:, n * t:n * t + n]
                    mm(o, xfh[:, tile(t)], wrs[:, 0, c0:c0 + n], True, False)
                    mm(o, xfl[:, tile(t)], wrs[:, 0, c0:c0 + n], False, False)
                    last = mm(o, xfh[:, tile(t)], wrs[:, 1, c0:c0 + n], False, True)
                last.then_inc(done, 1)

            router(E0, ER, r0_mm)

            def up(n, e, c, used):
                if used:
                    pe.wait_ge(relu0, n - 1)
                o = B[3 + c % 2][:]
                hi = w0h[:, bass.ds(1024 * e + P * c, P)]
                lo = w0l[:, bass.ds(1024 * e + P * c, P)]
                mm(o, hi, xfh[:], True, False)
                mm(o, hi, xfl[:], False, False)
                mm(o, lo, xfh[:], False, True).then_inc(up0, 1)

            def down(n, e, c, b, used):
                pe.wait_ge(lo0v, n + 1)
                pe.wait_ge(lo0p, n + 1)
                if c == 0 and used:
                    pe.wait_ge(yt0, e - 1)
                o = B[7 * (1 - b)][:]
                hi = w0h[:, bass.ds(1024 * e + F0 + P * c, P)]
                lo = w0l[:, bass.ds(1024 * e + F0 + P * c, P)]
                mm(o, hi, hh[:, c, :], c == 0, False)
                mm(o, hi, hl[:, c, :], False, False)
                last = mm(o, lo, hh[:, c, :], False, c == 3)
                last.then_inc(down0, 1)

            def y_done(e):
                pass

            def gate_mm(e, b, used):
                if used:
                    pe.wait_ge(gev0, e - 1)
                mm(B[5 + b][:], sel0[:].rearrange("p a b -> p (a b)")[:, bass.ds(P * e, P)], gT[:]).then_inc(gmm0, 1)

            pe.wait_ge(w0_hi, E0)
            pe.wait_ge(w0_lo, E0)
            up(0, 0, 0, False)
            up(1, 0, 1, False)
            up(2, 0, 2, True)
            pe.wait_ge(r0_gcb, 2)
            for t in range(NT):
                last = nc.tensor.transpose(B[2][0:16, tile(t)], gcb[:, t, 0:16], ident)
            last.then_inc(r0_T, 1)
            up(3, 0, 3, True)
            pe.wait_ge(act_setup, 2)
            pe.wait_ge(r0_gT, 1)
            mm(B[1][:], b2_sb[:], gT32[:]).then_inc(r0_b2, 1)
            gate_mm(0, 0, False)
            down(0, 0, 0, 0, False)
            with pe.Fori(0, 3) as m:
                for k in range(8):
                    up(8 * m + 4 + k, 2 * m + 1 + k // 4, k % 4, True)
                    if k == 3:
                        gate_mm(2 * m + 1, 1, False)
                    if k == 7:
                        gate_mm(2 * m + 2, 0, True)
                    down(8 * m + 1 + k, 2 * m + (1 + k) // 4, (1 + k) % 4, ((1 + k) // 4) % 2, False)
                    if k in (2, 6):
                        pe.wait_ge(down0, 8 * m + 2 + k)
                        nc.tensor.nop().then_inc(y0, 1)
            for n in range(28, 35):
                if n < 32:
                    up(n, 7, n % 4, True)
                if n == 31:
                    gate_mm(7, 1, True)
                down(n - 3, (n - 3) // 4, (n - 3) % 4, ((n - 3) // 4) % 2, True)
                if n % 4 == 2:
                    pe.wait_ge(down0, n - 2)
                    nc.tensor.nop().then_inc(y0, 1)
            pe.wait_ge(acc0, E0)
            for t in range(NT):
                nc.tensor.transpose(B[1 + t][:, 0:P], acc[:, tile(t)], ident).then_inc(f0_T, 1)

            transpose_norm(2)
            pe.wait_ge(w1_sum, 1)
            pe.wait_ge(xnT_a, 3)
            for t in range(NT):
                mm(B[1][:, tile(t)], xnT[:, tile(t)], w1t[:]).then_inc(w_mm, 1)
            pe.wait_ge(qk_n, 1)
            for t in range(NT):
                last = nc.tensor.transpose(B[2][:, tile(t)], qn[:, tile(t)], ident)
            last.then_inc(qk_T, 1)
            pe.wait_ge(qk_n, 2)
            for bank in (B[3], B[4]):
                for t in range(NT):
                    last = nc.tensor.transpose(bank[:, tile(t)], kn[:, tile(t)], ident)
            last.then_inc(qk_T, 1)

            def scores1(i):
                t, g = i // 2, i % 2
                mask = m1b[:].rearrange("p a b -> p (a b)")
                if i >= 2:
                    pe.wait_ge(t_subr, i - 1)
                mm(B[i % 2][:], negI[:], mask, True, False)
                mm(B[i % 2][:].rearrange("p (a b) -> p a b", b=P), qT1[:, tile(t)],
                   big[:, 4 * g:4 * g + 4, tile(t)], False, True).then_inc(t_mm, 1)
                if i >= 2:
                    pe.wait_ge(t_subc, i - 1)
                mm(B[4 + i % 2][:], negI[:], mask, True, False)
                for j in range(4):
                    last = mm(B[4 + i % 2][:, tile(j)], big[:, 4 * g + j, tile(t)], qT1[:, tile(t)], False, j == 3)
                last.then_inc(t_mm, 1)

            def values1(i):
                t, g = i // 2, i % 2
                pe.wait_ge(t_pT, i + 1)
                if i >= 1:
                    pe.wait_ge(t_y, i)
                for j in range(4):
                    mm(B[6][:, 256 * g + 17 * j:256 * g + 17 * j + 17], pT[:, i % 2, j, :], vA[:, t, 4 * g + j, 0:17])
                pe.wait_ge(t_vcs, i + 1)
                for j in range(4):
                    last = mm(B[6][:, 256 * g + 128 + 16 * j:256 * g + 144 + 16 * j], pc[:, i % 2, j, :],
                              vcs[:, i % 2, j, :])
                last.then_inc(t_av, 1)

            def transpose_y(t):
                pe.wait_ge(t_y, 2 * t + 2)
                if t >= 1:
                    pe.wait_ge(t_hup, t)
                flat = on[:, t % 2, 0:2, :].rearrange("p a b -> p (a b)")
                nc.tensor.transpose(B[7][:, 0:P], flat, ident).then_inc(t_yTp, 1)

            def project1(t):
                pe.wait_ge(t_yT, t + 1)
                mm(B[7][:, P + P * (t % 2):2 * P + P * (t % 2)], oT[:, t % 2, 0, :], w1n[:]).then_inc(t_proj, 1)

            pe.wait_ge(qT_ev, 1)
            pe.wait_ge(kM_v, 4)
            pe.wait_ge(kM_a, 4)
            scores1(0)
            scores1(1)
            for i in range(10):
                if i < 8:
                    transpose_p(i, t_expr, t_T)
                    if i + 2 < 8:
                        scores1(i + 2)
                if i >= 2 and i % 2 == 0:
                    transpose_y((i - 2) // 2)
                if i >= 3 and i % 2 == 1:
                    project1((i - 3) // 2)
                if i < 8:
                    values1(i)

            transpose_norm(3)
            pe.wait_ge(xfl_v, 2)
            router(ER, 0, r1_mm)

            def pair_up(p, slot, used):
                pe.wait_ge(w1_lo, p + 1)
                for b0, c0, bank_free, done in ((3, 0, silu1, h1mm), (5, P, u1, h3mm)):
                    if used:
                        pe.wait_ge(bank_free, p - 1)
                    o = B[b0 + slot % 2][:]
                    mm(o, w1h[:, slot, c0:c0 + P], xfh[:], True, False)
                    mm(o, w1h[:, slot, c0:c0 + P], xfl[:], False, False)
                    mm(o, w1l[:, slot, c0:c0 + P], xfh[:], False, True).then_inc(done, 1)

            def pair_gate(p, slot, used):
                if used:
                    pe.wait_ge(r1, p - 1)
                flat = sel1[:].rearrange("p a b -> p (a b)")
                mm(B[2 if slot % 2 else 7][:], flat[:, bass.ds(P * p - P, P)], gT[:]).then_inc(g1mm, 1)

            def pair_down(p, slot, first=False, last=False):
                pe.wait_ge(lo1, p + 1)
                b = slot % 2
                mm(B[0][:], w1h[:, slot, 2 * P:3 * P], hh[:, b, :], first, False)
                mm(B[0][:], w1h[:, slot, 2 * P:3 * P], hl[:, b, :], False, False)
                mm(B[0][:], w1l[:, slot, 2 * P:3 * P], hh[:, b, :], False, last).then_inc(down1, 1)

            pair_up(0, 0, False)
            pair_up(1, 1, False)
            pe.wait_ge(r1_gcb, 1)
            for t in range(NT):
                last = nc.tensor.transpose(B[2][:, tile(t)], gcb[:, t, :], ident)
            last.then_inc(r1_T, 1)
            pe.wait_ge(r1_gT, 1)
            pair_gate(1, 1, False)
            for p in range(2, 4):
                pair_up(p, p, True)
                pair_gate(p, p, p >= 3)
                pair_down(p - 2, p - 2, first=(p == 2))
            with pe.Fori(0, 6) as m:
                for k in range(4):
                    pair_up(4 * m + 4 + k, k, True)
                    pair_gate(4 * m + 4 + k, k, True)
                    pair_down(4 * m + 2 + k, (k + 2) % 4)
            for p in range(28, NP):
                pair_up(p, p % 4, True)
                pair_gate(p, p % 4, True)
                pair_down(p - 2, (p - 2) % 4)
            pair_down(31, 3)
            pair_down(32, 0, last=True)
            pe.wait_ge(down1, NP)
            nc.tensor.nop().then_inc(y1, 1)
            pe.wait_ge(y1_ev, 1)
            for t in range(NT):
                nc.tensor.transpose(B[1 + t][:, 0:P], acc[:, tile(t)], ident).then_inc(y1_T, 1)


def kernel(**inputs):
    import concourse.bacc as bacc
    import numpy as np
    from concourse.bass_utils import run_bass_kernel_spmd as run

    v = {k: np.asarray(a) for k, a in inputs.items()}
    f = np.float32
    x = v["x"].reshape(32, 3, 4, 16, 4, 16).transpose(0, 2, 4, 1, 3, 5).reshape(NT, P, KC, P).transpose(0, 3, 2, 1)
    tokWT = v["L0_tok_W"].reshape(P, KC, P).transpose(2, 1, 0)
    rows = np.concatenate([v[n].reshape(1, -1) for n in (
        "L0_tok_b", "L0_attn_b_out", "L0_ffn_br", "L1_attn_g1", "L1_attn_g2", "L1_attn_g3", "L1_ffn_gate_bias",
        "L0_attn_sigma_qkv", "L0_attn_sigma_out", "L0_attn_temperature")], axis=1)
    cols = np.concatenate([v["L0_attn_u_qkv"].reshape(P, 1), v["L0_attn_u_out"].reshape(C0, P).T,
                           v["L0_ffn_b1"].reshape(E0 * C0, P).T, v["L0_ffn_Wr"], v["L1_ffn_g_w"].T], axis=1)
    w = v["L0_attn_w_qkv"]
    wo = v["L0_attn_w_out"]
    w1 = v["L0_ffn_W1"]
    w2 = v["L0_ffn_W2"].reshape(E0, C0, P, P).transpose(0, 2, 1, 3).reshape(E0, P, F0)
    l1w = np.stack([v["L1_attn_qkv_w"], v["L1_attn_delta_w"], v["L1_attn_qkv_w"].T, v["L1_attn_delta_w"].T], axis=1)
    e1, e3 = (v[n].reshape(NP, 2, P, 64).transpose(0, 2, 1, 3).reshape(NP, P, P) for n in ("L1_ffn_w1", "L1_ffn_w3"))
    e2 = v["L1_ffn_w2"].reshape(NP, P, P)
    wl1 = np.concatenate([e1, e3, e2], axis=2).reshape(NP // 3, 3, P, PW).transpose(0, 2, 1, 3)
    i = np.arange(P)
    other = (i[:, None] // 16 != i[None, :] // 16).astype(f)
    ident = np.eye(P, dtype=f)
    pick1 = np.zeros((P, ER), f)
    pick1[np.arange(ER), np.arange(ER)] = 1
    pick1[ER + np.arange(ER), np.arange(ER)] = 2.0 ** -11
    pick0 = np.zeros((P, E0), f)
    pick0[np.arange(E0), np.arange(E0)] = 1
    pick0[E0 + np.arange(E0), np.arange(E0)] = 2.0 ** -11
    heads = (i[:, None] // DH1 == np.arange(H)[None, :]).astype(f)
    b2s = np.ones((P, 1), f)
    b2s[E0:16] = 2.0 ** -11
    consts = np.concatenate([ident, np.maximum(other, ident), other, pick1, pick0, heads, b2s], axis=1)

    arrays = {"xT": x.reshape(NT, P, KC * P), "tokWT": tokWT.reshape(P, KC * P), "rows": rows, "cols": cols,
              "consts": consts, "wqkvT": w.T, "wqkvN": w.reshape(12, P, P).transpose(1, 0, 2).reshape(P, 12 * P),
              "woT": wo.T.reshape(C0, P, P).transpose(1, 0, 2).reshape(P, C0 * P), "woN": wo,
              "l1w": l1w.reshape(P, 4 * P), "b2x": np.concatenate([v["L0_ffn_b2"]] * 2, axis=0),
              "wl0": np.concatenate([w1, w2], axis=2), "wl1": wl1.reshape(NP // 3, P, 3 * PW)}
    arrays = {k: np.ascontiguousarray(a) for k, a in arrays.items()}
    nc = bacc.Bacc("TRN2", target_bir_lowering=False, num_devices=1)
    args = [nc.dram_tensor(k, a.shape, mybir.dt.from_np(a.dtype), kind="ExternalInput").ap() for k, a in arrays.items()]
    out = nc.dram_tensor("out", (NT, P, P), F32, kind="ExternalOutput").ap()
    tower(nc, *args, out)
    res = run(nc, [arrays], core_ids=[0])
    return res.results[0]["out"].reshape(32, 16, P)
```

```python
from contextlib import ExitStack

import concourse.bass as bass
from concourse import mybir

F32 = mybir.dt.float32
F16 = mybir.dt.float16
BF16 = mybir.dt.bfloat16
ALU = mybir.AluOpType
ACT = mybir.ActivationFunctionType
AX = mybir.AxisListType.X

P = 128
NT = 4
N = NT * P
KC = 6
H = 8
DH0, DH1 = 64, 16
INNER = H * DH0
E0, F0 = 8, 512
C0 = F0 // P
NP = 33
ER = 64
TOPK1 = 6
RING = 6
ACT_UNITS = [0, 2, 4, 5, 6, 7, 8, 10]
DVE_UNITS = [1, 3, 4, 5, 6, 7, 9, 11]
PW = 3 * P
BIG = float(2 ** 100)
WS, HS, LS = 64.0, 16.0, 2048.0
EPS_LN, EPS_RMS = 1e-5, 1.1920929e-07

ROW = {"tok_b": (0, 128), "b_out": (128, 256), "br": (256, 264), "g1": (264, 280), "g2": (280, 296),
       "g3": (296, 312), "gate_bias": (312, 376), "sigma": (376, 378), "temp": (378, 379)}
ROWN = 379
COL = {"u_qkv": (0, 1), "u_out": (1, 5), "b1": (5, 37), "wr": (37, 45), "gw": (45, 109)}
COLN = 109
CST = {"ident": (0, 128), "mask0": (128, 160), "mask1": (160, 192), "pick1": (192, 256), "pick0": (256, 264),
       "heads": (264, 272), "b2scale": (272, 273)}
CSTN = 273


def tower(nc, xT, tokWT, rows, cols, consts, wqkvT, wqkvN, woT, woN, l1w, b2x, wl0, wl1, out):
    with ExitStack() as ctx:
        def sb(name, shape, dt=F32):
            return ctx.enter_context(nc.sbuf_tensor(name, shape, dt))

        def sem(name):
            return ctx.enter_context(nc.semaphore(name))

        x_sb = sb("x_sb", [P, NT, KC, P])
        tokw = sb("tokw", [P, KC, P])
        rows_sb = sb("rows_sb", [P, ROWN])
        cols_sb = sb("cols_sb", [P, COLN])
        cst = sb("cst", [P, CSTN])
        wqkvT_sb = sb("wqkvT_sb", [P, 3 * INNER])
        wqkvN_sb = sb("wqkvN_sb", [P, 3 * INNER // P, P])
        woT_sb = sb("woT_sb", [P, C0, P])
        woN_sb = sb("woN_sb", [P, INNER])
        l1w_sb = sb("l1w_sb", [P, 4, P])
        w1n = sb("w1n", [P, P])
        w1t = sb("w1t", [P, P])
        b2_sb = sb("b2_sb", [16, P])
        stage = sb("stage", [P, NP * PW])
        st0 = stage[:, 0:E0 * 2 * F0].rearrange("p (a b) -> p a b", b=2 * F0)
        st1 = stage
        w0h = sb("w0h", [P, E0 * 2 * F0], F16)
        w0l = sb("w0l", [P, E0 * 2 * F0], F16)
        w1h = sb("w1h", [P, RING, PW], F16)
        w1l = sb("w1l", [P, RING, PW], F16)
        negI = sb("negI", [P, P], BF16)
        m0b = sb("m0b", [P, H, 32], BF16)
        m1b = sb("m1b", [P, H, 32], BF16)
        ones = sb("ones", [P, P])
        mhalf = sb("mhalf", [P, 32])
        phalf = sb("phalf", [P, 2])
        sel1 = sb("sel1", [P, ER, DH0], F16)
        sel0 = sb("sel0", [P, E0, P], F16)
        wrs = sb("wrs", [P, 2, ER + E0], F16)
        h = sb("h", [P, NT, P])
        hb = sb("hb", [P, NT, P])
        stats = sb("stats", [P, NT, 6])
        mv = sb("mv", [P, NT, 2])
        vpe = sb("vpe", [P, NT])
        rstd = sb("rstd", [P, NT])
        xn = sb("xn", [P, NT, P])
        xnT = sb("xnT", [P, N])
        xfh = sb("xfh", [P, N], F16)
        xfl = sb("xfl", [P, N], F16)
        big = sb("big", [P, 8, N])
        qT1 = sb("qT1", [P, N])
        vA = sb("vA", [P, NT, H, DH0 + 1])
        pb = sb("pb", [P, 2, H, 32])
        pc = sb("pc", [P, 2, H, 32])
        pk = sb("pk", [P, 2, H, 32])
        pT = sb("pT", [P, 2, H, P])
        on = sb("on", [P, 2, H, DH0])
        oT = sb("oT", [P, 2, 4, P])
        mx = sb("mx", [P, 2, H])
        mxc = sb("mxc", [P, 2, H])
        rs = sb("rs", [P, 2, H])
        cs = sb("cs", [P, 2, H])
        gram = sb("gram", [P, P])
        sna = sb("sna", [P, 2])
        snb = sb("snb", [P, 5])
        snb2 = sb("snb2", [P, 5])
        sn4 = sb("sn4", [P, 4])
        snr = sb("snr", [P, 8])
        etemp = sb("etemp", [P, 1])
        cexp = sb("cexp", [P, 1])
        cout = sb("cout", [P, 1])
        lg0 = sb("lg0", [P, NT, ER])
        lgm = sb("lgm", [P, NT])
        lgs = sb("lgs", [P, NT])
        top8 = sb("top8", [P, NT, 8])
        gates = sb("gates", [P, NT, ER])
        g16 = sb("g16", [P, NT, ER], F16)
        gT = sb("gT", [P, N], F16)
        gT32 = sb("gT32", [16, N])
        b1s = sb("b1s", [P, E0 * C0])
        ms = sb("ms", [P, 32])
        xf = x_sb[:].rearrange("p a b c -> p (a b c)")

        def two(ap):
            return ap.rearrange("p (a b) -> p a b", b=N)
        r, u, s = two(xf[:, 0:2 * N]), two(xf[:, 2 * N:4 * N]), two(xf[:, 4 * N:6 * N])
        G, acc = two(wqkvT_sb[:, 0:2 * N]), wqkvT_sb[:, 2 * N:3 * N]
        nf = wqkvN_sb[:].rearrange("p a b -> p (a b)")
        yt, wtm = two(nf[:, 0:2 * N]), nf[:, 2 * N:3 * N]
        wsq = tokw[:].rearrange("p a b -> p (a b)")[:, 0:N]
        qn, kn = pb[:].rearrange("p a b c -> p (a b c)"), pk[:].rearrange("p a b c -> p (a b c)")
        q0 = two(stage[:, 3 * PW * 8:3 * PW * 8 + 4 * N])
        bf = big[:].rearrange("p a b -> p (a b)")
        hh, hl = two(bf[:, 0:2 * N].bitcast(F16)), two(bf[:, 2 * N:4 * N].bitcast(F16))
        k0 = bf.rearrange("p (j b c d) -> p j b c d", j=4, c=2, d=32)
        v1 = vA[:].rearrange("p a b c -> p (a b c)")[:, 0:N]
        k1 = bf.rearrange("p (a h d) -> p a h d", h=H, d=32)
        outs = hb
        of = oT[:].rearrange("p a b c -> p (a b c)")
        gcb = of[:, 0:N].rearrange("p (a b) -> p a b", a=NT)
        rep, bia = (of[:, N + 256 * i:N + 256 * (i + 1)].rearrange("p (a b) -> p a b", a=NT) for i in (0, 1))

        B = [ctx.enter_context(nc.psum_tensor(f"bank{i}", [P, 512], F32)) for i in range(8)]

        def row(name):
            a, b = ROW[name]
            return rows_sb[:, a:b]

        def col(name):
            a, b = COL[name]
            return cols_sb[:, a:b]

        def con(name):
            a, b = CST[name]
            return cst[:, a:b]

        def over(ap, n):
            return ap.unsqueeze(2).broadcast_to([ap.shape[0], ap.shape[1], n])

        def along(ap, n):
            return ap.unsqueeze(1).broadcast_to([ap.shape[0], n, ap.shape[1]])

        def tile(t):
            return slice(P * t, P * t + P)

        ident = con("ident")

        d_col, d_row, d_cst, d_tokw = sem("d_col"), sem("d_row"), sem("d_cst"), sem("d_tokw")
        d_x = [sem(f"d_x{t}") for t in range(NT)]
        d_wqT, d_wqN, d_wo, d_l1w = sem("d_wqT"), sem("d_wqN"), sem("d_wo"), sem("d_l1w")
        d_w0 = [sem(f"d_w0_{e}") for e in range(E0)]
        d_w1 = [sem(f"d_w1_{c}") for c in range(NP // 3)]
        d_out = sem("d_out")
        pool_const = sem("pool_const")
        mask_ready = sem("mask_ready")
        act_setup = sem("act_setup")
        sn_gram, sn_acopy, sn_b, sn_sums, sn_tot, sn_ratio, sn_norm, sn_scales, temp_exp = (
            sem(n) for n in ("sn_gram", "sn_acopy", "sn_b", "sn_sums", "sn_tot", "sn_ratio", "sn_norm", "sn_scales",
                             "temp_exp"))
        tok_done, ln_var, ln_rstd, ln_xn, ln_T = (sem(n) for n in ("tok_done", "ln_var", "ln_rstd", "ln_xn", "ln_T"))
        xnT_a, xfl_v = sem("xnT_a"), sem("xfl_v")
        qkv_mm, qkv_ev_a, qkv_ev_v = sem("qkv_mm"), sem("qkv_ev_a"), sem("qkv_ev_v")
        s_mm, s_sub, s_exp, s_tr, s_xa, s_xp, s_av, s_on, s_oTp, s_oT, s_proj, s_hup, hb_done = (
            sem(n) for n in ("s_mm", "s_sub", "s_exp", "s_tr", "s_xa", "s_xp", "s_av", "s_on", "s_oTp", "s_oT",
                             "s_proj", "s_hup", "hb_done"))
        w0_hi = sem("w0_hi")
        w0_lo = sem("w0_lo")
        r0_mm, r0_sub, r0_exp, r0_gcb, r0_T, r0_gT, r0_b2, r0_acc = (
            sem(n) for n in ("r0_mm", "r0_sub", "r0_exp", "r0_gcb", "r0_T", "r0_gT", "r0_b2", "r0_acc"))
        up0, relu0, hi0, lo0v, lo0p, down0, gmm0, gev0, y0, yt0, acc0 = (
            sem(n) for n in ("up0", "relu0", "hi0", "lo0v", "lo0p", "down0", "gmm0", "gev0", "y0", "yt0", "acc0"))
        f0_T, f0_h = sem("f0_T"), sem("f0_h")
        w1_sum, w_mm, w_sq, w_ms, w_inv, qkv_n, qk_T, k1_v, qk_a = (
            sem(n) for n in ("w1_sum", "w_mm", "w_sq", "w_ms", "w_inv", "qkv_n", "qk_T", "k1_v", "qk_a"))
        t_mm, t_subr, t_subc, t_expr, t_expc, t_pk, t_pc, t_xv, t_xp, t_av, t_y, t_yTp, t_yT, t_proj, t_hup = (
            sem(n) for n in ("t_mm", "t_subr", "t_subc", "t_expr", "t_expc", "t_pk", "t_pc", "t_xv", "t_xp", "t_av",
                             "t_y", "t_yTp", "t_yT", "t_proj", "t_hup"))
        r1_mm, r1_sub, r1_exp, r1_gcb, r1_T, r1_gT = (
            sem(n) for n in ("r1_mm", "r1_sub", "r1_exp", "r1_gcb", "r1_T", "r1_gT"))
        w1_hi, w1_lo, h1mm, h3mm, g1mm, silu1, u1, r1, hi1, lo1, down1, y1, y1_ev, y1_T, out_v = (
            sem(n) for n in ("w1_hi", "w1_lo", "h1mm", "h3mm", "g1mm", "silu1", "u1", "r1", "hi1", "lo1", "down1",
                             "y1", "y1_ev", "y1_T", "out_v"))
        dve_step, pool_step, act_step = sem("dve_step"), sem("pool_step"), sem("act_step")

        block = ctx.enter_context(nc.Block())

        @block.sync
        def _(sp):
            sp.dma_start(cst[:], consts).then_inc(d_cst, 16)
            sp.dma_start(tokw[:], tokWT).then_inc(d_tokw, 16)
            sp.dma_start(cols_sb[:], cols).then_inc(d_col, 16)
            sp.dma_start(rows_sb[:], rows.broadcast_to([P, ROWN])).then_inc(d_row, 16)
            for t in range(NT):
                sp.dma_start(x_sb[:, t], xT[t]).then_inc(d_x[t], 16)
            sp.dma_start(wqkvN_sb[:], wqkvN).then_inc(d_wqN, 16)
            sp.dma_start(wqkvT_sb[:], wqkvT).then_inc(d_wqT, 16)
            sp.dma_start(woT_sb[:], woT).then_inc(d_wo, 16)
            sp.dma_start(woN_sb[:], woN).then_inc(d_wo, 16)
            for e in range(E0):
                sp.dma_start(st0[:, e], wl0[e]).then_inc(d_w0[e], 16)
            sp.dma_start(l1w_sb[:], l1w).then_inc(d_l1w, 16)
            sp.dma_start(b2_sb[:], b2x).then_inc(d_l1w, 16)
            for c in range(NP // 3):
                if c < 8:
                    sp.wait_ge(w0_lo, min(3 * PW * (c + 1) - 1, E0 * 1024 - 1) // 1024 + 1)
                elif c == 8:
                    sp.wait_ge(s_mm, NT)
                sp.dma_start(st1[:, 3 * PW * c:3 * PW * (c + 1)], wl1[c]).then_inc(d_w1[c], 16)
            for t in range(NT):
                sp.wait_ge(out_v, t + 1)
                sp.dma_start(out[t], outs[:, t]).then_inc(d_out, 16)
            sp.wait_ge(d_out, 16 * NT)

        @block.gpsimd
        def _(pool):
            nc.gpsimd.memset(ones[:], 1.0)
            nc.gpsimd.memset(mhalf[:], -0.5)
            nc.gpsimd.memset(phalf[:], 0.5)
            nc.gpsimd.memset(gT[:], 0.0)
            nc.gpsimd.memset(vA[:, :, :, DH0:DH0 + 1], 1.0)
            nc.gpsimd.memset(bf, 0.0)
            nc.gpsimd.memset(pT[:], 0.0).then_inc(pool_const, 1)

            def norm(k):
                for t in range(NT):
                    pool.wait_ge(ln_var, NT * k + t + 1)
                    nc.gpsimd.tensor_tensor(rstd[:, t:t + 1], vpe[:, t:t + 1], mhalf[:, 0:1],
                                            ALU.pow).then_inc(ln_rstd, 1)

            pool.wait_ge(pool_const, 1)
            norm(0)
            for t in range(NT):
                nc.gpsimd.tensor_tensor(hb[:, t], h[:, t], row("b_out"), ALU.add).then_inc(hb_done, 1)
            pool.wait_ge(sn_ratio, 1)
            nc.gpsimd.tensor_tensor(snr[:, 4:6], snr[:, 2:4], phalf[:], ALU.pow).then_inc(sn_norm, 1)
            pool.wait_ge(d_l1w, 32)
            nc.gpsimd.tensor_tensor(w1n[:], l1w_sb[:, 0], l1w_sb[:, 1], ALU.add)
            nc.gpsimd.tensor_tensor(w1t[:], l1w_sb[:, 2], l1w_sb[:, 3], ALU.add).then_inc(w1_sum, 1)
            pool.wait_ge(w1_sum, 1)
            for t in range(NT):
                pool.wait_ge(s_tr, t + 1)
                if t >= 2:
                    pool.wait_ge(s_av, t - 1)
                for b in (2, 3):
                    if 2 * t + b > 2:
                        pool.wait_ge(s_xp, 2 * t + b - 2)
                    nc.gpsimd.tensor_copy(pT[32 * b:32 * b + 32, t % 2, :, 32 * b:32 * b + 32],
                                          pk[32 * b:32 * b + 32, t % 2]).then_inc(s_xp, 1)
            pool.wait_ge(s_xp, 2 * NT)
            norm(1)

            def lo_half(n, slot):
                pool.wait_ge(hi0, n + 1)
                nc.gpsimd.tensor_tensor(hl[:, slot, 256:512], r[:, slot % 2, 256:512], hh[:, slot, 256:512],
                                        ALU.subtract).then_inc(lo0p, 1)

            def add_expert(e, b):
                pool.wait_ge(yt0, e + 1)
                nc.gpsimd.tensor_tensor(acc[:], acc[:], yt[:, b], ALU.add).then_inc(acc0, 1)
                pool.wait_ge(acc0, e + 1)

            for n in range(4):
                lo_half(n, n)
            pool.wait_ge(r0_acc, 1)
            with pool.Fori(0, 3) as m:
                for k in range(8):
                    lo_half(8 * m + 4 + k, k % 4)
                    if k in (2, 6):
                        add_expert(2 * m + k // 4, k // 4)
            for n in range(28, 32):
                lo_half(n, n % 4)
                if n == 30:
                    add_expert(6, 0)
            add_expert(7, 1)
            norm(2)
            def inverse_rms(t):
                pool.wait_ge(w_ms, t + 1)
                nc.gpsimd.tensor_tensor(ms[:, 8 * t:8 * t + 8], ms[:, 8 * t:8 * t + 8], mhalf[:, 0:8],
                                        ALU.pow).then_inc(w_inv, 1)

            def expand1(t):
                pool.wait_ge(t_pk, t + 1)
                pool.wait_ge(t_pc, t + 1)
                if t >= 2:
                    pool.wait_ge(t_av, t - 1)
                for b in range(3):
                    q = slice(32 * b, 32 * b + 32)
                    if t + b > 0:
                        pool.wait_ge(t_xp, 3 * t + b)
                    nc.gpsimd.tensor_tensor(pT[q, t % 2, :, q], pk[q, t % 2], pc[q, t % 2], ALU.add).then_inc(t_xp, 1)

            for t in range(NT):
                inverse_rms(t)
            pool.wait_ge(w_inv, NT)
            for t in range(NT):
                expand1(t)
            pool.wait_ge(t_xp, 3 * NT)
            norm(3)

            def lo_pair(p, slot):
                pool.wait_ge(hi1, p + 1)
                src = u if slot is None else r
                b = 0 if slot is None else slot % 2
                nc.gpsimd.tensor_tensor(hl[:, b, :], src[:, b, :], hh[:, b, :], ALU.subtract).then_inc(lo1, 1)

            lo_pair(0, None)
            for p in range(1, 4):
                lo_pair(p, p)
            with pool.Fori(0, 4) as m:
                for k in range(6):
                    lo_pair(6 * m + 4 + k, k)
            for p in range(28, NP):
                lo_pair(p, p)

        @block.scalar
        def _(act):
            act.wait_ge(d_row, 16)
            nc.scalar.activation(etemp[:], row("temp"), ACT.Exp).then_inc(temp_exp, 1)
            act.wait_ge(d_col, 16)
            nc.scalar.activation(wrs[:, 0, 0:ER], col("gw"), ACT.Copy, scale=WS)
            nc.scalar.activation(wrs[:, 0, ER:ER + E0], col("wr"), ACT.Copy, scale=WS)
            nc.scalar.activation(b1s[:], col("b1"), ACT.Copy, scale=HS).then_inc(act_setup, 1)
            act.wait_ge(d_cst, 16)
            for e in range(0, ER, 16):
                nc.scalar.activation(sel1[:, e:e + 16, :], over(con("pick1")[:, e:e + 16], DH0), ACT.Copy)
            nc.scalar.activation(sel0[:], over(con("pick0"), P), ACT.Copy).then_inc(act_setup, 1)

            act.wait_ge(ln_T, NT)
            nc.scalar.activation(xnT[:], B[0][:], ACT.Copy).then_inc(xnT_a, 1)
            def hi_expert(e):
                act.wait_ge(d_w0[e], 16)
                nc.scalar.activation(w0h[:, 1024 * e:1024 * (e + 1)], st0[:, e, :], ACT.Copy,
                                     scale=WS).then_inc(w0_hi, 1)

            act.wait_ge(pool_const, 1)
            for k in ACT_UNITS:
                act.wait_ge(qkv_mm, k + 1)
                bank = B[2 + k % 4]
                if k < 4:
                    last = nc.scalar.activation(q0[:, k, :], bank[:], ACT.Copy)
                elif k < 8:
                    last = nc.scalar.activation(k0[0:64, k - 4, :, 0, :],
                                                bank[0:64].rearrange("p (a b) -> p a b", b=32), ACT.Copy)
                else:
                    last = nc.scalar.activation(vA[:, k - 8, :, 0:DH0], bank[:].rearrange("p (a b) -> p a b", b=DH0),
                                                ACT.Copy)
                last.then_inc(qkv_ev_a, 1)
                if k in (4, 6, 7, 8):
                    hi_expert((4, 6, 7, 8).index(k))

            def exp0(t):
                act.wait_ge(s_sub, t + 1)
                nc.scalar.activation(pb[:, t % 2], pb[:, t % 2], ACT.Exp, scale=cexp[:]).then_inc(s_exp, 1)

            def expand0(t):
                act.wait_ge(s_tr, t + 1)
                if t >= 2:
                    act.wait_ge(s_av, t - 1)
                for b in (0, 1):
                    last = nc.scalar.activation(pT[32 * b:32 * b + 32, t % 2, :, 32 * b:32 * b + 32],
                                                pk[32 * b:32 * b + 32, t % 2], ACT.Copy)
                last.then_inc(s_xa, 1)

            def ev_oT(t):
                act.wait_ge(s_oTp, t + 1)
                if t >= 2:
                    act.wait_ge(s_proj, t - 1)
                nc.scalar.activation(oT[:, t % 2], B[6][:].rearrange("p (a b) -> p a b", b=P),
                                     ACT.Copy).then_inc(s_oT, 1)

            act.wait_ge(sn_scales, 1)
            exp0(0)
            exp0(1)
            expand0(0)
            hi_expert(4)
            exp0(2)
            expand0(1)
            hi_expert(5)
            exp0(3)
            expand0(2)
            hi_expert(6)
            ev_oT(0)
            expand0(3)
            ev_oT(1)
            hi_expert(7)
            ev_oT(2)
            ev_oT(3)

            act.wait_ge(ln_T, 2 * NT)
            nc.scalar.activation(xfh[:], B[0][:], ACT.Copy).then_inc(xnT_a, 1)
            act.wait_ge(r0_sub, 1)
            nc.scalar.activation(lg0[:, :, 0:E0], lg0[:, :, 0:E0], ACT.Exp).then_inc(r0_exp, 1)

            def relu(n, c, slot):
                act.wait_ge(up0, n + 1)
                if slot is not None:
                    act.wait_ge(lo0v, n - 1)
                    act.wait_ge(lo0p, n - 1)
                nc.scalar.activation(r[:, c % 2], B[3 + c % 2][:], ACT.Relu, scale=HS / WS,
                                     bias=b1s[:, bass.ds(n, 1)]).then_inc(relu0, 1)

            def ev_gate(e, b, used):
                act.wait_ge(gmm0, e + 1)
                if used:
                    act.wait_ge(yt0, e - 1)
                nc.scalar.activation(G[:, b], B[5 + b][:], ACT.Copy).then_inc(gev0, 1)

            for n in range(2):
                relu(n, n, None)
            act.wait_ge(r0_T, 1)
            nc.scalar.activation(gT[0:16, :], B[2][0:16, :], ACT.Copy)
            nc.scalar.activation(gT32[:], B[2][0:16, :], ACT.Copy).then_inc(r0_gT, 1)
            for n in range(2, 4):
                relu(n, n, n)
            act.wait_ge(r0_b2, 1)
            nc.scalar.activation(acc[:], B[1][:], ACT.Copy).then_inc(r0_acc, 1)
            ev_gate(0, 0, False)
            with act.Fori(0, 3) as m:
                for k in range(8):
                    relu(8 * m + 4 + k, k, k)
                    if k == 3:
                        ev_gate(2 * m + 1, 1, False)
                    if k == 7:
                        ev_gate(2 * m + 2, 0, True)
            for n in range(28, 32):
                relu(n, n, n)
                if n == 31:
                    ev_gate(7, 1, True)

            act.wait_ge(ln_T, 3 * NT)
            nc.scalar.activation(xnT[:], B[0][:], ACT.Copy).then_inc(xnT_a, 1)
            for t in range(NT):
                act.wait_ge(w_mm, t + 1)
                nc.scalar.activation(wsq[:, tile(t)], B[1 + t][:, 0:P], ACT.Square).then_inc(w_sq, 1)

            def ev_qk(t):
                act.wait_ge(qk_T, t + 1)
                nc.scalar.activation(qT1[:, tile(t)], B[5][:, 0:P], ACT.Copy)
                for hd in range(4, H):
                    last = nc.scalar.activation(k1[:, 4 * t:4 * t + 4, hd, :],
                                                B[5][:, P:2 * P].rearrange("p (a b) -> p a b", b=32), ACT.Copy,
                                                scale=con("heads")[:, hd:hd + 1])
                last.then_inc(qk_a, 1)

            def exp1(t):
                act.wait_ge(t_subr, t + 1)
                nc.scalar.activation(pb[:, t % 2], pb[:, t % 2], ACT.Exp, scale=0.25).then_inc(t_expr, 1)
                act.wait_ge(t_subc, t + 1)
                nc.scalar.activation(pc[:, t % 2], pc[:, t % 2], ACT.Exp, scale=0.25).then_inc(t_expc, 1)

            def ev_y(t):
                act.wait_ge(t_av, t + 1)
                if t >= 2:
                    act.wait_ge(t_yTp, t - 1)
                nc.scalar.activation(on[:, t % 2, 0:2, :].rearrange("p a b -> p (a b)"), B[7 * ((t + 1) % 2)][:, 0:P],
                                     ACT.Copy).then_inc(t_y, 1)

            def ev_yT(t):
                act.wait_ge(t_yTp, t + 1)
                if t >= 2:
                    act.wait_ge(t_proj, t - 1)
                nc.scalar.activation(oT[:, t % 2, 0], B[6][:, 0:P], ACT.Copy).then_inc(t_yT, 1)

            for t in range(NT):
                ev_qk(t)
            exp1(0)
            exp1(1)
            exp1(2)
            ev_y(0)
            exp1(3)
            ev_yT(0)
            for t in range(1, NT):
                ev_y(t)
                ev_yT(t)

            def hi_weights(p, slot):
                nc.scalar.activation(w1h[:, slot], st1[:, bass.ds(PW * p, PW)], ACT.Copy, scale=WS).then_inc(w1_hi, 1)

            for c in range(NP // 3):
                act.wait_ge(d_w1[c], 16)
            for p in range(4):
                hi_weights(p, p)
            act.wait_ge(ln_T, 4 * NT)
            nc.scalar.activation(xfh[:], B[0][:], ACT.Copy).then_inc(xnT_a, 1)
            act.wait_ge(r1_sub, 1)
            nc.scalar.activation(lg0[:], lg0[:], ACT.Exp, scale=1.0 / WS).then_inc(r1_exp, 1)

            def silu(p, b, used):
                act.wait_ge(h1mm, p + 1)
                if used:
                    act.wait_ge(u1, p - 1)
                nc.scalar.activation(s[:, b], B[3 + b][:], ACT.Silu, scale=1.0 / WS).then_inc(silu1, 1)

            def hi_hidden(p, b, used):
                act.wait_ge(r1, p + 1)
                if used:
                    act.wait_ge(down1, p - 1)
                nc.scalar.activation(hh[:, b], r[:, b], ACT.Copy).then_inc(hi1, 1)

            def next_weights(p, slot):
                if not (isinstance(p, int) and p < RING):
                    act.wait_ge(down1, p - RING + 1)
                hi_weights(p, slot)

            silu(0, 0, False)
            act.wait_ge(u1, 1)
            nc.scalar.activation(hh[:, 0], u[:, 0], ACT.Copy).then_inc(hi1, 1)
            next_weights(4, 4)
            act.wait_ge(r1_T, 1)
            nc.scalar.activation(gT[:], B[2][:], ACT.Copy).then_inc(r1_gT, 1)
            for p in range(1, 4):
                silu(p, p % 2, p >= 2)
                hi_hidden(p, p % 2, p >= 2)
                next_weights(p + 4, (p + 4) % RING)
            with act.Fori(0, 4) as m:
                for k in range(RING):
                    silu(RING * m + 4 + k, k % 2, True)
                    hi_hidden(RING * m + 4 + k, k % 2, True)
                    next_weights(RING * m + 8 + k, (k + 8) % RING)
            for p in range(28, NP):
                silu(p, p % 2, True)
                hi_hidden(p, p % 2, True)
                if p + 4 < NP:
                    next_weights(p + 4, (p + 4) % RING)
            act.wait_ge(down1, NP)
            nc.scalar.activation(acc[:], B[0][:], ACT.Copy, scale=1.0 / (WS * HS)).then_inc(y1_ev, 1)

        @block.vector
        def _(dve):
            count = [0]

            def link(ins):
                count[0] += 1
                ins.then_inc(dve_step, 1)
                dve.wait_ge(dve_step, count[0])

            dve.wait_ge(act_setup, 1)
            nc.vector.scalar_tensor_tensor(wrs[:, 1, 0:ER], col("gw"), WS, wrs[:, 0, 0:ER], ALU.mult, ALU.subtract)
            nc.vector.scalar_tensor_tensor(wrs[:, 1, ER:ER + E0], col("wr"), WS, wrs[:, 0, ER:ER + E0],
                                           ALU.mult, ALU.subtract).then_inc(mask_ready, 1)
            dve.wait_ge(d_cst, 16)
            nc.vector.tensor_scalar(negI[:], ident, -BIG, None, ALU.mult)
            nc.vector.tensor_copy(m0b[:], along(con("mask0"), H))
            nc.vector.tensor_copy(m1b[:], along(con("mask1"), H)).then_inc(mask_ready, 1)

            def norm_stats(k, t):
                link(nc.vector.bn_stats(stats[:, t], h[:, t]))
                link(nc.vector.bn_aggr(mv[:, t], stats[:, t]))
                nc.vector.tensor_scalar_add(vpe[:, t:t + 1], mv[:, t, 1:2], EPS_LN).then_inc(ln_var, 1)

            def norm_apply(k):
                for t in range(NT):
                    dve.wait_ge(ln_rstd, NT * k + t + 1)
                    nc.vector.tensor_scalar(xn[:, t], h[:, t], mv[:, t, 0:1], rstd[:, t:t + 1],
                                            ALU.subtract, ALU.mult).then_inc(ln_xn, 1)

            dve.wait_ge(d_row, 16)
            for t in range(NT):
                dve.wait_ge(tok_done, t + 1)
                link(nc.vector.tensor_tensor(h[:, t], B[t][:, 0:P], row("tok_b"), ALU.add))
                norm_stats(0, t)
            norm_apply(0)

            dve.wait_ge(sn_gram, 1)
            nc.vector.tensor_copy(gram[:], B[6][:, 0:P])
            nc.vector.tensor_copy(sna[:, 0:1], B[6][:, P:P + 1]).then_inc(sn_acopy, 1)
            dve.wait_ge(sn_b, 1)
            link(nc.vector.tensor_copy(snb[:], B[7][:, 0:5]))
            nc.vector.tensor_tensor(sn4[:, 0:1], snb[:, 0:1], col("u_qkv"), ALU.mult)
            nc.vector.tensor_tensor(sn4[:, 1:2], sna[:, 0:1], sna[:, 0:1], ALU.mult)
            link(nc.vector.tensor_tensor(snb2[:], snb[:], snb[:], ALU.mult))
            nc.vector.tensor_copy(sn4[:, 2:3], snb2[:, 0:1])
            nc.vector.tensor_reduce(sn4[:, 3:4], snb2[:, 1:5], AX, ALU.add).then_inc(sn_sums, 1)

            def lo_expert(e):
                dve.wait_ge(w0_hi, e + 1)
                nc.vector.scalar_tensor_tensor(w0l[:, 1024 * e:1024 * (e + 1)], st0[:, e, :], WS,
                                               w0h[:, 1024 * e:1024 * (e + 1)], ALU.mult, ALU.subtract).then_inc(w0_lo, 1)

            dve.wait_ge(pool_const, 1)
            for k in DVE_UNITS:
                dve.wait_ge(qkv_mm, k + 1)
                bank = B[2 + k % 4]
                if k < 4:
                    last = nc.vector.tensor_copy(q0[:, k, :], bank[:])
                elif k < 8:
                    last = nc.vector.tensor_copy(k0[64:P, k - 4, :, 1, :],
                                                 bank[64:P].rearrange("p (a b) -> p a b", b=32))
                else:
                    last = nc.vector.tensor_copy(vA[:, k - 8, :, 0:DH0], bank[:].rearrange("p (a b) -> p a b", b=DH0))
                last.then_inc(qkv_ev_v, 1)
                if k == 3:
                    dve.wait_ge(sn_tot, 1)
                    link(nc.vector.reciprocal(snr[:, 0:2], B[7][:, 10:12]))
                    nc.vector.tensor_tensor(snr[:, 2:4], B[7][:, 8:10], snr[:, 0:2], ALU.mult).then_inc(sn_ratio, 1)
                if k in (4, 6, 7, 9):
                    lo_expert((4, 6, 7, 9).index(k))

            dve.wait_ge(sn_norm, 1)
            link(nc.vector.tensor_tensor(snr[:, 6:8], snr[:, 4:6], row("sigma"), ALU.mult))
            link(nc.vector.tensor_tensor(snr[:, 0:1], snr[:, 6:7], snr[:, 6:7], ALU.mult))
            nc.vector.tensor_tensor(cout[:], snr[:, 6:7], snr[:, 7:8], ALU.mult)
            dve.wait_ge(temp_exp, 1)
            nc.vector.tensor_tensor(cexp[:], snr[:, 0:1], etemp[:], ALU.mult).then_inc(sn_scales, 1)

            def by_head(ap):
                return ap.rearrange("p (a b) -> p a b", b=32)

            def center(dst, m, src, done):
                link(nc.vector.tensor_reduce(m, src, AX, ALU.max))
                nc.vector.tensor_tensor(dst, src, over(m, 32), ALU.subtract).then_inc(done, 1)

            def center0(t):
                dve.wait_ge(s_mm, t + 1)
                center(pb[:, t % 2], mx[:, t % 2], by_head(B[t][:, 0:256]), s_sub)

            def by_key0(t):
                dve.wait_ge(s_exp, t + 1)
                if t >= 2:
                    dve.wait_ge(s_xa, t - 1)
                    dve.wait_ge(s_xp, 2 * t - 2)
                nc.vector.transpose(pk[:, t % 2], pb[:, t % 2]).then_inc(s_tr, 1)

            def norm0(t):
                dve.wait_ge(s_av, t + 1)
                for g in (0, 1):
                    o = B[4 * (1 - t % 2) + g][:, 0:4 * (DH0 + 1)].rearrange("p (a b) -> p a b", b=DH0 + 1)
                    link(nc.vector.reciprocal(rs[:, t % 2, 4 * g:4 * g + 4], o[:, :, DH0]))
                    if g == 0 and t >= 2:
                        dve.wait_ge(s_oTp, t - 1)
                    last = nc.vector.tensor_tensor(on[:, t % 2, 4 * g:4 * g + 4], o[:, :, 0:DH0],
                                                   over(rs[:, t % 2, 4 * g:4 * g + 4], DH0), ALU.mult)
                last.then_inc(s_on, 1)

            def residual0(t):
                dve.wait_ge(s_proj, t + 1)
                dve.wait_ge(hb_done, NT)
                nc.vector.scalar_tensor_tensor(h[:, t], B[7][:, tile(t)], cout[:], hb[:, t], ALU.mult,
                                               ALU.add).then_inc(s_hup, 1)
                dve.wait_ge(s_hup, t + 1)
                norm_stats(1, t)

            center0(0)
            center0(1)
            by_key0(0)
            lo_expert(4)
            center0(2)
            by_key0(1)
            lo_expert(5)
            center0(3)
            by_key0(2)
            norm0(0)
            by_key0(3)
            lo_expert(6)
            norm0(1)
            residual0(0)
            norm0(2)
            residual0(1)
            lo_expert(7)
            norm0(3)
            residual0(2)
            residual0(3)
            norm_apply(1)

            dve.wait_ge(xnT_a, 2)
            nc.vector.tensor_tensor(xfl[:], B[0][:], xfh[:], ALU.subtract).then_inc(xfl_v, 1)
            dve.wait_ge(r0_mm, 1)
            lg = lg0[:, :, 0:E0]
            link(nc.vector.scalar_tensor_tensor(lg, B[1][:, 0:NT * E0].rearrange("p (a b) -> p a b", b=E0), 1.0 / WS,
                                                along(row("br"), NT), ALU.mult, ALU.add))
            link(nc.vector.tensor_reduce(lgm[:], lg, AX, ALU.max))
            nc.vector.tensor_tensor(lg, lg, over(lgm[:], E0), ALU.subtract).then_inc(r0_sub, 1)
            dve.wait_ge(r0_exp, 1)
            for t in range(NT):
                last = nc.vector.max(top8[:, t], lg0[:, t, 0:E0])
            link(last)
            link(nc.vector.memset(top8[:, :, 2:8], -3.0))
            for t in range(NT):
                last = nc.vector.match_replace(rep[:, t, 0:E0], top8[:, t], lg0[:, t, 0:E0], -1.0)
            link(last)
            gt = gates[:, :, 0:E0]
            link(nc.vector.scalar_tensor_tensor(gt, rep[:, :, 0:E0], 0.0, lg, ALU.is_lt, ALU.mult))
            link(nc.vector.tensor_reduce(lgs[:], gt, AX, ALU.add))
            link(nc.vector.reciprocal(lgs[:], lgs[:]))
            link(nc.vector.tensor_tensor(gt, gt, over(lgs[:], E0), ALU.mult))
            link(nc.vector.tensor_copy(g16[:, :, 0:E0], gt))
            nc.vector.tensor_copy(gcb[:, :, 0:E0], g16[:, :, 0:E0])
            link(nc.vector.tensor_tensor(gcb[:, :, E0:2 * E0], gt, g16[:, :, 0:E0], ALU.subtract))
            nc.vector.tensor_scalar(gcb[:, :, E0:2 * E0], gcb[:, :, E0:2 * E0], LS, None, ALU.mult).then_inc(r0_gcb, 1)
            dve.wait_ge(d_l1w, 32)
            nc.vector.tensor_scalar(b2_sb[:], b2_sb[:], con("b2scale")[0:16], None, ALU.mult).then_inc(r0_gcb, 1)

            def hi_lo(n, slot, used):
                dve.wait_ge(relu0, n + 1)
                if used:
                    dve.wait_ge(down0, n - 3)
                nc.vector.tensor_copy(hh[:, slot], r[:, slot % 2]).then_inc(hi0, 1)
                dve.wait_ge(hi0, n + 1)
                nc.vector.tensor_tensor(hl[:, slot, 0:256], r[:, slot % 2, 0:256], hh[:, slot, 0:256],
                                        ALU.subtract).then_inc(lo0v, 1)

            def gate0(e, b, used):
                dve.wait_ge(down0, 4 * e + 4)
                dve.wait_ge(gev0, e + 1)
                if used:
                    dve.wait_ge(acc0, e - 1)
                nc.vector.scalar_tensor_tensor(yt[:, b], B[7 * (1 - b)][:], 1.0 / (WS * HS), G[:, b], ALU.mult,
                                               ALU.mult).then_inc(yt0, 1)

            for n in range(4):
                hi_lo(n, n, False)
            with dve.Fori(0, 3) as m:
                for k in range(8):
                    hi_lo(8 * m + 4 + k, k % 4, True)
                    if k == 2:
                        gate0(2 * m, 0, False)
                    if k == 6:
                        gate0(2 * m + 1, 1, False)
            for n in range(28, 32):
                hi_lo(n, n % 4, True)
                if n == 30:
                    gate0(6, 0, True)
            gate0(7, 1, True)
            for t in range(NT):
                dve.wait_ge(f0_T, t + 1)
                nc.vector.tensor_tensor(h[:, t], h[:, t], B[1 + t][:, 0:P], ALU.add).then_inc(f0_h, 1)
                dve.wait_ge(f0_h, t + 1)
                norm_stats(2, t)
            norm_apply(2)

            def heads(ap):
                return ap.rearrange("p (a b) -> p a b", b=DH1)

            for t in range(NT):
                dve.wait_ge(w_sq, t + 1)
                nc.vector.tensor_copy(wtm[:, tile(t)], B[1 + t][:, 0:P])
                link(nc.vector.tensor_reduce(ms[:, 8 * t:8 * t + 8], heads(wsq[:, tile(t)]), AX, ALU.add))
                nc.vector.tensor_scalar(ms[:, 8 * t:8 * t + 8], ms[:, 8 * t:8 * t + 8], 1.0 / DH1, EPS_RMS, ALU.mult,
                                        ALU.add).then_inc(w_ms, 1)

            def qkv1(t):
                w = heads(wtm[:, tile(t)])
                dve.wait_ge(w_inv, t + 1)
                link(nc.vector.tensor_tensor(w, w, over(ms[:, 8 * t:8 * t + 8], DH1), ALU.mult))
                nc.vector.tensor_tensor(heads(qn[:, tile(t)]), w, along(row("g1"), H), ALU.mult)
                nc.vector.tensor_tensor(heads(kn[:, tile(t)]), w, along(row("g2"), H), ALU.mult)
                nc.vector.tensor_tensor(heads(v1[:, tile(t)]), w, along(row("g3"), H), ALU.mult).then_inc(qkv_n, 1)

            def masked_keys(t):
                dve.wait_ge(qk_T, t + 1)
                for hd in range(4):
                    last = nc.vector.tensor_scalar(k1[:, 4 * t:4 * t + 4, hd, :], by_head(B[6][:, 0:P]),
                                                   con("heads")[:, hd:hd + 1], None, ALU.mult)
                last.then_inc(k1_v, 1)

            def center1(t):
                src = by_head(B[1 + t][:, 0:256])
                dve.wait_ge(t_mm, t + 1)
                if t == 0:
                    dve.wait_ge(qk_T, NT)
                center(pb[:, t % 2], mx[:, t % 2], src, t_subr)
                if t >= 2:
                    dve.wait_ge(t_xp, 3 * t - 3)
                link(nc.vector.transpose(pc[:, t % 2], src))
                center(pc[:, t % 2], mxc[:, t % 2], pc[:, t % 2], t_subc)

            def softmax1(t):
                b = t % 2
                dve.wait_ge(t_expr, t + 1)
                link(nc.vector.tensor_reduce(rs[:, b], pb[:, b], AX, ALU.add))
                link(nc.vector.reciprocal(rs[:, b], rs[:, b]))
                link(nc.vector.tensor_tensor(pb[:, b], pb[:, b], over(rs[:, b], 32), ALU.mult))
                if t >= 2:
                    dve.wait_ge(t_xp, 3 * t - 3)
                nc.vector.transpose(pk[:, b], pb[:, b]).then_inc(t_pk, 1)
                dve.wait_ge(t_expc, t + 1)
                link(nc.vector.tensor_reduce(cs[:, b], pc[:, b], AX, ALU.add))
                link(nc.vector.reciprocal(cs[:, b], cs[:, b]))
                nc.vector.tensor_tensor(pc[:, b], pc[:, b], over(cs[:, b], 32), ALU.mult).then_inc(t_pc, 1)
                dve.wait_ge(t_pc, t + 1)
                if t >= 2:
                    dve.wait_ge(t_av, t - 1)
                nc.vector.tensor_tensor(pT[96:P, b, :, 96:P], pk[96:P, b], pc[96:P, b], ALU.add).then_inc(t_xv, 1)

            def residual1(t):
                dve.wait_ge(t_proj, t + 1)
                nc.vector.tensor_tensor(h[:, t], h[:, t], B[5][:, 0:P], ALU.add).then_inc(t_hup, 1)
                dve.wait_ge(t_hup, t + 1)
                norm_stats(3, t)

            qkv1(0)
            qkv1(1)
            masked_keys(0)
            qkv1(2)
            masked_keys(1)
            qkv1(3)
            masked_keys(2)
            masked_keys(3)
            center1(0)
            center1(1)
            softmax1(0)
            center1(2)
            softmax1(1)
            center1(3)
            softmax1(2)
            residual1(0)
            softmax1(3)
            residual1(1)
            residual1(2)
            residual1(3)
            norm_apply(3)

            def lo_weights(p, slot):
                dve.wait_ge(w1_hi, p + 1)
                nc.vector.scalar_tensor_tensor(w1l[:, slot], st1[:, bass.ds(PW * p, PW)], WS, w1h[:, slot], ALU.mult,
                                               ALU.subtract).then_inc(w1_lo, 1)

            for p in range(4):
                lo_weights(p, p)
            dve.wait_ge(xnT_a, 4)
            nc.vector.tensor_tensor(xfl[:], B[0][:], xfh[:], ALU.subtract).then_inc(xfl_v, 1)
            dve.wait_ge(r1_mm, 1)
            bank = B[1][:, 0:NT * ER].rearrange("p (a b) -> p a b", b=ER)
            link(nc.vector.tensor_reduce(lgm[:], bank, AX, ALU.max))
            nc.vector.tensor_tensor(lg0[:], bank, over(lgm[:], ER), ALU.subtract).then_inc(r1_sub, 1)

            def hidden(p, b, used, gated=True):
                dve.wait_ge(silu1, p + 1)
                dve.wait_ge(h3mm, p + 1)
                if used:
                    dve.wait_ge(r1, p - 1)
                if isinstance(p, int) and p == 2:
                    dve.wait_ge(lo1, 1)
                nc.vector.scalar_tensor_tensor(u[:, b], B[5 + b][:], HS / WS, s[:, b], ALU.mult, ALU.mult).then_inc(u1, 1)
                if gated:
                    dve.wait_ge(u1, p + 1)
                    dve.wait_ge(g1mm, p)
                    if used:
                        dve.wait_ge(lo1, p - 1)
                    nc.vector.tensor_tensor(r[:, b], u[:, b], B[[7, 2][b] if b else 7][:], ALU.mult).then_inc(r1, 1)

            dve.wait_ge(r1_exp, 1)
            hidden(0, 0, False, gated=False)
            link(nc.vector.tensor_reduce(lgs[:], lg0[:], AX, ALU.add))
            link(nc.vector.reciprocal(lgs[:], lgs[:]))
            link(nc.vector.tensor_tensor(lg0[:], lg0[:], over(lgs[:], ER), ALU.mult))
            link(nc.vector.tensor_tensor(bia[:], lg0[:], along(row("gate_bias"), NT), ALU.add))
            for t in range(NT):
                last = nc.vector.max(top8[:, t], bia[:, t])
            link(last)
            link(nc.vector.memset(top8[:, :, TOPK1:8], -2.0e38))
            for t in range(NT):
                last = nc.vector.match_replace(rep[:, t], top8[:, t], bia[:, t], -3.0e38)
            link(last)
            link(nc.vector.scalar_tensor_tensor(gates[:], rep[:], -2.5e38, lg0[:], ALU.is_lt, ALU.mult))
            link(nc.vector.tensor_copy(g16[:], gates[:]))
            nc.vector.tensor_copy(gcb[:, :, 0:ER], g16[:])
            link(nc.vector.tensor_tensor(gcb[:, :, ER:2 * ER], gates[:], g16[:], ALU.subtract))
            nc.vector.tensor_scalar(gcb[:, :, ER:2 * ER], gcb[:, :, ER:2 * ER], LS, None, ALU.mult).then_inc(r1_gcb, 1)
            dve.wait_ge(r1_gcb, 1)
            nc.vector.tensor_copy(lgm[:], lgs[:]).then_inc(r1, 1)
            lo_weights(4, 4)
            for p in range(1, 4):
                hidden(p, p % 2, p >= 2)
                lo_weights(p + 4, (p + 4) % RING)
            with dve.Fori(0, 4) as m:
                for k in range(RING):
                    hidden(RING * m + 4 + k, k % 2, True)
                    lo_weights(RING * m + 8 + k, (k + 8) % RING)
            for p in range(28, NP):
                hidden(p, p % 2, True)
                if p + 4 < NP:
                    lo_weights(p + 4, (p + 4) % RING)
            for t in range(NT):
                dve.wait_ge(y1_T, t + 1)
                nc.vector.tensor_tensor(outs[:, t], h[:, t], B[1 + t][:, 0:P], ALU.add).then_inc(out_v, 1)

        @block.tensor
        def _(pe):
            def mm(o, l, rr, start=True, stop=True):
                return nc.tensor.matmul(o, l, rr, start=start, stop=stop)

            pe.wait_ge(d_tokw, 16)
            for t in range(NT):
                pe.wait_ge(d_x[t], 16)
                for c in range(KC):
                    last = mm(B[t][:, 0:P], x_sb[:, t, c, :], tokw[:, c, :], c == 0, c == KC - 1)
                last.then_inc(tok_done, 1)

            def transpose_norm(k):
                for t in range(NT):
                    pe.wait_ge(ln_xn, NT * k + t + 1)
                    nc.tensor.transpose(B[0][:, tile(t)], xn[:, t], ident).then_inc(ln_T, 1)

            pe.wait_ge(d_cst, 16)
            pe.wait_ge(d_wqN, 16)
            for c in range(12):
                mm(B[6][:, 0:P], wqkvN_sb[:, c, :], wqkvN_sb[:, c, :], c == 0, c == 11)
            pe.wait_ge(d_wo, 32)
            pe.wait_ge(d_col, 16)
            for c in range(C0):
                last = mm(B[6][:, P:P + 1], woT_sb[:, c, :], col("u_out")[:, c:c + 1], c == 0, c == C0 - 1)
            last.then_inc(sn_gram, 1)
            transpose_norm(0)
            pe.wait_ge(d_wqT, 16)
            pe.wait_ge(xnT_a, 1)
            for k in range(12):
                if k >= 4:
                    if k - 4 in ACT_UNITS:
                        pe.wait_ge(qkv_ev_a, ACT_UNITS.index(k - 4) + 1)
                    if k - 4 in DVE_UNITS:
                        pe.wait_ge(qkv_ev_v, DVE_UNITS.index(k - 4) + 1)
                if k < 8:
                    last = mm(B[2 + k % 4][:], wqkvT_sb[:, P * k:P * k + P], xnT[:])
                else:
                    last = mm(B[2 + k % 4][:], xnT[:, tile(k - 8)], wqkvT_sb[:, 2 * INNER:3 * INNER])
                last.then_inc(qkv_mm, 1)
                if k == 0:
                    pe.wait_ge(sn_acopy, 1)
                    mm(B[7][:, 0:1], gram[:], col("u_qkv"))
                    for c in range(C0):
                        last = mm(B[7][:, 1 + c:2 + c], woN_sb[:, P * c:P * c + P], sna[:, 0:1])
                    last.then_inc(sn_b, 1)
                if k == 2:
                    pe.wait_ge(pool_const, 1)
                    pe.wait_ge(sn_sums, 1)
                    mm(B[7][:, 8:12], ones[:], sn4[:]).then_inc(sn_tot, 1)

            def scores0(t):
                bank = B[t]
                mm(bank[:, 0:256], negI[:], m0b[:].rearrange("p a b -> p (a b)"), True, False)
                for b in range(4):
                    for j in range(4):
                        last = mm(bank[32 * b:32 * b + 32, 64 * j:64 * j + 64],
                                  q0[:, j, P * t + 32 * b:P * t + 32 * b + 32],
                                  k0[:, j, 4 * t + b].rearrange("p a b -> p (a b)"), False, j == 3)
                last.then_inc(s_mm, 1)

            def values0(t):
                pe.wait_ge(s_xa, t + 1)
                pe.wait_ge(s_xp, 2 * t + 2)
                if t >= 2:
                    pe.wait_ge(s_on, t - 1)
                for hd in range(H):
                    j = hd % 4
                    last = mm(B[4 * (1 - t % 2) + hd // 4][:, 65 * j:65 * j + 65], pT[:, t % 2, hd, :], vA[:, t, hd, :])
                last.then_inc(s_av, 1)

            def transpose_o(t):
                pe.wait_ge(s_on, t + 1)
                if t >= 1:
                    pe.wait_ge(s_oT, t)
                flat = on[:, t % 2].rearrange("p a b -> p (a b)")
                for c in range(4):
                    last = nc.tensor.transpose(B[6][:, tile(c)], flat[:, tile(c)], ident)
                last.then_inc(s_oTp, 1)

            def project0(t):
                pe.wait_ge(s_oT, t + 1)
                if t >= 1:
                    pe.wait_ge(s_hup, t)
                for c in range(4):
                    last = mm(B[7][:, tile(t)], oT[:, t % 2, c, :], woT_sb[:, c, :], c == 0, c == 3)
                last.then_inc(s_proj, 1)

            pe.wait_ge(mask_ready, 2)
            pe.wait_ge(qkv_ev_a, len(ACT_UNITS))
            pe.wait_ge(qkv_ev_v, len(DVE_UNITS))
            for t in range(NT):
                scores0(t)
            values0(0)
            values0(1)
            transpose_o(0)
            values0(2)
            project0(0)
            transpose_o(1)
            values0(3)
            project0(1)
            transpose_o(2)
            project0(2)
            transpose_o(3)
            project0(3)

            transpose_norm(1)
            pe.wait_ge(xfl_v, 1)

            def router(n, c0, done):
                for t in range(NT):
                    o = B[1][:, n * t:n * t + n]
                    mm(o, xfh[:, tile(t)], wrs[:, 0, c0:c0 + n], True, False)
                    mm(o, xfl[:, tile(t)], wrs[:, 0, c0:c0 + n], False, False)
                    last = mm(o, xfh[:, tile(t)], wrs[:, 1, c0:c0 + n], False, True)
                last.then_inc(done, 1)

            router(E0, ER, r0_mm)

            def up(n, e, c, used):
                if used:
                    pe.wait_ge(relu0, n - 1)
                o = B[3 + c % 2][:]
                hi = w0h[:, bass.ds(1024 * e + P * c, P)]
                lo = w0l[:, bass.ds(1024 * e + P * c, P)]
                mm(o, hi, xfh[:], True, False)
                mm(o, hi, xfl[:], False, False)
                mm(o, lo, xfh[:], False, True).then_inc(up0, 1)

            def down(n, e, c, b, used):
                pe.wait_ge(lo0v, n + 1)
                pe.wait_ge(lo0p, n + 1)
                if c == 0 and used:
                    pe.wait_ge(yt0, e - 1)
                o = B[7 * (1 - b)][:]
                hi = w0h[:, bass.ds(1024 * e + F0 + P * c, P)]
                lo = w0l[:, bass.ds(1024 * e + F0 + P * c, P)]
                mm(o, hi, hh[:, c, :], c == 0, False)
                mm(o, hi, hl[:, c, :], False, False)
                last = mm(o, lo, hh[:, c, :], False, c == 3)
                last.then_inc(down0, 1)

            def gate_mm(e, b, used):
                if used:
                    pe.wait_ge(gev0, e - 1)
                mm(B[5 + b][:], sel0[:].rearrange("p a b -> p (a b)")[:, bass.ds(P * e, P)], gT[:]).then_inc(gmm0, 1)

            pe.wait_ge(w0_hi, E0)
            pe.wait_ge(w0_lo, E0)
            up(0, 0, 0, False)
            up(1, 0, 1, False)
            up(2, 0, 2, True)
            pe.wait_ge(r0_gcb, 2)
            for t in range(NT):
                last = nc.tensor.transpose(B[2][0:16, tile(t)], gcb[:, t, 0:16], ident)
            last.then_inc(r0_T, 1)
            up(3, 0, 3, True)
            pe.wait_ge(act_setup, 2)
            pe.wait_ge(r0_gT, 1)
            mm(B[1][:], b2_sb[:], gT32[:]).then_inc(r0_b2, 1)
            gate_mm(0, 0, False)
            down(0, 0, 0, 0, False)
            with pe.Fori(0, 3) as m:
                for k in range(8):
                    up(8 * m + 4 + k, 2 * m + 1 + k // 4, k % 4, True)
                    if k == 3:
                        gate_mm(2 * m + 1, 1, False)
                    if k == 7:
                        gate_mm(2 * m + 2, 0, True)
                    down(8 * m + 1 + k, 2 * m + (1 + k) // 4, (1 + k) % 4, ((1 + k) // 4) % 2, False)
            for n in range(28, 35):
                if n < 32:
                    up(n, 7, n % 4, True)
                if n == 31:
                    gate_mm(7, 1, True)
                down(n - 3, (n - 3) // 4, (n - 3) % 4, ((n - 3) // 4) % 2, True)
            pe.wait_ge(acc0, E0)
            for t in range(NT):
                nc.tensor.transpose(B[1 + t][:, 0:P], acc[:, tile(t)], ident).then_inc(f0_T, 1)

            transpose_norm(2)
            pe.wait_ge(w1_sum, 1)
            pe.wait_ge(xnT_a, 3)
            for t in range(NT):
                mm(B[1 + t][:, 0:P], xnT[:, tile(t)], w1t[:]).then_inc(w_mm, 1)

            def transpose_qk(t):
                pe.wait_ge(qkv_n, t + 1)
                if t >= 1:
                    pe.wait_ge(qk_a, t)
                    pe.wait_ge(k1_v, t)
                nc.tensor.transpose(B[5][:, 0:P], qn[:, tile(t)], ident)
                nc.tensor.transpose(B[5][:, P:2 * P], kn[:, tile(t)], ident)
                nc.tensor.transpose(B[6][:, 0:P], kn[:, tile(t)], ident).then_inc(qk_T, 1)

            def scores1(t):
                pe.wait_ge(qk_a, t + 1)
                pe.wait_ge(k1_v, t + 1)
                mm(B[1 + t][:, 0:256], negI[:], m1b[:].rearrange("p a b -> p (a b)"), True, False)
                for b in range(4):
                    last = mm(B[1 + t][32 * b:32 * b + 32, 0:256], qT1[:, P * t + 32 * b:P * t + 32 * b + 32],
                              k1[:, 4 * t + b].rearrange("p a b -> p (a b)"), False, True)
                last.then_inc(t_mm, 1)

            def values1(t):
                pe.wait_ge(t_xv, t + 1)
                pe.wait_ge(t_xp, 3 * t + 3)
                if t >= 2:
                    pe.wait_ge(t_y, t - 1)
                for hd in range(H):
                    last = mm(B[7 * ((t + 1) % 2)][:, DH1 * hd:DH1 * hd + DH1], pT[:, t % 2, hd, :],
                              v1[:, P * t + DH1 * hd:P * t + DH1 * hd + DH1])
                last.then_inc(t_av, 1)

            def transpose_y(t):
                pe.wait_ge(t_y, t + 1)
                if t >= 1:
                    pe.wait_ge(t_yT, t)
                nc.tensor.transpose(B[6][:, 0:P], on[:, t % 2, 0:2, :].rearrange("p a b -> p (a b)"),
                                    ident).then_inc(t_yTp, 1)

            def project1(t):
                pe.wait_ge(t_yT, t + 1)
                if t >= 1:
                    pe.wait_ge(t_hup, t)
                mm(B[5][:, 0:P], oT[:, t % 2, 0, :], w1n[:]).then_inc(t_proj, 1)

            transpose_qk(0)
            transpose_qk(1)
            scores1(0)
            transpose_qk(2)
            scores1(1)
            transpose_qk(3)
            scores1(2)
            scores1(3)
            for t in range(NT):
                values1(t)
                transpose_y(t)
                project1(t)

            transpose_norm(3)
            pe.wait_ge(xfl_v, 2)
            router(ER, 0, r1_mm)

            def pair_up(p, slot, used):
                pe.wait_ge(w1_lo, p + 1)
                for b0, c0, bank_free, done in ((3, 0, silu1, h1mm), (5, P, u1, h3mm)):
                    if used:
                        pe.wait_ge(bank_free, p - 1)
                    o = B[b0 + slot % 2][:]
                    mm(o, w1h[:, slot, c0:c0 + P], xfh[:], True, False)
                    mm(o, w1h[:, slot, c0:c0 + P], xfl[:], False, False)
                    mm(o, w1l[:, slot, c0:c0 + P], xfh[:], False, True).then_inc(done, 1)

            def pair_gate(p, slot, used):
                if used:
                    pe.wait_ge(r1, p - 1)
                flat = sel1[:].rearrange("p a b -> p (a b)")
                mm(B[2 if slot % 2 else 7][:], flat[:, bass.ds(P * p - P, P)], gT[:]).then_inc(g1mm, 1)

            def pair_down(p, slot, first=False, last=False):
                pe.wait_ge(lo1, p + 1)
                b = slot % 2
                mm(B[0][:], w1h[:, slot, 2 * P:3 * P], hh[:, b, :], first, False)
                mm(B[0][:], w1h[:, slot, 2 * P:3 * P], hl[:, b, :], False, False)
                mm(B[0][:], w1l[:, slot, 2 * P:3 * P], hh[:, b, :], False, last).then_inc(down1, 1)

            pair_up(0, 0, False)
            pair_up(1, 1, False)
            pe.wait_ge(r1_gcb, 1)
            for t in range(NT):
                last = nc.tensor.transpose(B[2][:, tile(t)], gcb[:, t, :], ident)
            last.then_inc(r1_T, 1)
            pe.wait_ge(r1_gT, 1)
            pair_gate(1, 1, False)
            for p in range(2, 4):
                pair_up(p, p, True)
                pair_gate(p, p, p >= 3)
                pair_down(p - 2, p - 2, first=(p == 2))
            with pe.Fori(0, 4) as m:
                for k in range(RING):
                    pair_up(RING * m + 4 + k, (k + 4) % RING, True)
                    pair_gate(RING * m + 4 + k, k, True)
                    pair_down(RING * m + 2 + k, (k + 2) % RING)
            for p in range(28, NP):
                pair_up(p, p % RING, True)
                pair_gate(p, p, True)
                pair_down(p - 2, (p - 2) % RING)
            pair_down(31, 31 % RING)
            pair_down(32, 32 % RING, last=True)
            pe.wait_ge(y1_ev, 1)
            for t in range(NT):
                nc.tensor.transpose(B[1 + t][:, 0:P], acc[:, tile(t)], ident).then_inc(y1_T, 1)


def kernel(**inputs):
    import concourse.bacc as bacc
    import numpy as np
    from concourse.bass_utils import run_bass_kernel_spmd as run

    v = {k: np.asarray(a) for k, a in inputs.items()}
    f = np.float32
    x = v["x"].reshape(32, 3, 4, 16, 4, 16).transpose(0, 2, 4, 1, 3, 5).reshape(NT, P, KC, P).transpose(0, 3, 2, 1)
    tokWT = v["L0_tok_W"].reshape(P, KC, P).transpose(2, 1, 0)
    rows = np.concatenate([v[n].reshape(1, -1) for n in (
        "L0_tok_b", "L0_attn_b_out", "L0_ffn_br", "L1_attn_g1", "L1_attn_g2", "L1_attn_g3", "L1_ffn_gate_bias",
        "L0_attn_sigma_qkv", "L0_attn_sigma_out", "L0_attn_temperature")], axis=1)
    cols = np.concatenate([v["L0_attn_u_qkv"].reshape(P, 1), v["L0_attn_u_out"].reshape(C0, P).T,
                           v["L0_ffn_b1"].reshape(E0 * C0, P).T, v["L0_ffn_Wr"], v["L1_ffn_g_w"].T], axis=1)
    w = v["L0_attn_w_qkv"]
    wo = v["L0_attn_w_out"]
    w1 = v["L0_ffn_W1"]
    w2 = v["L0_ffn_W2"].reshape(E0, C0, P, P).transpose(0, 2, 1, 3).reshape(E0, P, F0)
    l1w = np.stack([v["L1_attn_qkv_w"], v["L1_attn_delta_w"], v["L1_attn_qkv_w"].T, v["L1_attn_delta_w"].T], axis=1)
    e1, e3 = (v[n].reshape(NP, 2, P, 64).transpose(0, 2, 1, 3).reshape(NP, P, P) for n in ("L1_ffn_w1", "L1_ffn_w3"))
    e2 = v["L1_ffn_w2"].reshape(NP, P, P)
    wl1 = np.concatenate([e1, e3, e2], axis=2).reshape(NP // 3, 3, P, PW).transpose(0, 2, 1, 3)
    i = np.arange(P)
    j = np.arange(32)
    other = (i[:, None] % 32 // 16 != j[None, :] // 16).astype(f)
    itself = (i[:, None] % 32 == j[None, :]).astype(f)
    ident = np.eye(P, dtype=f)
    pick1 = np.zeros((P, ER), f)
    pick1[np.arange(ER), np.arange(ER)] = 1
    pick1[ER + np.arange(ER), np.arange(ER)] = 2.0 ** -11
    pick0 = np.zeros((P, E0), f)
    pick0[np.arange(E0), np.arange(E0)] = 1
    pick0[E0 + np.arange(E0), np.arange(E0)] = 2.0 ** -11
    heads = (i[:, None] // DH1 == np.arange(H)[None, :]).astype(f)
    b2s = np.ones((P, 1), f)
    b2s[E0:16] = 2.0 ** -11
    consts = np.concatenate([ident, np.maximum(other, itself), other, pick1, pick0, heads, b2s], axis=1)

    arrays = {"xT": x.reshape(NT, P, KC * P), "tokWT": tokWT.reshape(P, KC * P), "rows": rows, "cols": cols,
              "consts": consts, "wqkvT": w.T, "wqkvN": w.reshape(12, P, P).transpose(1, 0, 2).reshape(P, 12 * P),
              "woT": wo.T.reshape(C0, P, P).transpose(1, 0, 2).reshape(P, C0 * P), "woN": wo,
              "l1w": l1w.reshape(P, 4 * P), "b2x": np.concatenate([v["L0_ffn_b2"]] * 2, axis=0),
              "wl0": np.concatenate([w1, w2], axis=2), "wl1": wl1.reshape(NP // 3, P, 3 * PW)}
    arrays = {k: np.ascontiguousarray(a) for k, a in arrays.items()}
    nc = bacc.Bacc("TRN2", target_bir_lowering=False, num_devices=1)
    args = [nc.dram_tensor(k, a.shape, mybir.dt.from_np(a.dtype), kind="ExternalInput").ap() for k, a in arrays.items()]
    out = nc.dram_tensor("out", (NT, P, P), F32, kind="ExternalOutput").ap()
    tower(nc, *args, out)
    res = run(nc, [arrays], core_ids=[0])
    return res.results[0]["out"].reshape(32, 16, P)
```

```python
from contextlib import ExitStack

import concourse.bass as bass
from concourse import mybir

F32 = mybir.dt.float32
F16 = mybir.dt.float16
BF16 = mybir.dt.bfloat16
ALU = mybir.AluOpType
ACT = mybir.ActivationFunctionType
AX = mybir.AxisListType.X

P = 128
NT = 4
N = NT * P
KC = 6
H = 8
DH0, DH1 = 64, 16
INNER = H * DH0
E0, F0 = 8, 512
C0 = F0 // P
NP = 33
ER = 64
TOPK1 = 6
RING = 6
ACT_UNITS = [0, 2, 4, 5, 6, 7, 8, 10]
DVE_UNITS = [1, 3, 4, 5, 6, 7, 9, 11]
QW = 256
OUT0 = [2, 3, 7, 2]
PW = 3 * P
BIG = float(2 ** 100)
WS, HS, LS = 64.0, 16.0, 2048.0
EPS_LN, EPS_RMS = 1e-5, 1.1920929e-07

ROW = {"tok_b": (0, 128), "b_out": (128, 256), "br": (256, 264), "gate_bias": (264, 328), "sigma": (328, 330),
       "temp": (330, 331)}
ROWN = 331
COL = {"u_qkv": (0, 1), "u_out": (1, 5), "b1": (5, 37), "wr": (37, 45), "gw": (45, 109),
       "g": (109, 112)}
COLN = 112
CST = {"ident": (0, 128), "mask0": (128, 160), "parity": (160, 162), "pick1": (162, 226), "pick0": (226, 234),
       "heads": (234, 242), "lo_scale0": (242, 243), "lo_scale1": (243, 244)}
CSTN = 244


def tower(nc, xT, tokWT, rows, cols, consts, wqkvT, wqkvN, woT, woN, l1w, b2x, perms, wl0, wl1, out):
    with ExitStack() as ctx:
        def sb(name, shape, dt=F32):
            return ctx.enter_context(nc.sbuf_tensor(name, shape, dt))

        def sem(name):
            return ctx.enter_context(nc.semaphore(name))

        x_sb = sb("x_sb", [P, NT, KC, P])
        tokw = sb("tokw", [P, KC, P])
        rows_sb = sb("rows_sb", [P, ROWN])
        cols_sb = sb("cols_sb", [P, COLN])
        cst = sb("cst", [P, CSTN])
        wqkvT_sb = sb("wqkvT_sb", [P, 3 * INNER])
        wqkvN_sb = sb("wqkvN_sb", [P, 3 * INNER // P, P])
        woT_sb = sb("woT_sb", [P, C0, P])
        woN_sb = sb("woN_sb", [P, INNER])
        l1w_sb = sb("l1w_sb", [P, 4, P])
        w1n = sb("w1n", [P, P])
        w1t = sb("w1t", [P, P])
        b2_sb = sb("b2_sb", [16, P])
        stage = sb("stage", [P, NP * PW])
        st0 = stage[:, 0:E0 * 2 * F0].rearrange("p (a b) -> p a b", b=2 * F0)
        st1 = stage
        w0h = sb("w0h", [P, E0 * 2 * F0], F16)
        w0l = sb("w0l", [P, E0 * 2 * F0], F16)
        w1h = sb("w1h", [P, RING, PW], F16)
        w1l = sb("w1l", [P, RING, PW], F16)
        negI = sb("negI", [P, P], BF16)
        perm = sb("perm", [P, 2, P])
        m0b = sb("m0b", [P, H, 32], BF16)
        ones = sb("ones", [P, P])
        mhalf = sb("mhalf", [P, 32])
        phalf = sb("phalf", [P, 2])
        sel1 = sb("sel1", [P, ER, DH0], F16)
        sel0 = sb("sel0", [P, E0, P], F16)
        wrs = sb("wrs", [P, 2, ER + E0], F16)
        h = sb("h", [P, NT, P])
        hb = sb("hb", [P, NT, P])
        stats = sb("stats", [P, NT, 6])
        mv = sb("mv", [P, NT, 2])
        vpe = sb("vpe", [P, NT])
        rstd = sb("rstd", [P, NT])
        xn = sb("xn", [P, NT, P])
        xnT = sb("xnT", [P, N])
        xfh = sb("xfh", [P, N], F16)
        xfl = sb("xfl", [P, N], F16)
        big = sb("big", [P, 8, N])
        q1 = sb("q1", [P, N // 32, 2, 32])
        vA = sb("vA", [P, NT, H, DH0 + 1])
        on = sb("on", [P, 2, H, DH0])
        v1 = sb("v1", [P, NT, 2, 4, 32])
        pb = sb("pb", [P, 2, H, 32])
        pc = sb("pc", [P, NT, P])
        pk = sb("pk", [P, 2, H, 32])
        hg2 = sb("hg2", [P, H])
        oT = sb("oT", [P, 2, 4, P])
        mx = sb("mx", [P, 2, H])
        mxc = sb("mxc", [P, 2, H])
        rs = sb("rs", [P, 2, H])
        cs = sb("cs", [P, 2, H])
        gram = sb("gram", [P, P])
        sna = sb("sna", [P, 2])
        snb = sb("snb", [P, 5])
        snb2 = sb("snb2", [P, 5])
        sn4 = sb("sn4", [P, 4])
        snr = sb("snr", [P, 8])
        etemp = sb("etemp", [P, 1])
        cexp = sb("cexp", [P, 1])
        cout = sb("cout", [P, 1])
        lg0 = sb("lg0", [P, NT, ER])
        lgm = sb("lgm", [P, NT])
        lgs = sb("lgs", [P, NT])
        top8 = sb("top8", [P, NT, 8])
        gates = sb("gates", [P, NT, ER])
        g16 = sb("g16", [P, NT, ER], F16)
        gT = sb("gT", [P, N], F16)
        gT32 = sb("gT32", [16, N])
        b1s = sb("b1s", [P, E0 * C0])
        ms = sb("ms", [P, 32])
        xf = x_sb[:].rearrange("p a b c -> p (a b c)")

        def two(ap):
            return ap.rearrange("p (a b) -> p a b", b=N)
        r, u, s = two(xf[:, 0:2 * N]), two(xf[:, 2 * N:4 * N]), two(xf[:, 4 * N:6 * N])
        r0 = two(xf[:, 0:4 * N])
        G, acc = two(wqkvT_sb[:, 0:2 * N]), wqkvT_sb[:, 2 * N:3 * N]
        nf = wqkvN_sb[:].rearrange("p a b -> p (a b)")
        yt, wtm = two(nf[:, 0:2 * N]), nf[:, 2 * N:3 * N]
        wsq = tokw[:].rearrange("p a b -> p (a b)")[:, 0:N]
        q0 = two(stage[:, 3 * PW * 8:3 * PW * 8 + 4 * N])
        pb1, pk1 = (p[:].rearrange("p a b c -> p (a b c)").rearrange("p (a b) -> p a b", b=P)
                    for p in (pb, pk))
        bf = big[:].rearrange("p a b -> p (a b)")
        wqh, wql = (w[:].rearrange("p a b -> p (a b)")[:, 0:3 * INNER] for w in (w1h, w1l))
        hh, hl = two(bf[:, 0:2 * N].bitcast(F16)), two(bf[:, 2 * N:4 * N].bitcast(F16))
        k0 = bf.rearrange("p (j b c d) -> p j b c d", j=4, c=2, d=32)
        k1 = bf.rearrange("p (a h d) -> p a h d", h=H, d=32)
        outs = hb
        of = oT[:].rearrange("p a b c -> p (a b c)")
        gcb = of[:, 0:N].rearrange("p (a b) -> p a b", a=NT)
        rep, bia = (of[:, N + 256 * i:N + 256 * (i + 1)].rearrange("p (a b) -> p a b", a=NT) for i in (0, 1))

        lower = [ctx.enter_context(nc.psum_tensor(f"bank{i}", [P, 512], F32)) for i in range(4)]
        upper = ctx.enter_context(nc.psum_tensor("banks4to7", [P, 4, 512], F32))
        B = [b[:] for b in lower] + [upper[:, i] for i in range(4)]

        def row(name):
            a, b = ROW[name]
            return rows_sb[:, a:b]

        def col(name):
            a, b = COL[name]
            return cols_sb[:, a:b]

        def con(name):
            a, b = CST[name]
            return cst[:, a:b]

        def over(ap, n):
            return ap.unsqueeze(2).broadcast_to([ap.shape[0], ap.shape[1], n])

        def along(ap, n):
            return ap.unsqueeze(1).broadcast_to([ap.shape[0], n, ap.shape[1]])

        def by_head(ap):
            return ap.rearrange("p (a b) -> p a b", b=32)

        def by16(ap):
            return ap.rearrange("p (a b) -> p a b", b=16)

        def tile(t):
            return slice(P * t, P * t + P)

        ident = con("ident")

        d_col, d_row, d_cst, d_tokw = sem("d_col"), sem("d_row"), sem("d_cst"), sem("d_tokw")
        d_x = [sem(f"d_x{t}") for t in range(NT)]
        d_wqT, d_wqN, d_wo, d_l1w = sem("d_wqT"), sem("d_wqN"), sem("d_wo"), sem("d_l1w")
        d_perm = sem("d_perm")
        d_w0 = [sem(f"d_w0_{e}") for e in range(E0)]
        d_w1 = [sem(f"d_w1_{c}") for c in range(NP // 3)]
        d_out = sem("d_out")
        pool_const = sem("pool_const")
        hg2_ready = sem("hg2_ready")
        mask_ready = sem("mask_ready")
        act_setup = sem("act_setup")
        sn_gram, sn_acopy, sn_b, sn_sums, sn_tot, sn_ratio, sn_norm, sn_scales, temp_exp = (
            sem(n) for n in ("sn_gram", "sn_acopy", "sn_b", "sn_sums", "sn_tot", "sn_ratio", "sn_norm", "sn_scales",
                             "temp_exp"))
        tok_done, ln_var, ln_rstd, ln_xn, ln_T = (sem(n) for n in ("tok_done", "ln_var", "ln_rstd", "ln_xn", "ln_T"))
        xnT_a, xfl_v = sem("xnT_a"), sem("xfl_v")
        wq_hi, wq_lo = sem("wq_hi"), sem("wq_lo")
        qkv_mm, qkv_ev_a, qkv_ev_v = sem("qkv_mm"), sem("qkv_ev_a"), sem("qkv_ev_v")
        s_mm, s_sub, s_exp, s_tr, s_av, s_on, s_oTp, s_oT, s_proj, s_hup, hb_done = (
            sem(n) for n in ("s_mm", "s_sub", "s_exp", "s_tr", "s_av", "s_on", "s_oTp", "s_oT", "s_proj", "s_hup",
                             "hb_done"))
        w0_hi = sem("w0_hi")
        w0_lo = sem("w0_lo")
        r0_mm, r0_sub, r0_exp, r0_gcb, r0_T, r0_gT, r0_b2, r0_acc = (
            sem(n) for n in ("r0_mm", "r0_sub", "r0_exp", "r0_gcb", "r0_T", "r0_gT", "r0_b2", "r0_acc"))
        up0, relu0, hi0, lo0v, lo0p, down0, gmm0, gev0, y0, yt0, acc0 = (
            sem(n) for n in ("up0", "relu0", "hi0", "lo0v", "lo0p", "down0", "gmm0", "gev0", "y0", "yt0", "acc0"))
        f0_T, f0_h = sem("f0_T"), sem("f0_h")
        w1_sum, w_mm, w_sq, w_tm, w_ms, w_inv, w_n, v_mm, v_a, qk_T, k1_v, qk_a = (
            sem(n) for n in ("w1_sum", "w_mm", "w_sq", "w_tm", "w_ms", "w_inv", "w_n", "v_mm", "v_a",
                             "qk_T", "k1_v", "qk_a"))
        t_mm, t_subr, t_subc, t_expr, t_expc, t_cinv, t_col, t_probs, t_av, t_yT, t_proj, t_hup = (
            sem(n) for n in ("t_mm", "t_subr", "t_subc", "t_expr", "t_expc", "t_cinv", "t_col", "t_probs", "t_av", "t_yT", "t_proj",
                             "t_hup"))
        r1_mm, r1_sub, r1_exp, r1_inv, r1_norm, r1_g16, r1_gcb, r1_T, r1_gT = (
            sem(n) for n in ("r1_mm", "r1_sub", "r1_exp", "r1_inv", "r1_norm", "r1_g16", "r1_gcb", "r1_T",
                             "r1_gT"))
        w1_hi, w1_lo, h1mm, h3mm, g1mm, silu1, u1, r1, hi1, lo1, down1, y1, y1_ev, y1_T, out_v = (
            sem(n) for n in ("w1_hi", "w1_lo", "h1mm", "h3mm", "g1mm", "silu1", "u1", "r1", "hi1", "lo1", "down1",
                             "y1", "y1_ev", "y1_T", "out_v"))
        dve_step, pool_step, act_step = sem("dve_step"), sem("pool_step"), sem("act_step")

        block = ctx.enter_context(nc.Block())

        @block.sync
        def _(sp):
            sp.dma_start(tokw[:], tokWT).then_inc(d_tokw, 16)
            for t in range(NT):
                sp.dma_start(x_sb[:, t], xT[t]).then_inc(d_x[t], 16)
                if t == 0:
                    sp.dma_start(rows_sb[:], rows.broadcast_to([P, ROWN])).then_inc(d_row, 16)
            sp.dma_start(cst[:], consts).then_inc(d_cst, 16)
            sp.dma_start(cols_sb[:], cols).then_inc(d_col, 16)
            sp.dma_start(wqkvN_sb[:], wqkvN).then_inc(d_wqN, 16)
            sp.dma_start(wqkvT_sb[:], wqkvT).then_inc(d_wqT, 16)
            sp.dma_start(woT_sb[:], woT).then_inc(d_wo, 16)
            sp.dma_start(woN_sb[:], woN).then_inc(d_wo, 16)
            for e in range(E0):
                sp.dma_start(st0[:, e], wl0[e]).then_inc(d_w0[e], 16)
            sp.dma_start(l1w_sb[:], l1w).then_inc(d_l1w, 16)
            sp.dma_start(b2_sb[:], b2x).then_inc(d_l1w, 16)
            sp.dma_start(perm[:], perms).then_inc(d_perm, 16)
            for c in range(NP // 3):
                if c < 8:
                    sp.wait_ge(w0_lo, min(3 * PW * (c + 1) - 1, E0 * 1024 - 1) // QW + 1)
                elif c == 8:
                    sp.wait_ge(s_mm, NT)
                sp.dma_start(st1[:, 3 * PW * c:3 * PW * (c + 1)], wl1[c]).then_inc(d_w1[c], 16)
            for t in range(NT):
                sp.wait_ge(out_v, t + 1)
                sp.dma_start(out[t], outs[:, t]).then_inc(d_out, 16)
            sp.wait_ge(d_out, 16 * NT)

        @block.gpsimd
        def _(pool):
            nc.gpsimd.memset(ones[:], 1.0)
            nc.gpsimd.memset(mhalf[:], -0.5)
            nc.gpsimd.memset(phalf[:], 0.5)
            nc.gpsimd.memset(gT[:], 0.0)
            nc.gpsimd.memset(q1[:], 0.0)
            nc.gpsimd.memset(vA[:, :, :, DH0:DH0 + 1], 1.0)
            nc.gpsimd.memset(bf, 0.0).then_inc(pool_const, 1)

            def norm(k):
                for t in range(NT):
                    pool.wait_ge(ln_var, NT * k + t + 1)
                    nc.gpsimd.tensor_tensor(rstd[:, t:t + 1], vpe[:, t:t + 1], mhalf[:, 0:1],
                                            ALU.pow).then_inc(ln_rstd, 1)

            pool.wait_ge(pool_const, 1)
            norm(0)
            for t in range(NT):
                nc.gpsimd.tensor_tensor(hb[:, t], h[:, t], row("b_out"), ALU.add).then_inc(hb_done, 1)
            pool.wait_ge(sn_ratio, 1)
            nc.gpsimd.tensor_tensor(snr[:, 4:6], snr[:, 2:4], phalf[:], ALU.pow).then_inc(sn_norm, 1)
            pool.wait_ge(d_l1w, 32)
            nc.gpsimd.tensor_tensor(w1n[:], l1w_sb[:, 0], l1w_sb[:, 1], ALU.add)
            nc.gpsimd.tensor_tensor(w1t[:], l1w_sb[:, 2], l1w_sb[:, 3], ALU.add).then_inc(w1_sum, 1)
            norm(1)

            def lo_half(n, slot):
                pool.wait_ge(hi0, n + 1)
                nc.gpsimd.tensor_tensor(hl[:, slot, 256:512], r0[:, slot, 256:512], hh[:, slot, 256:512],
                                        ALU.subtract).then_inc(lo0p, 1)

            def add_expert(e, b):
                pool.wait_ge(yt0, e + 1)
                nc.gpsimd.tensor_tensor(acc[:], acc[:], yt[:, b], ALU.add).then_inc(acc0, 1)
                pool.wait_ge(acc0, e + 1)

            def step0(n, e, k):
                lo_half(n, k % 4)
                if k % 4 == 2 and not (isinstance(n, int) and n == 6):
                    add_expert(e - 1, (k // 4 + 1) % 2)

            for n in range(4):
                lo_half(n, n)
            for n in range(4, 8):
                step0(n, 1, n)
            pool.wait_ge(r0_acc, 1)
            add_expert(0, 0)
            with pool.Fori(0, 2) as m:
                for k in range(8):
                    step0(8 * m + 8 + k, 2 * m + 2 + k // 4, k)
            for n in range(24, 32):
                step0(n, n // 4, n % 8)
            norm(2)
            def column_part(t):
                b = t % 2
                pool.wait_ge(t_cinv, t + 1)
                nc.gpsimd.tensor_tensor(by16(pc[:, t]), by16(pc[:, t]), over(cs[:, b], DH1), ALU.mult).then_inc(t_col, 1)

            for t in range(NT):
                column_part(t)
            norm(3)
            pool.wait_ge(r1_inv, 1)
            nc.gpsimd.tensor_tensor(gates[:], lg0[:], over(lgs[:], ER), ALU.mult).then_inc(r1_norm, 1)

            def lo_pair(p, k):
                pool.wait_ge(hi1, p + 1)
                src = u if isinstance(p, int) and p == 0 else r
                nc.gpsimd.tensor_tensor(hl[:, k % 3, :], src[:, k % 2, :], hh[:, k % 3, :],
                                        ALU.subtract).then_inc(lo1, 1)

            for p in range(4):
                lo_pair(p, p)
            with pool.Fori(0, 4) as m:
                for k in range(RING):
                    lo_pair(RING * m + 4 + k, k + 4)
            for p in range(28, NP):
                lo_pair(p, p)

        @block.scalar
        def _(act):
            act.wait_ge(d_row, 16)
            nc.scalar.activation(etemp[:], row("temp"), ACT.Exp).then_inc(temp_exp, 1)
            act.wait_ge(d_col, 16)
            nc.scalar.activation(wrs[:, 0, 0:ER], col("gw"), ACT.Copy, scale=WS)
            nc.scalar.activation(wrs[:, 0, ER:ER + E0], col("wr"), ACT.Copy, scale=WS)
            nc.scalar.activation(b1s[:], col("b1"), ACT.Copy, scale=HS).then_inc(act_setup, 1)
            act.wait_ge(d_cst, 16)
            nc.scalar.activation(sel0[:], over(con("pick0"), P), ACT.Copy).then_inc(act_setup, 1)

            act.wait_ge(d_wqT, 16)
            for i in range(3):
                nc.scalar.activation(wqh[:, INNER * i:INNER * (i + 1)], wqkvT_sb[:, INNER * i:INNER * (i + 1)],
                                     ACT.Copy, scale=WS).then_inc(wq_hi, 1)
            act.wait_ge(ln_T, NT)
            nc.scalar.activation(xfh[:], B[0], ACT.Copy).then_inc(xnT_a, 1)
            def hi_expert(e):
                act.wait_ge(d_w0[e], 16)
                nc.scalar.activation(w0h[:, 1024 * e:1024 * (e + 1)], st0[:, e, :], ACT.Copy,
                                     scale=WS).then_inc(w0_hi, 4)

            act.wait_ge(pool_const, 1)
            for k in ACT_UNITS:
                act.wait_ge(qkv_mm, k + 1)
                bank = B[2 + k % 4]
                if k < 4:
                    last = nc.scalar.activation(q0[:, k, :], bank[:], ACT.Copy)
                elif k < 8:
                    last = nc.scalar.activation(k0[0:64, k - 4, :, 0, :],
                                                bank[0:64].rearrange("p (a b) -> p a b", b=32), ACT.Copy)
                else:
                    last = nc.scalar.activation(vA[:, k - 8, :, 0:DH0], bank[:].rearrange("p (a b) -> p a b", b=DH0),
                                                ACT.Copy)
                last.then_inc(qkv_ev_a, 1)

            def exp0(t):
                act.wait_ge(s_sub, t + 1)
                nc.scalar.activation(pb[:, t % 2], pb[:, t % 2], ACT.Exp, scale=cexp[:]).then_inc(s_exp, 1)

            def ev_oT(t):
                act.wait_ge(s_oTp, t + 1)
                if t >= 2:
                    act.wait_ge(s_proj, t - 1)
                nc.scalar.activation(oT[:, t % 2], B[6].rearrange("p (a b) -> p a b", b=P), ACT.Copy).then_inc(s_oT, 1)

            act.wait_ge(sn_scales, 1)
            exp0(0)
            exp0(1)
            hi_expert(0)
            exp0(2)
            exp0(3)
            ev_oT(0)
            for e in range(0, ER, 16):
                last = nc.scalar.activation(sel1[:, e:e + 16, :], over(con("pick1")[:, e:e + 16], DH0), ACT.Copy)
                if e == 16:
                    ev_oT(1)
            last.then_inc(act_setup, 1)
            hi_expert(1)
            ev_oT(2)
            ev_oT(3)
            for e in range(2, E0):
                act.wait_ge(d_w0[e], 16)

            act.wait_ge(ln_T, 2 * NT)
            nc.scalar.activation(xfh[:], B[0], ACT.Copy).then_inc(xnT_a, 1)
            act.wait_ge(r0_sub, 1)
            nc.scalar.activation(lg0[:, :, 0:E0], lg0[:, :, 0:E0], ACT.Exp).then_inc(r0_exp, 1)

            def relu(n, c, slot):
                act.wait_ge(up0, n + 1)
                if slot is not None:
                    act.wait_ge(lo0v, n - 3)
                    act.wait_ge(lo0p, n - 3)
                nc.scalar.activation(r0[:, c % 4], B[3 + c % 2], ACT.Relu, scale=HS / WS,
                                     bias=b1s[:, bass.ds(n, 1)]).then_inc(relu0, 1)

            def ev_gate(e, b, used):
                act.wait_ge(gmm0, e + 1)
                if used:
                    act.wait_ge(yt0, e - 1)
                nc.scalar.activation(G[:, b], B[5 + b], ACT.Copy).then_inc(gev0, 1)

            def hi_quarter(i):
                nc.scalar.activation(w0h[:, bass.ds(QW * i, QW)], stage[:, bass.ds(QW * i, QW)], ACT.Copy,
                                     scale=WS).then_inc(w0_hi, 1)

            def step0(n, e, k, used=True):
                if not isinstance(n, int) or n < 28:
                    hi_quarter(n + 4)
                relu(n, k, n)
                if k % 4 == 3:
                    ev_gate(e, k // 4, used)

            for n in range(4):
                relu(n, n, None)
            for n in range(4, 8):
                if n == 6:
                    act.wait_ge(r0_T, 1)
                    nc.scalar.activation(gT[0:16, :], B[2][0:16, :], ACT.Copy, scale=con("lo_scale0")[0:16])
                    nc.scalar.activation(gT32[:], B[2][0:16, :], ACT.Copy).then_inc(r0_gT, 1)
                if n == 7:
                    act.wait_ge(r0_b2, 1)
                    nc.scalar.activation(acc[:], B[1], ACT.Copy).then_inc(r0_acc, 1)
                    ev_gate(0, 0, False)
                step0(n, 1, n, used=False)
            with act.Fori(0, 2) as m:
                for k in range(8):
                    step0(8 * m + 8 + k, 2 * m + 2 + k // 4, k)
            for n in range(24, 32):
                step0(n, n // 4, n % 8)

            def preload(function):
                nc.scalar.activation(etemp[:], ones[:, 0:1], function)

            preload(ACT.Sqrt)
            act.wait_ge(ln_T, 3 * NT)
            nc.scalar.activation(xnT[:], B[0], ACT.Copy).then_inc(xnT_a, 1)
            for t in range(NT):
                act.wait_ge(w_mm, t + 1)
                nc.scalar.activation(wsq[:, tile(t)], B[t][:, 0:P], ACT.Square).then_inc(w_sq, 1)
            for t in range(NT):
                nc.scalar.activation(wtm[:, tile(t)], B[t][:, 0:P], ACT.Copy).then_inc(w_tm, 1)
                act.wait_ge(w_ms, t + 1)
                nc.scalar.activation(ms[:, 8 * t:8 * t + 8], ms[:, 8 * t:8 * t + 8], ACT.Sqrt).then_inc(w_inv, 1)

            def ev_qk(t):
                act.wait_ge(qk_T, t + 1)
                qT = B[4 + t][:, 0:P].rearrange("p (a b c) -> p a b c", b=2, c=16)
                for i in (0, 1):
                    nc.scalar.activation(q1[:, 4 * t:4 * t + 4, i, 16 * i:16 * i + 16], qT[:, :, i], ACT.Copy,
                                         scale=col("g")[:, 0:1])
                for hd in range(4, H):
                    last = nc.scalar.activation(k1[:, 4 * t:4 * t + 4, hd, :], by_head(B[4 + t][:, 0:P]),
                                                ACT.Copy, scale=hg2[:, hd:hd + 1])
                last.then_inc(qk_a, 1)

            def exp1(t):
                act.wait_ge(t_subr, t + 1)
                nc.scalar.activation(pb1[:, t % 2], pb1[:, t % 2], ACT.Exp, scale=0.25).then_inc(t_expr, 1)
                act.wait_ge(t_subc, t + 1)
                nc.scalar.activation(pc[:, t], pc[:, t], ACT.Exp, scale=0.25).then_inc(t_expc, 1)

            def ev_v(g):
                act.wait_ge(v_mm, g + 1)
                src = B[4 + g].rearrange("p (a b c) -> p a b c", b=2, c=DH1)
                dst = v1[:, 2 * g:2 * g + 2].rearrange("p t i j c -> p (t i j) c")
                for i in (0, 1):
                    last = nc.scalar.activation(dst[:, :, DH1 * i:DH1 * i + DH1], src[:, :, i], ACT.Copy,
                                                scale=con("parity")[:, i:i + 1])
                last.then_inc(v_a, 1)

            def ev_yT(t):
                act.wait_ge(t_av, t + 1)
                if t >= 2:
                    act.wait_ge(t_proj, t - 1)
                nc.scalar.activation(by_head(oT[:, t % 2, 0]), upper[:, :, 0:32], ACT.Copy,
                                     scale=col("g")[:, 2:3]).then_inc(t_yT, 1)

            act.wait_ge(hg2_ready, 1)
            ev_qk(0)
            preload(ACT.Exp)
            ev_qk(1)
            exp1(0)
            ev_qk(2)
            ev_qk(3)
            exp1(1)
            ev_v(0)
            exp1(2)
            ev_v(1)
            exp1(3)
            ev_yT(0)
            ev_yT(1)
            ev_yT(2)
            ev_yT(3)

            def hi_weights(p, slot):
                nc.scalar.activation(w1h[:, slot], st1[:, bass.ds(PW * p, PW)], ACT.Copy, scale=WS).then_inc(w1_hi, 1)

            for c in range(NP // 3):
                act.wait_ge(d_w1[c], 16)
            for p in range(4):
                hi_weights(p, p)
            act.wait_ge(ln_T, 4 * NT)
            nc.scalar.activation(xfh[:], B[0], ACT.Copy).then_inc(xnT_a, 1)
            act.wait_ge(r1_sub, 1)
            nc.scalar.activation(lg0[:], lg0[:], ACT.Exp, scale=1.0 / WS).then_inc(r1_exp, 1)

            def silu(p, b, used):
                act.wait_ge(h1mm, p + 1)
                if used:
                    act.wait_ge(u1, p - 1)
                nc.scalar.activation(s[:, b], B[3 + b], ACT.Silu, scale=1.0 / WS).then_inc(silu1, 1)

            def hi_hidden(p, k, used):
                act.wait_ge(r1, p + 1)
                if used:
                    act.wait_ge(down1, p - 2)
                nc.scalar.activation(hh[:, k % 3], r[:, k % 2], ACT.Copy).then_inc(hi1, 1)

            def next_weights(p, slot, used):
                if used:
                    act.wait_ge(down1, p - RING + 1)
                hi_weights(p, slot)

            silu(0, 0, False)
            act.wait_ge(u1, 1)
            nc.scalar.activation(hh[:, 0], u[:, 0], ACT.Copy).then_inc(hi1, 1)
            silu(1, 1, False)
            silu(2, 0, True)
            next_weights(4, 4, False)
            act.wait_ge(r1_g16, 1)
            nc.scalar.activation(gcb[:, :, 0:ER], g16[:], ACT.Copy).then_inc(r1_gcb, 1)
            silu(3, 1, True)
            next_weights(5, 5, False)
            act.wait_ge(r1_T, 1)
            nc.scalar.activation(gT[:], B[2], ACT.Copy, scale=con("lo_scale1")).then_inc(r1_gT, 1)
            hi_hidden(1, 1, False)
            hi_hidden(2, 2, False)
            with act.Fori(0, 4) as m:
                for k in range(RING):
                    silu(RING * m + 4 + k, k % 2, True)
                    next_weights(RING * m + 6 + k, k, True)
                    hi_hidden(RING * m + 3 + k, k + 3, True)
            for p in range(28, NP):
                silu(p, p % 2, True)
                if p + 2 < NP:
                    next_weights(p + 2, (p + 2) % RING, True)
                hi_hidden(p - 1, p - 1, True)
            hi_hidden(NP - 1, NP - 1, True)
            act.wait_ge(down1, NP)
            for t in range(NT):
                nc.scalar.activation(acc[:, tile(t)], B[0][:, tile(t)], ACT.Copy,
                                     scale=1.0 / (WS * HS)).then_inc(y1_ev, 1)

        @block.vector
        def _(dve):
            count = [0]

            def mark(ins):
                count[0] += 1
                ins.then_inc(dve_step, 1)
                return count[0]

            def link(ins):
                dve.wait_ge(dve_step, mark(ins))

            def norm_stats(k, t):
                link(nc.vector.bn_stats(stats[:, t], h[:, t]))
                link(nc.vector.bn_aggr(mv[:, t], stats[:, t]))
                nc.vector.tensor_scalar_add(vpe[:, t:t + 1], mv[:, t, 1:2], EPS_LN).then_inc(ln_var, 1)

            def norm_apply(k, t):
                dve.wait_ge(ln_rstd, NT * k + t + 1)
                nc.vector.tensor_scalar(xn[:, t], h[:, t], mv[:, t, 0:1], rstd[:, t:t + 1],
                                        ALU.subtract, ALU.mult).then_inc(ln_xn, 1)

            dve.wait_ge(d_row, 16)
            for t in range(NT):
                dve.wait_ge(tok_done, t + 1)
                link(nc.vector.tensor_tensor(h[:, t], B[t][:, 0:P], row("tok_b"), ALU.add))
                norm_stats(0, t)
                if t >= 1:
                    norm_apply(0, t - 1)
            norm_apply(0, NT - 1)

            dve.wait_ge(act_setup, 1)
            nc.vector.scalar_tensor_tensor(wrs[:, 1, 0:ER], col("gw"), WS, wrs[:, 0, 0:ER], ALU.mult, ALU.subtract)
            nc.vector.scalar_tensor_tensor(wrs[:, 1, ER:ER + E0], col("wr"), WS, wrs[:, 0, ER:ER + E0],
                                           ALU.mult, ALU.subtract).then_inc(mask_ready, 1)
            dve.wait_ge(d_cst, 16)
            nc.vector.tensor_scalar(negI[:], ident, -BIG, None, ALU.mult)
            nc.vector.tensor_copy(m0b[:], along(con("mask0"), H)).then_inc(mask_ready, 1)
            nc.vector.tensor_scalar(hg2[:], con("heads"), col("g")[:, 1:2], None, ALU.mult).then_inc(hg2_ready, 1)

            def lo_qkv(i):
                part = slice(INNER * i, INNER * (i + 1))
                dve.wait_ge(wq_hi, i + 1)
                nc.vector.scalar_tensor_tensor(wql[:, part], wqkvT_sb[:, part], WS, wqh[:, part], ALU.mult,
                                               ALU.subtract).then_inc(wq_lo, 1)

            lo_qkv(0)
            dve.wait_ge(sn_gram, 1)
            nc.vector.tensor_copy(gram[:], B[6][:, 0:P])
            nc.vector.tensor_copy(sna[:, 0:1], B[6][:, P:P + 1]).then_inc(sn_acopy, 1)
            dve.wait_ge(xnT_a, 1)
            nc.vector.tensor_tensor(xfl[:], B[0], xfh[:], ALU.subtract).then_inc(xfl_v, 1)
            lo_qkv(1)
            lo_qkv(2)
            dve.wait_ge(sn_b, 1)
            link(nc.vector.tensor_copy(snb[:], B[7][:, 0:5]))
            nc.vector.tensor_tensor(sn4[:, 0:1], snb[:, 0:1], col("u_qkv"), ALU.mult)
            nc.vector.tensor_tensor(sn4[:, 1:2], sna[:, 0:1], sna[:, 0:1], ALU.mult)
            link(nc.vector.tensor_tensor(snb2[:], snb[:], snb[:], ALU.mult))
            nc.vector.tensor_copy(sn4[:, 2:3], snb2[:, 0:1])
            nc.vector.tensor_reduce(sn4[:, 3:4], snb2[:, 1:5], AX, ALU.add).then_inc(sn_sums, 1)

            def lo_expert(e):
                dve.wait_ge(w0_hi, 4 * e + 4)
                nc.vector.scalar_tensor_tensor(w0l[:, 1024 * e:1024 * (e + 1)], st0[:, e, :], WS,
                                               w0h[:, 1024 * e:1024 * (e + 1)], ALU.mult, ALU.subtract).then_inc(w0_lo, 4)

            dve.wait_ge(pool_const, 1)
            for k in DVE_UNITS:
                dve.wait_ge(qkv_mm, k + 1)
                bank = B[2 + k % 4]
                if k < 4:
                    last = nc.vector.tensor_copy(q0[:, k, :], bank[:])
                elif k < 8:
                    last = nc.vector.tensor_copy(k0[64:P, k - 4, :, 1, :],
                                                 bank[64:P].rearrange("p (a b) -> p a b", b=32))
                else:
                    last = nc.vector.tensor_copy(vA[:, k - 8, :, 0:DH0], bank[:].rearrange("p (a b) -> p a b", b=DH0))
                last.then_inc(qkv_ev_v, 1)
                if k == 3:
                    dve.wait_ge(sn_tot, 1)
                    link(nc.vector.reciprocal(snr[:, 0:2], B[7][:, 10:12]))
                    nc.vector.tensor_tensor(snr[:, 2:4], B[7][:, 8:10], snr[:, 0:2], ALU.mult).then_inc(sn_ratio, 1)

            dve.wait_ge(sn_norm, 1)
            link(nc.vector.tensor_tensor(snr[:, 6:8], snr[:, 4:6], row("sigma"), ALU.mult))
            link(nc.vector.tensor_tensor(snr[:, 0:1], snr[:, 6:7], snr[:, 6:7], ALU.mult))
            nc.vector.scalar_tensor_tensor(cout[:], snr[:, 6:7], 1.0 / WS, snr[:, 7:8], ALU.mult, ALU.mult)
            dve.wait_ge(temp_exp, 1)
            nc.vector.scalar_tensor_tensor(cexp[:], snr[:, 0:1], 1.0 / (WS * WS), etemp[:], ALU.mult,
                                           ALU.mult).then_inc(sn_scales, 1)

            def center(dst, m, src, done):
                link(nc.vector.tensor_reduce(m, src, AX, ALU.max))
                nc.vector.tensor_tensor(dst, src, over(m, 32), ALU.subtract).then_inc(done, 1)

            def center0(t):
                dve.wait_ge(s_mm, t + 1)
                center(pb[:, t % 2], mx[:, t % 2], by_head(B[t][:, 0:256]), s_sub)

            def by_key0(t):
                dve.wait_ge(s_exp, t + 1)
                if t >= 2:
                    dve.wait_ge(s_av, t - 1)
                nc.vector.transpose(pk[:, t % 2], pb[:, t % 2]).then_inc(s_tr, 1)

            def norm0(t):
                b = t % 2
                dve.wait_ge(s_av, t + 1)
                o = [B[4 * (1 - b) + g][:, 0:4 * (DH0 + 1)].rearrange("p (a b) -> p a b", b=DH0 + 1) for g in (0, 1)]
                nc.vector.reciprocal(rs[:, b, 0:4], o[0][:, :, DH0])
                link(nc.vector.reciprocal(rs[:, b, 4:8], o[1][:, :, DH0]))
                if t >= 2:
                    dve.wait_ge(s_oTp, t - 1)
                for g in (0, 1):
                    last = nc.vector.tensor_tensor(on[:, b, 4 * g:4 * g + 4], o[g][:, :, 0:DH0],
                                                   over(rs[:, b, 4 * g:4 * g + 4], DH0), ALU.mult)
                last.then_inc(s_on, 1)

            def residual0(t):
                dve.wait_ge(s_proj, t + 1)
                dve.wait_ge(hb_done, NT)
                nc.vector.scalar_tensor_tensor(h[:, t], B[OUT0[t]][:, 0:P], cout[:], hb[:, t], ALU.mult,
                                               ALU.add).then_inc(s_hup, 1)
                dve.wait_ge(s_hup, t + 1)
                norm_stats(1, t)

            center0(0)
            center0(1)
            by_key0(0)
            center0(2)
            by_key0(1)
            center0(3)
            norm0(0)
            by_key0(2)
            norm0(1)
            by_key0(3)
            lo_expert(0)
            norm0(2)
            residual0(0)
            norm0(3)
            residual0(1)
            norm_apply(1, 0)
            lo_expert(1)
            residual0(2)
            norm_apply(1, 1)
            residual0(3)
            norm_apply(1, 2)
            norm_apply(1, 3)

            def lo_quarter(i):
                dve.wait_ge(w0_hi, i + 1)
                nc.vector.scalar_tensor_tensor(w0l[:, bass.ds(QW * i, QW)], stage[:, bass.ds(QW * i, QW)], WS,
                                               w0h[:, bass.ds(QW * i, QW)], ALU.mult, ALU.subtract).then_inc(w0_lo, 1)

            def hi_lo(n, slot, used, weights=False):
                dve.wait_ge(relu0, n + 1)
                if used:
                    dve.wait_ge(down0, n - 3)
                nc.vector.tensor_copy(hh[:, slot], r0[:, slot]).then_inc(hi0, 1)
                if weights:
                    lo_quarter(n + 4)
                dve.wait_ge(hi0, n + 1)
                nc.vector.tensor_tensor(hl[:, slot, 0:256], r0[:, slot, 0:256], hh[:, slot, 0:256],
                                        ALU.subtract).then_inc(lo0v, 1)

            dve.wait_ge(xnT_a, 2)
            nc.vector.tensor_tensor(xfl[:], B[0], xfh[:], ALU.subtract).then_inc(xfl_v, 1)
            dve.wait_ge(r0_mm, 1)
            lg = lg0[:, :, 0:E0]
            link(nc.vector.scalar_tensor_tensor(lg, B[1][:, 0:NT * E0].rearrange("p (a b) -> p a b", b=E0), 1.0 / WS,
                                                along(row("br"), NT), ALU.mult, ALU.add))
            link(nc.vector.tensor_reduce(lgm[:], lg, AX, ALU.max))
            nc.vector.tensor_tensor(lg, lg, over(lgm[:], E0), ALU.subtract).then_inc(r0_sub, 1)
            dve.wait_ge(r0_exp, 1)
            for t in range(NT):
                last = nc.vector.max(top8[:, t], lg0[:, t, 0:E0])
            link(last)
            hi_lo(0, 0, False)
            link(nc.vector.memset(top8[:, :, 2:8], -3.0))
            for t in range(NT):
                last = nc.vector.match_replace(rep[:, t, 0:E0], top8[:, t], lg0[:, t, 0:E0], -1.0)
            link(last)
            gt = gates[:, :, 0:E0]
            link(nc.vector.scalar_tensor_tensor(gt, rep[:, :, 0:E0], 0.0, lg, ALU.is_lt, ALU.mult))
            link(nc.vector.tensor_reduce(lgs[:], gt, AX, ALU.add))
            link(nc.vector.reciprocal(lgs[:], lgs[:]))
            link(nc.vector.tensor_tensor(gt, gt, over(lgs[:], E0), ALU.mult))
            hi_lo(1, 1, False)
            link(nc.vector.tensor_copy(g16[:, :, 0:E0], gt))
            nc.vector.tensor_copy(gcb[:, :, 0:E0], g16[:, :, 0:E0])
            nc.vector.tensor_tensor(gcb[:, :, E0:2 * E0], gt, g16[:, :, 0:E0], ALU.subtract).then_inc(r0_gcb, 1)

            def gate0(e, b, used):
                dve.wait_ge(down0, 4 * e + 4)
                dve.wait_ge(gev0, e + 1)
                if used:
                    dve.wait_ge(acc0, e - 1)
                nc.vector.scalar_tensor_tensor(yt[:, b], B[7 * (1 - b)], 1.0 / (WS * HS), G[:, b], ALU.mult,
                                               ALU.mult).then_inc(yt0, 1)

            for n in range(2, 4):
                hi_lo(n, n, False)
            def step0(n, e, k, used=True):
                hi_lo(n, k % 4, True, weights=not isinstance(n, int) or n < 28)
                if k % 4 == 2 and not (isinstance(n, int) and n == 6):
                    gate0(e - 1, (k // 4 + 1) % 2, used)

            for n in range(4, 8):
                step0(n, 1, n, used=False)
            gate0(0, 0, False)
            with dve.Fori(0, 2) as m:
                for k in range(8):
                    step0(8 * m + 8 + k, 2 * m + 2 + k // 4, k, used=False)
            for n in range(24, 32):
                step0(n, n // 4, n % 8)
            gate0(7, 1, True)
            def residual(t):
                dve.wait_ge(f0_T, t + 1)
                nc.vector.tensor_tensor(h[:, t], h[:, t], B[1 + t][:, 0:P], ALU.add).then_inc(f0_h, 1)

            bn, ag = {}, {}

            def stats_of(t):
                dve.wait_ge(f0_h, t + 1)
                bn[t] = mark(nc.vector.bn_stats(stats[:, t], h[:, t]))

            def aggregate(t):
                dve.wait_ge(dve_step, bn[t])
                ag[t] = mark(nc.vector.bn_aggr(mv[:, t], stats[:, t]))

            def variance(t):
                dve.wait_ge(dve_step, ag[t])
                nc.vector.tensor_scalar_add(vpe[:, t:t + 1], mv[:, t, 1:2], EPS_LN).then_inc(ln_var, 1)

            residual(0)
            residual(1)
            stats_of(0)
            residual(2)
            aggregate(0)
            stats_of(1)
            variance(0)
            residual(3)
            aggregate(1)
            stats_of(2)
            variance(1)
            norm_apply(2, 0)
            aggregate(2)
            stats_of(3)
            variance(2)
            norm_apply(2, 1)
            aggregate(3)
            norm_apply(2, 2)
            variance(3)
            norm_apply(2, 3)

            def heads(ap):
                return ap.rearrange("p (a b) -> p a b", b=DH1)

            def mean_square(t):
                dve.wait_ge(w_sq, t + 1)
                link(nc.vector.tensor_reduce(ms[:, 8 * t:8 * t + 8], heads(wsq[:, tile(t)]), AX, ALU.add))
                link(nc.vector.tensor_scalar(ms[:, 8 * t:8 * t + 8], ms[:, 8 * t:8 * t + 8], 1.0 / DH1, EPS_RMS,
                                             ALU.mult, ALU.add))
                nc.vector.reciprocal(ms[:, 8 * t:8 * t + 8], ms[:, 8 * t:8 * t + 8]).then_inc(w_ms, 1)

            def normalised(t):
                w = heads(wtm[:, tile(t)])
                dve.wait_ge(w_inv, t + 1)
                dve.wait_ge(w_tm, t + 1)
                nc.vector.tensor_tensor(w, w, over(ms[:, 8 * t:8 * t + 8], DH1), ALU.mult).then_inc(w_n, 1)

            def masked_keys(t):
                dve.wait_ge(qk_T, t + 1)
                keys = by_head(B[t][:, P:2 * P]).unsqueeze(2).broadcast_to([P, 4, 4, 32])
                mask = hg2[:, 0:4].unsqueeze(1).unsqueeze(3).broadcast_to([P, 4, 4, 32])
                nc.vector.tensor_tensor(k1[:, 4 * t:4 * t + 4, 0:4, :], keys, mask, ALU.mult).then_inc(k1_v, 1)

            def softmaxes(c, d):
                b, e = (c or 0) % 2, (d or 0) % 2
                if c is not None:
                    src = by16(B[c][:, 0:P])
                    dve.wait_ge(t_mm, c + 1)
                    row_max = mark(nc.vector.tensor_reduce(mx[:, b], src, AX, ALU.max))
                    by_key = mark(nc.vector.transpose(pc[:, c], B[c][:, 0:P]))
                    dve.wait_ge(dve_step, row_max)
                    nc.vector.tensor_tensor(by16(pb1[:, b]), src, over(mx[:, b], 16), ALU.subtract).then_inc(t_subr, 1)
                if d is not None:
                    dve.wait_ge(t_expc, d + 1)
                    col_sum = mark(nc.vector.tensor_reduce(cs[:, e], by16(pc[:, d]), AX, ALU.add))
                if c is not None:
                    dve.wait_ge(dve_step, by_key)
                    col_max = mark(nc.vector.tensor_reduce(mxc[:, b], by16(pc[:, c]), AX, ALU.max))
                if d is not None:
                    row_sum = mark(nc.vector.tensor_reduce(rs[:, e], by16(pb1[:, e]), AX, ALU.add))
                    dve.wait_ge(dve_step, col_sum)
                    nc.vector.reciprocal(cs[:, e], cs[:, e]).then_inc(t_cinv, 1)
                if c is not None:
                    dve.wait_ge(dve_step, col_max)
                    nc.vector.tensor_tensor(by16(pc[:, c]), by16(pc[:, c]), over(mxc[:, b], 16), ALU.subtract).then_inc(t_subc, 1)
                if d is not None:
                    dve.wait_ge(dve_step, row_sum)
                    link(nc.vector.reciprocal(rs[:, e], rs[:, e]))
                    link(nc.vector.tensor_tensor(by16(pb1[:, e]), by16(pb1[:, e]), over(rs[:, e], 16), ALU.mult))
                    link(nc.vector.transpose(pk1[:, d], pb1[:, e]))
                    dve.wait_ge(t_col, d + 1)
                    nc.vector.tensor_tensor(pk1[:, d], pk1[:, d], pc[:, d], ALU.add).then_inc(t_probs, 1)

            def residual1(t):
                dve.wait_ge(t_proj, t + 1)
                nc.vector.tensor_tensor(h[:, t], h[:, t], B[t][:, 0:P], ALU.add).then_inc(t_hup, 1)
                dve.wait_ge(t_hup, t + 1)
                norm_stats(3, t)

            dve.wait_ge(hg2_ready, 1)
            mean_square(0)
            mean_square(1)
            mean_square(2)
            normalised(0)
            mean_square(3)
            normalised(1)
            normalised(2)
            normalised(3)
            masked_keys(0)
            masked_keys(1)
            masked_keys(2)
            softmaxes(0, None)
            masked_keys(3)
            softmaxes(1, 0)
            softmaxes(2, 1)
            softmaxes(3, 2)
            softmaxes(None, 3)
            residual1(0)
            residual1(1)
            norm_apply(3, 0)
            residual1(2)
            norm_apply(3, 1)
            residual1(3)
            norm_apply(3, 2)
            norm_apply(3, 3)

            def lo_weights(p, slot):
                dve.wait_ge(w1_hi, p + 1)
                nc.vector.scalar_tensor_tensor(w1l[:, slot], st1[:, bass.ds(PW * p, PW)], WS, w1h[:, slot], ALU.mult,
                                               ALU.subtract).then_inc(w1_lo, 1)

            for p in range(4):
                lo_weights(p, p)
            dve.wait_ge(xnT_a, 4)
            nc.vector.tensor_tensor(xfl[:], B[0], xfh[:], ALU.subtract).then_inc(xfl_v, 1)
            dve.wait_ge(r1_mm, 1)
            bank = B[1][:, 0:NT * ER].rearrange("p (a b) -> p a b", b=ER)
            link(nc.vector.tensor_reduce(lgm[:], bank, AX, ALU.max))
            nc.vector.tensor_tensor(lg0[:], bank, over(lgm[:], ER), ALU.subtract).then_inc(r1_sub, 1)

            def product(p, b, used):
                dve.wait_ge(silu1, p + 1)
                dve.wait_ge(h3mm, p + 1)
                if used:
                    dve.wait_ge(r1, p - 1)
                nc.vector.scalar_tensor_tensor(u[:, b], B[5 + b], HS / WS, s[:, b], ALU.mult, ALU.mult).then_inc(u1, 1)

            def gated(p, b, used):
                dve.wait_ge(u1, p + 1)
                dve.wait_ge(g1mm, p)
                if used:
                    dve.wait_ge(lo1, p - 1)
                nc.vector.tensor_tensor(r[:, b], u[:, b], B[2 if b else 7], ALU.mult).then_inc(r1, 1)

            dve.wait_ge(r1_exp, 1)
            link(nc.vector.tensor_reduce(lgs[:], lg0[:], AX, ALU.add))
            nc.vector.reciprocal(lgs[:], lgs[:]).then_inc(r1_inv, 1)
            dve.wait_ge(r1_inv, 1)
            for t in range(NT):
                last = nc.vector.scalar_tensor_tensor(bia[:, t], lg0[:, t], lgs[:, t:t + 1], row("gate_bias"),
                                                      ALU.mult, ALU.add)
            link(last)
            for t in range(NT):
                last = nc.vector.max(top8[:, t], bia[:, t])
            biggest = mark(last)
            product(0, 0, False)
            dve.wait_ge(dve_step, biggest)
            link(nc.vector.memset(top8[:, :, TOPK1:8], -2.0e38))
            for t in range(NT):
                last = nc.vector.match_replace(rep[:, t], top8[:, t], bia[:, t], -3.0e38)
            replaced = mark(last)
            product(1, 1, False)
            dve.wait_ge(dve_step, replaced)
            dve.wait_ge(r1_norm, 1)
            link(nc.vector.scalar_tensor_tensor(gates[:], rep[:], -2.5e38, gates[:], ALU.is_lt, ALU.mult))
            nc.vector.tensor_copy(g16[:], gates[:]).then_inc(r1_g16, 1)
            dve.wait_ge(r1_g16, 1)
            nc.vector.tensor_tensor(gcb[:, :, ER:2 * ER], gates[:], g16[:], ALU.subtract).then_inc(r1_gcb, 1)
            nc.vector.tensor_copy(lgm[:], lgs[:]).then_inc(r1, 1)
            dve.wait_ge(lo1, 1)
            product(2, 0, False)
            lo_weights(4, 4)
            gated(1, 1, False)
            lo_weights(5, 5)
            product(3, 1, True)
            gated(2, 0, True)
            gated(3, 1, True)
            with dve.Fori(0, 4) as m:
                for k in range(RING):
                    product(RING * m + 4 + k, k % 2, True)
                    lo_weights(RING * m + 6 + k, k)
                    gated(RING * m + 4 + k, k % 2, True)
            for p in range(28, NP):
                product(p, p % 2, True)
                if p + 2 < NP:
                    lo_weights(p + 2, (p + 2) % RING)
                gated(p, p % 2, True)
            for t in range(NT):
                dve.wait_ge(y1_T, t + 1)
                nc.vector.tensor_tensor(outs[:, t], h[:, t], B[1 + t][:, 0:P], ALU.add).then_inc(out_v, 1)

        @block.tensor
        def _(pe):
            def mm(o, l, rr, start=True, stop=True):
                return nc.tensor.matmul(o, l, rr, start=start, stop=stop)

            pe.wait_ge(d_tokw, 16)
            for t in range(NT):
                pe.wait_ge(d_x[t], 16)
                for c in range(KC):
                    last = mm(B[t][:, 0:P], x_sb[:, t, c, :], tokw[:, c, :], c == 0, c == KC - 1)
                last.then_inc(tok_done, 1)

            def keep_warm(bank, n):
                for _ in range(n):
                    mm(bank[:, 0:256], negI[:], m0b[:].rearrange("p a b -> p (a b)"))

            def transpose_norm(k, warm=0):
                for t in range(NT):
                    keep_warm(B[6], warm)
                    pe.wait_ge(ln_xn, NT * k + t + 1)
                    nc.tensor.transpose(B[0][:, tile(t)], xn[:, t], ident).then_inc(ln_T, 1)

            pe.wait_ge(d_cst, 16)
            pe.wait_ge(d_wqN, 16)
            for c in range(12):
                mm(B[6][:, 0:P], wqkvN_sb[:, c, :], wqkvN_sb[:, c, :], c == 0, c == 11)
            pe.wait_ge(d_wo, 32)
            pe.wait_ge(d_col, 16)
            for c in range(C0):
                last = mm(B[6][:, P:P + 1], woT_sb[:, c, :], col("u_out")[:, c:c + 1], c == 0, c == C0 - 1)
            last.then_inc(sn_gram, 1)
            transpose_norm(0)
            pe.wait_ge(xnT_a, 1)
            for k in range(12):
                if k >= 4:
                    if k - 4 in ACT_UNITS:
                        pe.wait_ge(qkv_ev_a, ACT_UNITS.index(k - 4) + 1)
                    if k - 4 in DVE_UNITS:
                        pe.wait_ge(qkv_ev_v, DVE_UNITS.index(k - 4) + 1)
                if k % 4 == 0:
                    pe.wait_ge(wq_lo, k // 4 + 1)
                if k < 8:
                    c = slice(P * k, P * k + P)
                    mm(B[2 + k % 4], wqh[:, c], xfh[:], True, False)
                    mm(B[2 + k % 4], wql[:, c], xfh[:], False, False)
                    if k == 0:
                        pe.wait_ge(xfl_v, 1)
                    last = mm(B[2 + k % 4], wqh[:, c], xfl[:], False, True)
                else:
                    c = slice(2 * INNER, 3 * INNER)
                    mm(B[2 + k % 4], xfh[:, tile(k - 8)], wqh[:, c], True, False)
                    mm(B[2 + k % 4], xfh[:, tile(k - 8)], wql[:, c], False, False)
                    last = mm(B[2 + k % 4], xfl[:, tile(k - 8)], wqh[:, c], False, True)
                last.then_inc(qkv_mm, 1)
                if k == 0:
                    pe.wait_ge(sn_acopy, 1)
                    mm(B[7][:, 0:1], gram[:], col("u_qkv"))
                    for c in range(C0):
                        last = mm(B[7][:, 1 + c:2 + c], woN_sb[:, P * c:P * c + P], sna[:, 0:1])
                    last.then_inc(sn_b, 1)
                if k == 2:
                    pe.wait_ge(pool_const, 1)
                    pe.wait_ge(sn_sums, 1)
                    mm(B[7][:, 8:12], ones[:], sn4[:]).then_inc(sn_tot, 1)

            def scores0(t):
                bank = B[t]
                mm(bank[:, 0:256], negI[:], m0b[:].rearrange("p a b -> p (a b)"), True, False)
                for b in range(4):
                    for j in range(4):
                        last = mm(bank[32 * b:32 * b + 32, 64 * j:64 * j + 64],
                                  q0[:, j, P * t + 32 * b:P * t + 32 * b + 32],
                                  k0[:, j, 4 * t + b].rearrange("p a b -> p (a b)"), False, j == 3)
                last.then_inc(s_mm, 1)

            def values0(t, warm):
                if t >= 2:
                    pe.wait_ge(s_on, t - 1)
                keep_warm(B[4 * (1 - t % 2)], warm)
                pe.wait_ge(s_tr, t + 1)
                for b in range(4):
                    q = slice(32 * b, 32 * b + 32)
                    for hd in range(H):
                        j = hd % 4
                        last = mm(B[4 * (1 - t % 2) + hd // 4][q, 65 * j:65 * j + 65], pk[q, t % 2, hd, :],
                                  vA[q, t, hd, :])
                last.then_inc(s_av, 1)

            def transpose_o(t, warm):
                if t >= 1:
                    pe.wait_ge(s_oT, t)
                keep_warm(B[6], warm)
                pe.wait_ge(s_on, t + 1)
                flat = on[:, t % 2].rearrange("p a b -> p (a b)")
                for c in range(4):
                    last = nc.tensor.transpose(B[6][:, tile(c)], flat[:, tile(c)], ident)
                last.then_inc(s_oTp, 1)

            def project0(t, warm):
                if t == 3:
                    pe.wait_ge(s_hup, 1)
                keep_warm(B[OUT0[t]], warm)
                pe.wait_ge(s_oT, t + 1)
                for c in range(4):
                    last = mm(B[OUT0[t]][:, 0:P], oT[:, t % 2, c, :], woT_sb[:, c, :], c == 0, c == 3)
                last.then_inc(s_proj, 1)

            pe.wait_ge(mask_ready, 2)
            pe.wait_ge(qkv_ev_a, len(ACT_UNITS))
            pe.wait_ge(qkv_ev_v, len(DVE_UNITS))
            for t in range(NT):
                scores0(t)
            values0(0, 6)
            values0(1, 6)
            transpose_o(0, 6)
            values0(2, 4)
            transpose_o(1, 2)
            project0(0, 2)
            values0(3, 2)
            transpose_o(2, 2)
            project0(1, 2)
            transpose_o(3, 2)
            project0(2, 2)
            project0(3, 2)

            transpose_norm(1, 3)
            keep_warm(B[6], 8)
            pe.wait_ge(xfl_v, 2)

            def router(n, c0, done):
                for t in range(NT):
                    o = B[1][:, n * t:n * t + n]
                    mm(o, xfh[:, tile(t)], wrs[:, 0, c0:c0 + n], True, False)
                    mm(o, xfl[:, tile(t)], wrs[:, 0, c0:c0 + n], False, False)
                    last = mm(o, xfh[:, tile(t)], wrs[:, 1, c0:c0 + n], False, True)
                last.then_inc(done, 1)

            router(E0, ER, r0_mm)

            def up(n, e, c, used):
                if used:
                    pe.wait_ge(relu0, n - 1)
                if c == 0:
                    pe.wait_ge(w0_lo, n + 2)
                o = B[3 + c % 2]
                hi = w0h[:, bass.ds(1024 * e + P * c, P)]
                lo = w0l[:, bass.ds(1024 * e + P * c, P)]
                mm(o, hi, xfh[:], True, False)
                mm(o, hi, xfl[:], False, False)
                mm(o, lo, xfh[:], False, True).then_inc(up0, 1)

            def down(n, e, c, b, used):
                pe.wait_ge(lo0v, n + 1)
                pe.wait_ge(lo0p, n + 1)
                if c == 0:
                    pe.wait_ge(w0_lo, n + 4)
                if c == 0 and used:
                    pe.wait_ge(yt0, e - 1)
                o = B[7 * (1 - b)]
                hi = w0h[:, bass.ds(1024 * e + F0 + P * c, P)]
                lo = w0l[:, bass.ds(1024 * e + F0 + P * c, P)]
                mm(o, hi, hh[:, c, :], c == 0, False)
                mm(o, hi, hl[:, c, :], False, False)
                last = mm(o, lo, hh[:, c, :], False, c == 3)
                last.then_inc(down0, 1)

            def gate_mm(e, b, used):
                if used:
                    pe.wait_ge(gev0, e - 1)
                mm(B[5 + b], sel0[:].rearrange("p a b -> p (a b)")[:, bass.ds(P * e, P)], gT[:]).then_inc(gmm0, 1)

            def step0(n, e, k, used=True):
                up(n, e, k % 4, True)
                if k % 4 == 3:
                    gate_mm(e, k // 4, used)
                down(n - 3, e + (k % 4 - 3) // 4, (k - 3) % 4, ((k - 3) // 4) % 2, used)

            for n in range(4):
                up(n, 0, n, n >= 2)
            down(0, 0, 0, 0, False)
            for n in range(4, 8):
                if n == 5:
                    pe.wait_ge(r0_gcb, 1)
                    for t in range(NT):
                        last = nc.tensor.transpose(B[2][0:16, tile(t)], gcb[:, t, 0:16], ident)
                    last.then_inc(r0_T, 1)
                if n == 7:
                    pe.wait_ge(act_setup, 2)
                    pe.wait_ge(d_l1w, 32)
                    pe.wait_ge(r0_gT, 1)
                    mm(B[1], b2_sb[:], gT32[:]).then_inc(r0_b2, 1)
                    gate_mm(0, 0, False)
                step0(n, 1, n, used=False)
            with pe.Fori(0, 2) as m:
                for k in range(8):
                    step0(8 * m + 8 + k, 2 * m + 2 + k // 4, k)
            for n in range(24, 32):
                step0(n, n // 4, n % 8)
            for n in range(29, 32):
                down(n, 7, n % 4, 1, True)
            pe.wait_ge(acc0, E0 - 1)
            for t in range(NT):
                mm(B[1 + t][:, 0:P], acc[:, tile(t)], ident, True, False)
            pe.wait_ge(yt0, E0)
            for t in range(NT):
                mm(B[1 + t][:, 0:P], yt[:, 1, tile(t)], ident, False, True).then_inc(f0_T, 1)

            transpose_norm(2)
            pe.wait_ge(w1_sum, 1)
            keep_warm(B[7], 6)
            pe.wait_ge(xnT_a, 3)
            for t in range(NT):
                mm(B[t][:, 0:P], xnT[:, tile(t)], w1t[:]).then_inc(w_mm, 1)

            def transpose_w(t):
                pe.wait_ge(w_n, t + 1)
                nc.tensor.transpose(B[4 + t][:, 0:P], wtm[:, tile(t)], ident)
                nc.tensor.transpose(B[t][:, P:2 * P], wtm[:, tile(t)], ident).then_inc(qk_T, 1)

            def permute_v(g):
                pe.wait_ge(qk_a, g + 1)
                for t in (0, 1):
                    for i in (0, 1):
                        c = P * (2 * t + i)
                        last = mm(B[4 + g][:, c:c + P], perm[:, i], wtm[:, tile(2 * g + t)])
                last.then_inc(v_mm, 1)

            def scores1(t):
                pe.wait_ge(qk_a, t + 1)
                pe.wait_ge(k1_v, t + 1)
                for b in range(4):
                    for i in (0, 1):
                        last = mm(by16(B[t][32 * b:32 * b + 32, 0:P]), q1[:, 4 * t + b, i, :],
                                  k1[:, 4 * t + b, :, 16 * i:16 * i + 16], i == 0, i == 1)
                last.then_inc(t_mm, 1)

            def values1(t):
                if t >= 1:
                    pe.wait_ge(t_yT, t)
                pe.wait_ge(t_probs, t + 1)
                if t == 0:
                    pe.wait_ge(v_a, 2)
                    keep_warm(B[4], 8)
                for j in range(4):
                    for i in range(2):
                        for b in range(4):
                            q = slice(32 * b, 32 * b + 32)
                            c = 32 * j + 16 * i
                            last = mm(B[4 + b][32 * j:32 * j + 32, 16 * i:16 * i + 16], v1[q, t, i, j, :],
                                      pk1[q, t, c:c + 16])
                last.then_inc(t_av, 1)

            def project1(t):
                pe.wait_ge(t_yT, t + 1)
                mm(B[t][:, 0:P], oT[:, t % 2, 0, :], w1n[:]).then_inc(t_proj, 1)

            pe.wait_ge(d_perm, 16)
            keep_warm(B[7], 8)
            transpose_w(0)
            transpose_w(1)
            transpose_w(2)
            keep_warm(B[7], 4)
            scores1(0)
            transpose_w(3)
            scores1(1)
            permute_v(0)
            scores1(2)
            permute_v(1)
            scores1(3)
            values1(0)
            values1(1)
            project1(0)
            values1(2)
            project1(1)
            values1(3)
            project1(2)
            project1(3)

            transpose_norm(3)
            pe.wait_ge(xfl_v, 3)
            router(ER, 0, r1_mm)

            def pair_up(p, slot, used):
                pe.wait_ge(w1_lo, p + 1)
                for b0, c0, bank_free, done in ((3, 0, silu1, h1mm), (5, P, u1, h3mm)):
                    if used:
                        pe.wait_ge(bank_free, p - 1)
                    o = B[b0 + slot % 2]
                    mm(o, w1h[:, slot, c0:c0 + P], xfh[:], True, False)
                    mm(o, w1h[:, slot, c0:c0 + P], xfl[:], False, False)
                    mm(o, w1l[:, slot, c0:c0 + P], xfh[:], False, True).then_inc(done, 1)

            def pair_gate(p, slot, used):
                if used:
                    pe.wait_ge(r1, p - 1)
                flat = sel1[:].rearrange("p a b -> p (a b)")
                mm(B[2 if slot % 2 else 7], flat[:, bass.ds(P * p - P, P)], gT[:]).then_inc(g1mm, 1)

            def pair_down(p, slot, first=False, last=False):
                pe.wait_ge(lo1, p + 1)
                b = slot % 3
                mm(B[0], w1h[:, slot, 2 * P:3 * P], hh[:, b, :], first, False)
                mm(B[0], w1h[:, slot, 2 * P:3 * P], hl[:, b, :], False, False)
                mm(B[0], w1l[:, slot, 2 * P:3 * P], hh[:, b, :], False, last).then_inc(down1, 1)

            pair_up(0, 0, False)
            pair_up(1, 1, False)
            pair_up(2, 2, True)
            pair_down(0, 0, first=True)
            pair_up(3, 3, True)
            pe.wait_ge(r1_gcb, 2)
            for t in range(NT):
                last = nc.tensor.transpose(B[2][:, tile(t)], gcb[:, t, :], ident)
            last.then_inc(r1_T, 1)
            pe.wait_ge(r1_gT, 1)
            pe.wait_ge(act_setup, 3)
            pair_gate(1, 1, False)
            pair_gate(2, 2, False)
            pair_up(4, 4, True)
            pair_gate(3, 3, True)
            with pe.Fori(0, 4) as m:
                for k in range(RING):
                    pair_gate(RING * m + 4 + k, k, True)
                    pair_down(RING * m + 1 + k, (k + 1) % RING)
                    pair_up(RING * m + 5 + k, (k + 5) % RING, True)
            for p in range(28, NP):
                pair_gate(p, p, True)
                pair_down(p - 3, (p - 3) % RING)
                if p + 1 < NP:
                    pair_up(p + 1, (p + 1) % RING, True)
            for p in range(NP - 3, NP):
                pair_down(p, p % RING, last=(p == NP - 1))
            for t in range(NT):
                pe.wait_ge(y1_ev, t + 1)
                nc.tensor.transpose(B[1 + t][:, 0:P], acc[:, tile(t)], ident).then_inc(y1_T, 1)


def kernel(**inputs):
    import concourse.bacc as bacc
    import numpy as np
    from concourse.bass_utils import run_bass_kernel_spmd as run

    v = {k: np.asarray(a) for k, a in inputs.items()}
    f = np.float32
    x = v["x"].reshape(32, 3, 4, 16, 4, 16).transpose(0, 2, 4, 1, 3, 5).reshape(NT, P, KC, P).transpose(0, 3, 2, 1)
    tokWT = v["L0_tok_W"].reshape(P, KC, P).transpose(2, 1, 0)
    rows = np.concatenate([v[n].reshape(1, -1) for n in (
        "L0_tok_b", "L0_attn_b_out", "L0_ffn_br", "L1_ffn_gate_bias", "L0_attn_sigma_qkv", "L0_attn_sigma_out", "L0_attn_temperature")], axis=1)
    cols = np.concatenate([v["L0_attn_u_qkv"].reshape(P, 1), v["L0_attn_u_out"].reshape(C0, P).T,
                           v["L0_ffn_b1"].reshape(E0 * C0, P).T, v["L0_ffn_Wr"], v["L1_ffn_g_w"].T]
                          + [np.tile(v[n].reshape(-1), H).reshape(P, 1) for n in
                             ("L1_attn_g1", "L1_attn_g2", "L1_attn_g3")], axis=1)
    w = v["L0_attn_w_qkv"]
    wo = v["L0_attn_w_out"]
    w1 = v["L0_ffn_W1"]
    w2 = v["L0_ffn_W2"].reshape(E0, C0, P, P).transpose(0, 2, 1, 3).reshape(E0, P, F0)
    l1w = np.stack([v["L1_attn_qkv_w"], v["L1_attn_delta_w"], v["L1_attn_qkv_w"].T, v["L1_attn_delta_w"].T], axis=1)
    e1, e3 = (v[n].reshape(NP, 2, P, 64).transpose(0, 2, 1, 3).reshape(NP, P, P) for n in ("L1_ffn_w1", "L1_ffn_w3"))
    e2 = v["L1_ffn_w2"].reshape(NP, P, P)
    wl1 = np.concatenate([e1, e3, e2], axis=2).reshape(NP // 3, 3, P, PW).transpose(0, 2, 1, 3)
    i = np.arange(P)
    j = np.arange(32)
    other = (i[:, None] % 32 // 16 != j[None, :] // 16).astype(f)
    parity = (i[:, None] % 32 // 16 == np.arange(2)[None, :]).astype(f)
    itself = (i[:, None] % 32 == j[None, :]).astype(f)
    ident = np.eye(P, dtype=f)
    pick1 = np.zeros((P, ER), f)
    pick1[np.arange(ER), np.arange(ER)] = 1
    pick1[ER + np.arange(ER), np.arange(ER)] = 2.0 ** -11
    pick0 = np.zeros((P, E0), f)
    pick0[np.arange(E0), np.arange(E0)] = 1
    pick0[E0 + np.arange(E0), np.arange(E0)] = 2.0 ** -11
    heads = (i[:, None] // DH1 == np.arange(H)[None, :]).astype(f)
    lo_scales = np.ones((P, 2), f)
    lo_scales[E0:16, 0] = lo_scales[ER:, 1] = LS
    consts = np.concatenate([ident, np.maximum(other, itself), parity, pick1, pick0, heads, lo_scales], axis=1)

    perms = [(i[:, None] == i[None, :] // 32 * 32 + 16 * image + i[None, :] % 16).astype(f) for image in (0, 1)]

    arrays = {"xT": x.reshape(NT, P, KC * P), "tokWT": tokWT.reshape(P, KC * P), "rows": rows, "cols": cols,
              "consts": consts, "wqkvT": w.T, "wqkvN": w.reshape(12, P, P).transpose(1, 0, 2).reshape(P, 12 * P),
              "woT": wo.T.reshape(C0, P, P).transpose(1, 0, 2).reshape(P, C0 * P), "woN": wo,
              "l1w": l1w.reshape(P, 4 * P), "b2x": np.concatenate([v["L0_ffn_b2"]] * 2, axis=0),
              "perms": np.concatenate(perms, axis=1),
              "wl0": np.concatenate([w1, w2], axis=2), "wl1": wl1.reshape(NP // 3, P, 3 * PW)}
    arrays = {k: np.ascontiguousarray(a) for k, a in arrays.items()}
    nc = bacc.Bacc("TRN2", target_bir_lowering=False, num_devices=1)
    args = [nc.dram_tensor(k, a.shape, mybir.dt.from_np(a.dtype), kind="ExternalInput").ap() for k, a in arrays.items()]
    out = nc.dram_tensor("out", (NT, P, P), F32, kind="ExternalOutput").ap()
    tower(nc, *args, out)
    res = run(nc, [arrays], core_ids=[0])
    return res.results[0]["out"].reshape(32, 16, P)
```
